# Optimizing a Trainium2 kernel written in Bass

```python
import numpy as np
import jax
import jax.numpy as jnp

def _softmax(x, axis=-1):
    return jax.nn.softmax(x, axis=axis)

def _gelu(x):
    return jax.nn.gelu(x, approximate=True)

def _silu(x):
    return jax.nn.silu(x)

def _sigmoid(x):
    return jax.nn.sigmoid(x)

def _layernorm(x, axis=-1, eps=1e-05):
    m = jnp.mean(x, axis=axis, keepdims=True)
    v = jnp.var(x, axis=axis, keepdims=True)
    return (x - m) / jnp.sqrt(v + eps)

def _scatter_add(tgt, idx, src, axis=0):
    return tgt.at[idx].add(src)

def _segment_sum(src, seg, n):
    return jax.ops.segment_sum(src, seg, n)
kernel_name = 'mk_xattn_ffn_d2_seqx_r4_319758'

def setup_inputs(seed: int=0):
    np.random.seed(seed)
    _w = jnp.asarray

    def _rec_inputs():
        import jax
        import jax.numpy as jnp
        _rk = jax.random.key(seed)
        x = -0.0002928 + 1 * jax.random.normal(jax.random.fold_in(_rk, 1), (32, 256, 256), jnp.float32)
        _lenS = 256 - jax.random.randint(jax.random.fold_in(_rk, 7), (32,), 0, max(1, 256 // 4) + 1, jnp.int32)
        _lenS2 = 256 - jax.random.randint(jax.random.fold_in(_rk, 8), (32,), 0, max(1, 256 // 4) + 1, jnp.int32)
        _ctx_1024P = jax.random.normal(jax.random.fold_in(_rk, 11), (32, 16, 256), jnp.float32)
        _ctx_1024c = jax.random.dirichlet(jax.random.fold_in(_rk, 511), 0.3 * jnp.ones((16,), jnp.float32), (32, 256))
        _ctx_1024t = jnp.einsum('bsk,bkd->bsd', _ctx_1024c, _ctx_1024P)
        _ctx_1024t = _ctx_1024t * jax.lax.rsqrt(jnp.mean(jnp.square(_ctx_1024t)) + 1e-12) * 0.953939
        ctx_1024 = -1.39393e-06 + 0.999914 * (_ctx_1024t + 0.3 * jax.random.normal(jax.random.fold_in(_rk, 611), (32, 256, 256), jnp.float32))
        return (x, ctx_1024)
    x, ctx_1024 = _rec_inputs()

    def _L0_xattn_setup():
        import jax, jax.numpy as jnp
        import numpy as np
        D_MODEL = 256
        NUM_HEADS = 16
        HEAD_DIM = D_MODEL // NUM_HEADS
        key = jax.random.key(seed)
        ks = jax.random.split(key, 11)
        B, T, S = (2, 512, 512)
        s = 1.0 / np.sqrt(D_MODEL)
        return {'query': jax.random.normal(ks[0], (B, T, D_MODEL), jnp.float32), 'key': jax.random.normal(ks[1], (B, S, D_MODEL), jnp.float32), 'value': jax.random.normal(ks[2], (B, S, D_MODEL), jnp.float32), 'Wq': jax.random.normal(ks[3], (D_MODEL, D_MODEL), jnp.float32) * s, 'bq': jnp.zeros((D_MODEL,), jnp.float32), 'Wk': jax.random.normal(ks[4], (D_MODEL, D_MODEL), jnp.float32) * s, 'bk': jnp.zeros((D_MODEL,), jnp.float32), 'Wv': jax.random.normal(ks[5], (D_MODEL, D_MODEL), jnp.float32) * s, 'bv': jnp.zeros((D_MODEL,), jnp.float32), 'Wo': jax.random.normal(ks[6], (D_MODEL, D_MODEL), jnp.float32) * s, 'bo': jnp.zeros((D_MODEL,), jnp.float32)}
    _L0_xattn_all = _L0_xattn_setup()
    _L0_xattn_in = {k: v for k, v in _L0_xattn_all.items() if k in ('Wq', 'bq', 'Wk', 'bk', 'Wv', 'bv', 'Wo', 'bo')}
    del _L0_xattn_all

    def _L0_ffn_setup():
        import jax, jax.numpy as jnp
        import numpy as np
        TAU = 1.0
        K_ROUTE = 3
        EPS = 1e-08

        def _route_combine_weights(x_addr, U, k, tau):
            z = x_addr @ U.T
            topv, topi = jax.lax.top_k(z, k)
            w = jax.nn.softmax(topv / (tau + EPS), axis=1)
            N, L = z.shape
            rows = jnp.arange(N)[:, None]
            return jnp.zeros((N, L), z.dtype).at[rows, topi].add(w)

        def _mixture(inp, C, W):
            L = W.shape[0]
            y = jnp.zeros((inp.shape[0], W.shape[1]), inp.dtype)
            for e in range(L):
                y = y + C[:, e:e + 1] * (inp @ W[e].T)
            return y
        key = jax.random.key(seed)
        ks = jax.random.split(key, 8)
        B, T, D_in, H, D_out, L, d_addr = (8, 2048, 256, 256, 256, 12, 64)

        def unit_rows(k, L_, d_):
            U = jax.random.normal(k, (L_, d_), dtype=jnp.float32)
            U = U - U.mean(axis=1, keepdims=True)
            return U / (jnp.linalg.norm(U, axis=1, keepdims=True) + EPS)

        def norm_tape(k, shape):
            W = jax.random.normal(k, shape, dtype=jnp.float32)
            n = jnp.sqrt(jnp.sum(W * W, axis=tuple(range(1, W.ndim)), keepdims=True)) + 1e-12
            return W / n
        x = jax.random.normal(ks[0], (B, T, D_in), dtype=jnp.float32)
        P_w = jax.random.normal(ks[1], (d_addr, D_in), dtype=jnp.float32) / np.sqrt(D_in)
        U1 = unit_rows(ks[2], L, d_addr)
        U2 = unit_rows(ks[3], L, d_addr)
        U3 = unit_rows(ks[4], L, d_addr)
        W1 = norm_tape(ks[5], (L, H, D_in))
        W2 = norm_tape(ks[6], (L, D_out, H))
        b2 = norm_tape(ks[7], (L, D_out))
        return {'x': x, 'P_w': P_w, 'U1': U1, 'U2': U2, 'U3': U3, 'W1': W1, 'W2': W2, 'b2': b2}
    _L0_ffn_all = _L0_ffn_setup()
    _L0_ffn_in = {k: v for k, v in _L0_ffn_all.items() if k in ('P_w', 'U1', 'U2', 'U3', 'W1', 'W2', 'b2')}
    del _L0_ffn_all

    def _L1_xattn_setup():
        import jax, jax.numpy as jnp
        import numpy as np
        NUM_HEADS = 16
        key = jax.random.key(seed)
        kq, kk, kv = jax.random.split(key, 3)
        B, S, DIM = (2, 512, 256)
        q = jax.random.normal(kq, (B, S, DIM), dtype=jnp.float32)
        k = jax.random.normal(kk, (B, S, DIM), dtype=jnp.float32)
        v = jax.random.normal(kv, (B, S, DIM), dtype=jnp.float32)
        return {'q': q, 'k': k, 'v': v}
    _L1_xattn_all = _L1_xattn_setup()
    _L1_xattn_in = {k: v for k, v in _L1_xattn_all.items() if k in ()}
    del _L1_xattn_all

    def _L1_ffn_setup():
        import jax, jax.numpy as jnp
        import numpy as np
        B, S, D = (1, 512, 256)
        E, K, F = (64, 8, 192)
        SF = 192
        C = 128
        ROUTED_SCALE = 1.0

        def _moe_forward(x, router_w, w_gate, w_up, w_down, ws_gate_up, ws_down):
            T = x.shape[0]
            logits = x.astype(jnp.float32) @ router_w.T
            probs = jax.nn.softmax(logits, axis=-1)
            topk_w, topk_ids = jax.lax.top_k(probs, K)
            topk_w = topk_w / jnp.sum(topk_w, axis=-1, keepdims=True)
            topk_w = topk_w.astype(x.dtype)
            N = T * K
            flat_e = topk_ids.reshape(-1)
            flat_w = topk_w.reshape(-1)
            tok = jnp.arange(N) // K
            onehot = flat_e[:, None] == jnp.arange(E)[None, :]
            pos = jnp.cumsum(onehot, axis=0)[jnp.arange(N), flat_e] - 1
            valid = pos < C
            idx = jnp.where(valid, flat_e * C + pos, E * C)
            x_buf = jnp.zeros((E * C + 1, x.shape[1]), x.dtype).at[idx].set(x[tok])
            xb = x_buf[:E * C].reshape(E, C, -1)
            g = jnp.einsum('ecd,edf->ecf', xb, w_gate)
            u = jnp.einsum('ecd,edf->ecf', xb, w_up)
            h = jax.nn.silu(g) * u
            y = jnp.einsum('ecf,efd->ecd', h, w_down).reshape(E * C, -1)
            safe = jnp.where(valid, idx, 0)
            contrib = y[safe] * (flat_w * valid.astype(flat_w.dtype))[:, None]
            routed = jax.ops.segment_sum(contrib, tok, num_segments=T)
            routed = routed * ROUTED_SCALE
            gu = x @ ws_gate_up
            sg, su = (gu[:, :SF], gu[:, SF:])
            shared = jax.nn.silu(sg) * su @ ws_down
            return routed + shared
        key = jax.random.key(seed)
        ks = jax.random.split(key, 7)
        w = 0.02
        return {'hidden_states': jax.random.normal(ks[0], (B, S, D), jnp.float32), 'router_w': jax.random.normal(ks[1], (E, D), jnp.float32) * w, 'w_gate': jax.random.normal(ks[2], (E, D, F), jnp.float32) * w, 'w_up': jax.random.normal(ks[3], (E, D, F), jnp.float32) * w, 'w_down': jax.random.normal(ks[4], (E, F, D), jnp.float32) * w, 'ws_gate_up': jax.random.normal(ks[5], (D, 2 * SF), jnp.float32) * w, 'ws_down': jax.random.normal(ks[6], (SF, D), jnp.float32) * w}
    _L1_ffn_all = _L1_ffn_setup()
    _L1_ffn_in = {k: v for k, v in _L1_ffn_all.items() if k in ('router_w', 'w_gate', 'w_up', 'w_down', 'ws_gate_up', 'ws_down')}
    del _L1_ffn_all
    return {'x': x, 'ctx_1024': ctx_1024, 'L0_xattn_Wq': _L0_xattn_in['Wq'], 'L0_xattn_bq': _L0_xattn_in['bq'], 'L0_xattn_Wk': _L0_xattn_in['Wk'], 'L0_xattn_bk': _L0_xattn_in['bk'], 'L0_xattn_Wv': _L0_xattn_in['Wv'], 'L0_xattn_bv': _L0_xattn_in['bv'], 'L0_xattn_Wo': _L0_xattn_in['Wo'], 'L0_xattn_bo': _L0_xattn_in['bo'], 'L0_ffn_P_w': _L0_ffn_in['P_w'], 'L0_ffn_U1': _L0_ffn_in['U1'], 'L0_ffn_U2': _L0_ffn_in['U2'], 'L0_ffn_U3': _L0_ffn_in['U3'], 'L0_ffn_W1': _L0_ffn_in['W1'], 'L0_ffn_W2': _L0_ffn_in['W2'], 'L0_ffn_b2': _L0_ffn_in['b2'], 'L1_ffn_router_w': _L1_ffn_in['router_w'], 'L1_ffn_w_gate': _L1_ffn_in['w_gate'], 'L1_ffn_w_up': _L1_ffn_in['w_up'], 'L1_ffn_w_down': _L1_ffn_in['w_down'], 'L1_ffn_ws_gate_up': _L1_ffn_in['ws_gate_up'], 'L1_ffn_ws_down': _L1_ffn_in['ws_down']}

def reference(x, ctx_1024, L0_xattn_Wq, L0_xattn_bq, L0_xattn_Wk, L0_xattn_bk, L0_xattn_Wv, L0_xattn_bv, L0_xattn_Wo, L0_xattn_bo, L0_ffn_P_w, L0_ffn_U1, L0_ffn_U2, L0_ffn_U3, L0_ffn_W1, L0_ffn_W2, L0_ffn_b2, L1_ffn_router_w, L1_ffn_w_gate, L1_ffn_w_up, L1_ffn_w_down, L1_ffn_ws_gate_up, L1_ffn_ws_down):
    import jax
    import jax.numpy as jnp

    def _L0_xattn_ref(query, key, value, Wq, bq, Wk, bk, Wv, bv, Wo, bo):
        import jax, jax.numpy as jnp
        import numpy as np
        D_MODEL = 256
        NUM_HEADS = 16
        HEAD_DIM = D_MODEL // NUM_HEADS
        B, T, _ = query.shape
        S = key.shape[1]
        q = query @ Wq.T + bq
        k = key @ Wk.T + bk
        v = value @ Wv.T + bv
        q = q.reshape(B, T, NUM_HEADS, HEAD_DIM).transpose(0, 2, 1, 3)
        k = k.reshape(B, S, NUM_HEADS, HEAD_DIM).transpose(0, 2, 1, 3)
        v = v.reshape(B, S, NUM_HEADS, HEAD_DIM).transpose(0, 2, 1, 3)
        scale = 1.0 / jnp.sqrt(jnp.asarray(HEAD_DIM, q.dtype))
        scores = jnp.einsum('bhtd,bhsd->bhts', q, k) * scale
        attn = jax.nn.softmax(scores, axis=-1)
        ctx = jnp.einsum('bhts,bhsd->bhtd', attn, v)
        ctx = ctx.transpose(0, 2, 1, 3).reshape(B, T, D_MODEL)
        return ctx @ Wo.T + bo

    def _L0_ffn_ref(x, P_w, U1, U2, U3, W1, W2, b2):
        import jax, jax.numpy as jnp
        import numpy as np
        TAU = 1.0
        K_ROUTE = 3
        EPS = 1e-08

        def _route_combine_weights(x_addr, U, k, tau):
            z = x_addr @ U.T
            topv, topi = jax.lax.top_k(z, k)
            w = jax.nn.softmax(topv / (tau + EPS), axis=1)
            N, L = z.shape
            rows = jnp.arange(N)[:, None]
            return jnp.zeros((N, L), z.dtype).at[rows, topi].add(w)

        def _mixture(inp, C, W):
            L = W.shape[0]
            y = jnp.zeros((inp.shape[0], W.shape[1]), inp.dtype)
            for e in range(L):
                y = y + C[:, e:e + 1] * (inp @ W[e].T)
            return y
        B, T, D = x.shape
        xf = x.reshape(B * T, D)
        xa = xf @ P_w.T
        C1 = _route_combine_weights(xa, U1, K_ROUTE, TAU)
        C2 = _route_combine_weights(xa, U2, K_ROUTE, TAU)
        C3 = _route_combine_weights(xa, U3, K_ROUTE, TAU)
        h = jax.nn.gelu(_mixture(xf, C1, W1), approximate=False)
        y = _mixture(h, C2, W2) + C3 @ b2
        return y.reshape(B, T, -1)

    def _L1_xattn_ref(q, k, v):
        import jax, jax.numpy as jnp
        import numpy as np
        NUM_HEADS = 16
        B, S, dim = q.shape
        H = NUM_HEADS
        D = dim // H
        scale = D ** (-0.5)
        qh = q.reshape(B, S, H, D) * scale
        kh = k.reshape(B, S, H, D)
        vh = v.reshape(B, S, H, D)
        scores = jnp.einsum('bqhd,bkhd->bhqk', qh, kh)
        weights = jax.nn.softmax(scores, axis=-1)
        out = jnp.einsum('bhqk,bkhd->bqhd', weights, vh)
        return out.reshape(B, S, dim)

    def _L1_ffn_ref(hidden_states, router_w, w_gate, w_up, w_down, ws_gate_up, ws_down):
        import jax, jax.numpy as jnp
        import numpy as np
        B, S, D = (1, 512, 256)
        E, K, F = (64, 8, 192)
        SF = 192
        C = 128
        ROUTED_SCALE = 1.0

        def _moe_forward(x, router_w, w_gate, w_up, w_down, ws_gate_up, ws_down):
            T = x.shape[0]
            logits = x.astype(jnp.float32) @ router_w.T
            probs = jax.nn.softmax(logits, axis=-1)
            topk_w, topk_ids = jax.lax.top_k(probs, K)
            topk_w = topk_w / jnp.sum(topk_w, axis=-1, keepdims=True)
            topk_w = topk_w.astype(x.dtype)
            N = T * K
            flat_e = topk_ids.reshape(-1)
            flat_w = topk_w.reshape(-1)
            tok = jnp.arange(N) // K
            onehot = flat_e[:, None] == jnp.arange(E)[None, :]
            pos = jnp.cumsum(onehot, axis=0)[jnp.arange(N), flat_e] - 1
            valid = pos < C
            idx = jnp.where(valid, flat_e * C + pos, E * C)
            x_buf = jnp.zeros((E * C + 1, x.shape[1]), x.dtype).at[idx].set(x[tok])
            xb = x_buf[:E * C].reshape(E, C, -1)
            g = jnp.einsum('ecd,edf->ecf', xb, w_gate)
            u = jnp.einsum('ecd,edf->ecf', xb, w_up)
            h = jax.nn.silu(g) * u
            y = jnp.einsum('ecf,efd->ecd', h, w_down).reshape(E * C, -1)
            safe = jnp.where(valid, idx, 0)
            contrib = y[safe] * (flat_w * valid.astype(flat_w.dtype))[:, None]
            routed = jax.ops.segment_sum(contrib, tok, num_segments=T)
            routed = routed * ROUTED_SCALE
            gu = x @ ws_gate_up
            sg, su = (gu[:, :SF], gu[:, SF:])
            shared = jax.nn.silu(sg) * su @ ws_down
            return routed + shared
        b, s, d = hidden_states.shape
        x = hidden_states.reshape(-1, d)
        out = _moe_forward(x, router_w, w_gate, w_up, w_down, ws_gate_up, ws_down)
        return out.reshape(b, s, d)
    x = x + _L0_xattn_ref(_layernorm(x, axis=-1), ctx_1024, ctx_1024, L0_xattn_Wq, L0_xattn_bq, L0_xattn_Wk, L0_xattn_bk, L0_xattn_Wv, L0_xattn_bv, L0_xattn_Wo, L0_xattn_bo)
    x = x + _L0_ffn_ref(_layernorm(x, axis=-1), L0_ffn_P_w, L0_ffn_U1, L0_ffn_U2, L0_ffn_U3, L0_ffn_W1, L0_ffn_W2, L0_ffn_b2)
    x = x + _L1_xattn_ref(_layernorm(x, axis=-1), ctx_1024, ctx_1024)
    x = x + _L1_ffn_ref(_layernorm(x, axis=-1), L1_ffn_router_w, L1_ffn_w_gate, L1_ffn_w_up, L1_ffn_w_down, L1_ffn_ws_gate_up, L1_ffn_ws_down)
    return x

_drawn_inputs = setup_inputs


def setup_inputs(seed=0):
    import zlib

    import numpy as np

    out = dict(_drawn_inputs(seed))
    spreads = {'L0_xattn_bq': (0.0, 0.409),
     'L0_xattn_bk': (0.0, 0.8),
     'L0_xattn_bv': (0.0, 0.1),
     'L0_xattn_bo': (0.0, 0.1)}
    factors = {'L0_ffn_U1': 8.0,
     'L0_ffn_U2': 8.0,
     'L0_ffn_W1': 8.0,
     'L0_ffn_W2': 8.0,
     'L1_ffn_router_w': 8.0,
     'L1_ffn_w_gate': 8.0,
     'L1_ffn_w_up': 8.0,
     'L1_ffn_w_down': 8.0,
     'L1_ffn_ws_gate_up': 5.553,
     'L1_ffn_ws_down': 5.561}
    for name, (base, spread) in spreads.items():
        noise = np.random.default_rng([zlib.crc32(name.encode()), seed]).standard_normal(out[name].shape)
        drawn = base * np.exp(spread * noise) if base else spread * noise
        out[name] = jnp.asarray(drawn.astype(out[name].dtype))
    for name, factor in factors.items():
        out[name] = (out[name] * factor).astype(out[name].dtype)
    return out
```

```python
from contextlib import ExitStack

import numpy as np

import concourse.bass as bass
from concourse import mybir

F32 = mybir.dt.float32
F32R = mybir.dt.float32r
BF16 = mybir.dt.bfloat16
U32 = mybir.dt.uint32
ALU = mybir.AluOpType
ACT = mybir.ActivationFunctionType
AX_X = mybir.AxisListType.X

P = 128
EPS = 1e-5
SENTINEL = -1.0e30
TAKEN = -3.0e30


class Engine:

    def __init__(self, engine, sem):
        self.engine, self.sem, self.count, self.seen = engine, sem, 0, {}

    def wait(self, marks):
        for sem, value in marks:
            if self.seen.get(sem.name, 0) < value:
                self.seen[sem.name] = value
                self.engine.wait_ge(sem, value)

    def do(self, fn, after=(), reuse=()):
        self.wait(after)
        self.wait(reuse)
        self.count += 1
        fn(self.engine).then_inc(self.sem, 1)
        return (self.sem, self.count)

    def dma(self, fn, counter, after=(), reuse=()):
        self.wait(after)
        self.wait(reuse)
        counter.count += 16
        fn(self.engine).then_inc(counter.sem, 16)
        return (counter.sem, counter.count)


class Counter:
    def __init__(self, sem):
        self.sem, self.count = sem, 0


class Ring:

    def __init__(self, buffers):
        self.buffers, self.free = buffers, [()] * len(buffers)
        self.idle = list(range(len(buffers)))

    def take(self):
        i = self.idle.pop(0)
        return i, self.buffers[i], self.free[i]

    def give(self, i, marks):
        assert i not in self.idle
        self.free[i] = tuple(marks)
        self.idle.append(i)


def build(nc, x_in, ctx_in, ctxT_in, wqT_in, wkvT_in, woT_in, bq_in, bkv_in, bo_in, pw_in, uT_in,
          w1T_in, w2T_in, b2_in, rT_in, wg_in, wu_in, wd_in, wsgu_in, wsd_in, out_pad):
    NB, S, D = x_in.shape
    T = NB * S
    TILES = S // P
    DT = D // P
    H, HD = 16, D // 16
    PAIRS = H // 2
    ROWS = P // 2
    L = w1T_in.shape[1]
    KR = 3
    NE = rT_in.shape[2]
    CAP = 128
    FH = wg_in.shape[2]
    FC = FH // 2
    ROW = D + NE + 1
    SLOTS = NE * CAP

    slots_dram = nc.dram_tensor("expert_slots", (SLOTS, ROW), F32, kind="Internal").ap()

    ctx = ExitStack()
    with ctx:
        def sb(name, shape, dt=F32):
            return ctx.enter_context(nc.sbuf_tensor(name, list(shape), dt))

        def ps(name):
            return ctx.enter_context(nc.psum_tensor(name, [P, 512], F32))

        def sem(name):
            return ctx.enter_context(nc.semaphore(name))

        pe = Engine(nc.tensor, sem("pe_done"))
        dve = Engine(nc.vector, sem("dve_done"))
        act = Engine(nc.scalar, sem("act_done"))
        pool = Engine(nc.gpsimd, sem("pool_done"))
        sp = Engine(nc.sync, sem("sp_done"))

        ident = sb("ident", (P, P))
        identr = sb("identr", (P, P), F32R)
        before = sb("before", (P, P), BF16)
        ones_bf = sb("ones_bf", (P, P), BF16)
        minus_half = sb("minus_half", (P, 2))
        low_rows = sb("low_rows", (P, 1))
        one_rows = sb("one_rows", (P, 1))
        token_no = sb("token_no", (P, 1))
        empty_rows = sb("empty_rows", (P, ROW))
        expert_end = sb("expert_end", (P, NE))

        wq = [sb(f"wq_{p}", (P, DT, D), F32R) for p in "hl"]
        wkv = [sb(f"wkv_{p}", (P, DT, 2 * D), F32R) for p in "hl"]
        wo = [sb(f"wo_{p}", (P, DT, D), F32R) for p in "hl"]
        wmix = [[sb(f"w{n}_{p}", (P, L, DT, D), F32R) for p in "hl"] for n in (1, 2)]
        bq = sb("bq", (P, D))
        bkv = sb("bkv", (P, 2 * D))
        bo = sb("bo", (P, D))
        b2 = sb("b2", (L, D))
        pw = sb("pw", (64, D))
        uT = sb("uT", (64, 3 * L))
        gT = [sb(f"gT_{p}", (P, DT, 3 * L), F32R) for p in "hl"]
        rT = sb("rT", (P, DT, NE))
        wsgu = sb("wsgu", (P, DT, 2 * FH))
        wsd = sb("wsd", (FC, 2, D))
        stage = sb("stage", (P, 2, 2 * D * DT))

        X = Ring([sb(f"x{i}", (P, TILES, D)) for i in range(4)])
        xhat = Ring([sb(f"xhat{i}", (P, TILES, D)) for i in range(2)])
        parts = Ring([[sb(f"part{i}{p}", (P, DT, S), F32R) for p in "hl"] for i in range(2)])
        ctxTr = Ring([sb(f"ctxT{i}", (P, DT, S)) for i in range(1)])
        tok_f = Ring([sb(f"tokf{i}", (P, D)) for i in range(1)])
        q_tok = Ring([sb(f"qtok{i}", (P, H, ROWS), F32R) for i in range(1)])
        q_st = [sb(f"qst{i}", (P, PAIRS, 2, S), F32R) for i in range(1)]
        k_st = sb("kst", (P, PAIRS, S), F32R)
        k1_raw = stage[:, :, :].rearrange("p i (n s) -> p (i n) s", s=S)
        v_x = [sb(f"vx{i}", (P, TILES, H, HD + 1)) for i in range(2)]
        ctx_tok = ctxTr.buffers[0]
        exps = sb("exps", (P, 2, TILES, 2, S))
        E = Ring([exps[:, i] for i in range(2)])
        nm = sb("nm", (P, TILES, H))
        nmp = sb("nmp", (P, TILES, 2, 2, PAIRS), F32R)
        mT = sb("mT", (4 * PAIRS, S), F32R)
        rsum = Ring([sb(f"rsum{i}", (P, H)) for i in range(2)])
        stats = Ring([sb(f"stats{i}", (P, 6)) for i in range(2)])
        mv = Ring([sb(f"mv{i}", (P, TILES, 2)) for i in range(2)])
        veps = Ring([sb(f"veps{i}", (P, TILES)) for i in range(2)])
        rstd = Ring([sb(f"rstd{i}", (P, TILES)) for i in range(2)])
        ctx_o = sb("ctx_o", (P, TILES, D))
        acc = sb("acc", (P, TILES, D))
        zb = sb("zb", (P, TILES, 3, L + 5))
        zr = sb("zr", (P, TILES, 3, L + 5))
        top = sb("top", (P, TILES, 3, 8))
        top3 = sb("top3", (P, TILES, 3, 8))
        zmask = sb("zmask", (P, TILES, 3, L))
        zexp = sb("zexp", (P, TILES, 3, L))
        zsum = sb("zsum", (P, TILES, 3))
        C = sb("C", (P, TILES, 3, L))
        c3T = sb("c3T", (L, S))
        row = Ring([sb(f"row{i}", (P, TILES, ROW)) for i in range(1)])
        xdT = sb("xdT", (P, DT, S))
        lmax = sb("lmax", (P, TILES))
        prob = sb("prob", (P, TILES, NE))
        psum_ = sb("psum_", (P, TILES))
        ptop = sb("ptop", (P, TILES, 8))
        prep = sb("prep", (P, TILES, NE))
        pmask = sb("pmask", (P, TILES, NE))
        pmask_bf = sb("pmask_bf", (P, TILES, NE), BF16)
        tsum = sb("tsum", (P, TILES))
        seen_cnt = [sb(f"seen_cnt{i}", (P, NE)) for i in range(2)]
        pos = sb("pos", (P, TILES, NE))
        sval = sb("sval", (P, TILES, NE))
        stop8 = sb("stop8", (P, TILES, 8))
        sidx = Ring([sb(f"sidx{i}", (P, TILES, 8), U32) for i in range(2)])
        sT_t = acc[0:FC, :, :]
        sT_a = sb("sT_a", (FC, 2, S))
        sT_h = sT_a
        NW = 2
        WE = 2 * DT * FH + 2 * D
        ew_mem = [exps[:, :, :, :, :].rearrange("p i t k s -> p (i t k s)")[:, 0:WE],
                  stage[:, :, :].rearrange("p i n -> p (i n)")[:, 0:WE]]
        ewg = [w[:, 0:DT * FH].rearrange("p (a f) -> p a f", a=DT) for w in ew_mem]
        ewu = [w[:, DT * FH:2 * DT * FH].rearrange("p (a f) -> p a f", a=DT) for w in ew_mem]
        ewd = [w[0:FC, 2 * DT * FH:WE].rearrange("p (a d) -> p a d", a=2) for w in ew_mem]
        NX = 2
        erow = [row.buffers[0][:, 0, :], row.buffers[0][:, 1, :]]
        eid = [sidx.buffers[0][:, 0, 0:1], sidx.buffers[0][:, 0, 1:2], sidx.buffers[0][:, 0, 2:3]]
        exT = [xhat.buffers[i][:, t, :] for i in range(2) for t in range(2)]
        ey = [X.buffers[i][:, 0, :] for i in range(3)]

        work = Ring([ps(f"work{i}") for i in range(4)])
        score = Ring([ps(f"score{i}") for i in range(2)])
        attn_out = [ps(f"attn_out{i}") for i in range(TILES)]
        attn_out_free = [()] * TILES

        c_w = Counter(sem("weights_in"))
        c_stage = [Counter(sem(f"stage_in{i}")) for i in range(2)]
        c_x = [Counter(sem(f"x_in{i}")) for i in range(4)]
        c_ctxT = Counter(sem("ctxT_in"))
        c_ctx = Counter(sem("ctx_in"))
        c_k1 = Counter(sem("k1_in"))
        c_m = Counter(sem("max_rows"))
        c_init = Counter(sem("slots_init"))
        c_out = [Counter(sem(f"out_store{i}")) for i in range(2)]
        c_scat = [Counter(sem(f"dispatch{i}")) for i in range(2)]
        c_ew = [Counter(sem(f"expert_w{i}")) for i in range(NW)]
        c_er = [Counter(sem(f"expert_rows{i}")) for i in range(NX)]
        c_add = Counter(sem("combine"))

        m_id0 = pool.do(lambda e: e.memset(ident[:, :], 0.0))
        m_id = pool.do(lambda e: e.affine_select(out=ident[:, :], in_=ident[:, :], compare_op=ALU.not_equal,
                                                 fill=1.0, base=0, pattern=[[-1, P]], channel_multiplier=1),
                       after=[m_id0])
        m_idr = act.do(lambda e: e.copy(identr[:, :], ident[:, :]), after=[m_id])
        m_b0 = pool.do(lambda e: e.memset(before[:, :], 1.0))
        m_before = pool.do(lambda e: e.affine_select(out=before[:, :], in_=before[:, :], compare_op=ALU.is_ge,
                                                     fill=0.0, base=-1, pattern=[[1, P]],
                                                     channel_multiplier=-1), after=[m_b0])
        m_ones = pool.do(lambda e: e.memset(ones_bf[:, :], 1.0))
        m_mh = pool.do(lambda e: e.memset(minus_half[:, :], -0.5))
        m_tok0 = pool.do(lambda e: e.iota(token_no[:, :], [[0, 1]], base=0, channel_multiplier=1,
                                          allow_small_or_imprecise_dtypes=True))
        m_er0 = pool.do(lambda e: e.memset(empty_rows[:, :], 0.0))
        m_er = pool.do(lambda e: e.tensor_scalar(empty_rows[:, ROW - 1:ROW], token_no[:, :], float(T), None,
                                                 ALU.add), after=[m_er0, m_tok0])
        m_end = pool.do(lambda e: e.iota(expert_end[:, :], [[-CAP, NE]], base=SLOTS, channel_multiplier=0,
                                         allow_small_or_imprecise_dtypes=True))
        m_lr = pool.do(lambda e: e.memset(low_rows[:, :], 0.0), after=[m_end])
        for base in (0, ROWS):
            m_lr = pool.do(lambda e, b=base: e.memset(low_rows[b + 32:b + 64, :], -1.0), after=[m_lr])
            m_lr = pool.do(lambda e, b=base: e.affine_select(
                out=low_rows[b + 32:b + 64, :], in_=low_rows[b + 32:b + 64, :], compare_op=ALU.is_ge, fill=0.0,
                base=-16, pattern=[[0, 1]], channel_multiplier=1), after=[m_lr])
        m_or = pool.do(lambda e: e.memset(one_rows[:, :], 0.0), after=[m_lr])
        for base in (0, ROWS):
            m_or = pool.do(lambda e, b=base: e.memset(one_rows[b + 32:b + 64, :], 1.0), after=[m_or])
            m_or = pool.do(lambda e, b=base: e.affine_select(
                out=one_rows[b + 32:b + 64, :], in_=one_rows[b + 32:b + 64, :], compare_op=ALU.is_gt, fill=0.0,
                base=16, pattern=[[0, 1]], channel_multiplier=-1), after=[m_or])
        m_qz = []
        for t in q_tok.buffers:
            m_qz.append(dve.do(lambda e, t=t: e.memset(t[:, :, :].bitcast(F32), 0.0)))
        for t in q_st:
            m_qz.append(pool.do(lambda e, t=t: e.memset(t[:, :, :, :].bitcast(F32), 0.0), after=[m_or]))
        for t in v_x:
            m_qz.append(dve.do(lambda e, t=t: e.memset(t[:, :, :, HD:HD + 1], 1.0)))
        m_qz.append(dve.do(lambda e: e.memset(zb[:, :, :, L:], SENTINEL)))
        m_qz.append(dve.do(lambda e: e.memset(top3[:, :, :, KR:], SENTINEL)))
        m_cnt0 = dve.do(lambda e: e.memset(seen_cnt[0][:, :], 0.0))

        m_init = sp.dma(lambda e: e.dma_start(slots_dram.rearrange("(e c) f -> c e f", c=CAP),
                                              empty_rows[:, :].unsqueeze(1).broadcast_to([P, NE, ROW])),
                        c_init, after=[m_er])

        m_init = sp.dma(lambda e: e.dma_start(out_pad[T:T + CAP, :], empty_rows[:, 0:D]), c_init, after=[m_er])

        def bcast(v, n):
            return v.rearrange("(a d) -> a d", a=1).broadcast_to([P, n])

        for dst, src in ((bq[:, :], bcast(bq_in, D)), (bkv[:, :], bcast(bkv_in, 2 * D)), (bo[:, :], bcast(bo_in, D)),
                         (b2[:, :], b2_in), (pw[:, :], pw_in), (uT[:, :], uT_in), (rT[:, :, :], rT_in),
                         (wsgu[:, :, :], wsgu_in), (wsd[:, :, :], wsd_in)):
            m_w = sp.dma(lambda e, d=dst, s=src: e.dma_start(d, s), c_w)

        _, wk, free = work.take()
        for dt in range(DT):
            m = pe.do(lambda e, wk=wk, dt=dt: e.matmul(wk[:, dt * 64:dt * 64 + 3 * L], pw[:, dt * P:(dt + 1) * P],
                                                      uT[:, :], start=True, stop=True), after=[m_w])
        gsrc = wk[:, 0:DT * 64].rearrange("p (t n) -> p t n", t=DT)[:, :, 0:3 * L]
        m1 = act.do(lambda e: e.copy(gT[0][:, :, :], gsrc), after=[m])
        m_g = dve.do(lambda e: e.tensor_tensor(gT[1][:, :, :], gsrc, gT[0][:, :, :].bitcast(F32), ALU.subtract),
                     after=[m, m1])
        work.give(0, [m1, m_g])

        stage_free = [(), ()]
        n_st = 0

        def load_parts(dst, src, n):
            nonlocal n_st
            i = n_st % 2
            n_st += 1
            buf = stage[:, i, 0:n]
            m = sp.dma(lambda e: e.dma_start(buf, src), c_stage[i], reuse=stage_free[i])
            mh = act.do(lambda e: e.copy(dst[0], buf), after=[m])
            ml = dve.do(lambda e: e.tensor_tensor(dst[1], buf, dst[0].bitcast(F32), ALU.subtract), after=[m, mh])
            stage_free[i] = (mh, ml)
            return ml

        def flat(t):
            return t.rearrange("p a b -> p (a b)")

        m_wq = load_parts([flat(w[:, :, :]) for w in wq], flat(wq_in_ap := wqT_in), DT * D)
        m_wkv = load_parts([flat(w[:, :, :]) for w in wkv], flat(wkvT_in), DT * 2 * D)
        m_wo = load_parts([flat(w[:, :, :]) for w in wo], flat(woT_in), DT * D)
        m_wmix = []
        mix_jobs = []
        for n, src in ((0, w1T_in), (1, w2T_in)):
            for l in range(0, L, 2):
                mix_jobs.append((n, l, src))

        def load_mix():
            for n, l, src in mix_jobs:
                m = load_parts([w[:, l:l + 2, :, :].rearrange("p l a b -> p (l a b)") for w in wmix[n]],
                               src[:, l:l + 2, :, :].rearrange("p l a b -> p (l a b)"), 2 * DT * D)
                m_wmix.append(m)
            return dve.do(lambda e: e.memset(k1_raw, 1.0), reuse=[*stage_free[0], *stage_free[1]])

        def layer_norm(src, src_marks, dst, dst_free, dst_scale_marks=()):
            im, mvb, fm = mv.take()
            iv, ve, fv = veps.take()
            ir, rs, fr = rstd.take()
            last = None
            for t in range(TILES):
                i, st, f = stats.take()
                m = dve.do(lambda e, st=st, t=t: e.bn_stats(st[:, :], src[:, t, :]), after=[src_marks[t]])
                m = dve.do(lambda e, st=st, t=t: e.bn_aggr(mvb[:, t, :], st[:, :]), after=[m], reuse=fm)
                stats.give(i, [m])
            m = dve.do(lambda e: e.tensor_scalar(ve[:, :], mvb[:, :, 1], EPS, None, ALU.add), after=[m], reuse=fv)
            m = pool.do(lambda e: e.tensor_tensor(rs[:, :], ve[:, :], minus_half[:, :], ALU.pow),
                        after=[m, m_mh], reuse=fr)
            veps.give(iv, [m])
            out = []
            for t in range(TILES):
                out.append(dve.do(lambda e, t=t: e.tensor_scalar(dst[:, t, 0:D], src[:, t, :], mvb[:, t, 0:1],
                                                                rs[:, t:t + 1], ALU.subtract, ALU.mult),
                                  after=[m], reuse=dst_free))
            mv.give(im, out)
            rstd.give(ir, out)
            return out

        def transposed(src, marks):
            i, wk, free = work.take()
            v = wk[:, :].rearrange("p (a b) -> p a b", a=DT)
            for t in range(TILES):
                for dt in range(DT):
                    m = pe.do(lambda e, t=t, dt=dt: e.transpose(v[:, dt, t * P:(t + 1) * P],
                                                                src[:, t, dt * P:(dt + 1) * P], ident[:, :]),
                              after=[marks[t], m_id], reuse=free)
            return i, v, m

        def transposed_parts(src, marks):
            i, v, m = transposed(src, marks)
            ip, (hi, lo), free = parts.take()
            mh = act.do(lambda e: e.copy(hi[:, :, :], v[:, :, :]), after=[m], reuse=free)
            ml = dve.do(lambda e: e.tensor_tensor(lo[:, :, :], v[:, :, :], hi[:, :, :].bitcast(F32), ALU.subtract),
                        after=[m, mh], reuse=free)
            work.give(i, [mh, ml])
            return ip, (hi, lo), ml, m

        TERMS = ((0, 0), (1, 0), (0, 1))

        def product3(out, left, right, after, reuse):
            n = 0
            for a, b in TERMS:
                for dt in range(DT):
                    lhs, rhs = left(a, dt), right(b, dt)
                    m = pe.do(lambda e: e.matmul(out, lhs, rhs, start=(n == 0), stop=(n == 3 * DT - 1)),
                              after=after, reuse=reuse)
                    n += 1
            return m

        def stack_tokens(src, src_mark, ring, is_q, src_is_psum_bias=None):
            i, st, free = ring.take()
            v = src.rearrange("p (h r) -> p h r", h=H)
            hi = st[:, :, 0:16]
            m1 = pool.do(lambda e: e.tensor_copy(hi, v), after=[src_mark, *m_qz], reuse=free)
            a, b = (48, 16) if is_q else (16, 48)
            m2 = act.do(lambda e: e.copy(st[:, :, a:a + 16], hi.bitcast(F32)), after=[m1], reuse=free)
            m3 = pool.do(lambda e: e.tensor_tensor(st[:, :, b:b + 16], v, hi.bitcast(F32), ALU.subtract),
                         after=[m1], reuse=free)
            return i, st, [m2, m3], [m1, m3]

        def stack_to_rows(st, marks, t, dst, is_q, dst_free):
            v = st[:, :, :].rearrange("p (n k) r -> p n (k r)", k=2)
            done = []
            for half in range(2):
                i, wk, free = work.take()
                for n in range(4):
                    m = pe.do(lambda e, n=n, half=half, wk=wk: e.transpose(
                        wk[:, n * P:(n + 1) * P].bitcast(F32R), v[:, half * 4 + n, :], identr[:, :]),
                        after=[*marks, m_idr], reuse=free)
                src = wk[:, :].rearrange("p (n t) -> p n t", n=4)
                pr = slice(half * 4, half * 4 + 4)
                tk = slice(t * P, (t + 1) * P)
                if is_q:
                    a = act.do(lambda e, src=src, pr=pr, tk=tk: e.copy(dst[0:ROWS, pr, 0, tk], src[0:ROWS]),
                               after=[m, *m_qz], reuse=dst_free)
                    b = act.do(lambda e, src=src, pr=pr, tk=tk: e.copy(dst[ROWS:P, pr, 1, tk], src[ROWS:P]),
                               after=[m], reuse=dst_free)
                    work.give(i, [a, b])
                    done += [a, b]
                else:
                    a = act.do(lambda e, src=src, pr=pr, tk=tk: e.activation(
                        dst[:, pr, tk], src, ACT.Identity, bias=one_rows[:, :]), after=[m, m_or], reuse=dst_free)
                    work.give(i, [a])
                    done.append(a)
            return done, m

        state = {"nm_free": (), "mmark": (), "kst_free": (), "qst_free": (), "vx_free": [(), ()],
                 "o_free": (), "acc_free": ()}

        def attention(qs, ks, vx, q_marks, k_marks, v_marks, dst, dst_free):
            red = []
            for p in range(PAIRS):
                for t in range(TILES):
                    i, wk, free = work.take()
                    for k in range(2):
                        m = pe.do(lambda e, wk=wk, p=p, t=t, k=k: e.matmul(
                            wk[:, k * S:(k + 1) * S], qs[:, p, k, t * P:(t + 1) * P], ks[:, p, :],
                            start=True, stop=True), after=[*q_marks, *k_marks], reuse=free)
                    r = dve.do(lambda e, wk=wk, p=p, t=t: e.tensor_reduce(
                        nm[:, t, 2 * p:2 * p + 2], wk[:, :].rearrange("p (k s) -> p k s", k=2), AX_X, ALU.max,
                        negate=True), after=[m], reuse=state["nm_free"])
                    work.give(i, [r])
                    yield 0.5
            v = nm[:, :, :].rearrange("p t (n k) -> p t k n", k=2)
            m1 = dve.do(lambda e: e.tensor_copy(nmp[:, :, 0, :, :], v), after=[r], reuse=state["mmark"])
            m2 = dve.do(lambda e: e.tensor_tensor(nmp[:, :, 1, :, :], v, nmp[:, :, 0, :, :].bitcast(F32),
                                                  ALU.subtract), after=[m1])
            state["nm_free"] = (m2,)
            i, wk, free = work.take()
            for t in range(TILES):
                m = pe.do(lambda e, t=t, wk=wk: e.transpose(
                    wk[0:4 * PAIRS, t * P:(t + 1) * P].bitcast(F32R),
                    nmp[:, t, :, :, :].rearrange("p a k n -> p (a k n)"), identr[:, :]),
                    after=[m1, m2], reuse=free)
            mc = act.do(lambda e, wk=wk: e.copy(mT[:, :], wk[0:4 * PAIRS, 0:S]), after=[m], reuse=state["mmark"])
            work.give(i, [mc])
            for part in range(2):
                for k in range(2):
                    r0 = (part * 2 + k) * PAIRS
                    mm = sp.dma(lambda e, part=part, k=k, r0=r0: e.dma_start(
                        qs[ROWS * k + 32 + part:ROWS * k + 33 + part, :, k, :].bitcast(F32),
                        mT[r0:r0 + PAIRS, :].bitcast(F32)), c_m,
                        after=[mc], reuse=[m, *q_marks])
            state["mmark"] = (mm,)
            for _ in range(4):
                yield 1.0
            pend = None

            def times_v(p, iE, Eb, marks):
                for t in range(TILES):
                    for k in range(2):
                        h = 2 * p + k
                        for s in range(TILES):
                            m = pe.do(lambda e, t=t, k=k, h=h, s=s: e.matmul(
                                attn_out[t][:, h * 17:(h + 1) * 17], Eb[:, s, k, t * P:(t + 1) * P],
                                vx[:, s, h, :], start=(s == 0), stop=(s == TILES - 1)),
                                after=[*marks, *v_marks], reuse=attn_out_free[t])
                E.give(iE, [m])
                return m

            for p in range(PAIRS):
                iE, Eb, fE = E.take()
                marks = []
                for s in range(TILES):
                    i, sc, free = score.take()
                    m = pe.do(lambda e, sc=sc, p=p, s=s: e.matmul(
                        sc[:, :], ks[:, p, s * P:(s + 1) * P], qs[:, p, :, :].rearrange("p k t -> p (k t)"),
                        start=True, stop=True), after=[mm], reuse=free)
                    a = act.do(lambda e, sc=sc, s=s, Eb=Eb: e.activation(
                        Eb[:, s, :, :].rearrange("p k t -> p (k t)"), sc[:, :], ACT.Exp, scale=0.25),
                        after=[m], reuse=fE)
                    score.give(i, [a])
                    marks.append(a)
                    yield 0.3
                if pend:
                    times_v(*pend)
                pend = (p, iE, Eb, marks)
                yield 0.5
            qk_last = m
            m = times_v(*pend)
            out = []
            for t in range(TILES):
                i, rs, fr = rsum.take()
                o = attn_out[t][:, 0:H * 17].rearrange("p (h r) -> p h r", h=H)
                r = dve.do(lambda e, o=o, rs=rs: e.reciprocal(rs[:, :], o[:, :, HD]), after=[m], reuse=fr)
                w = dve.do(lambda e, o=o, rs=rs, t=t: e.tensor_tensor(
                    dst[:, t, :].rearrange("p (h r) -> p h r", h=H), o[:, :, 0:HD],
                    rs[:, :].unsqueeze(2).broadcast_to([P, H, HD]), ALU.mult), after=[r], reuse=dst_free)
                attn_out_free[t] = (w,)
                rsum.give(i, [w])
                out.append(w)
            return out, qk_last, m

        xs = {}

        def stage_a(b):
            ix, xb, fx = X.take()
            mx = sp.dma(lambda e: e.dma_start(xb[:, :, :], x_in[b].rearrange("(t p) d -> p t d", p=P)), c_x[ix],
                        reuse=fx)
            i, ct, fc = ctxTr.take()
            mc = sp.dma(lambda e: e.dma_start(ct[:, :, :], ctxT_in[b].rearrange("(a p) s -> p a s", p=P)), c_ctxT,
                        reuse=fc)
            ic, (ch, cl), fcp = parts.take()
            c1 = pool.do(lambda e: e.tensor_copy(ch[:, :, :], ct[:, :, :]), after=[mc], reuse=fcp)
            c2 = pool.do(lambda e: e.tensor_tensor(cl[:, :, :], ct[:, :, :], ch[:, :, :].bitcast(F32), ALU.subtract),
                         after=[c1], reuse=fcp)
            ctxTr.give(i, [c2])
            if b >= 2:
                prefetch_v(b - 2)
            yield 0.5
            k_marks, v_marks = [], []
            for t in range(TILES):
                i, wk, free = work.take()
                tk = slice(t * P, (t + 1) * P)
                m = product3(wk[:, :], lambda a, dt, tk=tk: (ch, cl)[a][:, dt, tk], lambda a, dt: wkv[a][:, dt, :],
                             after=[c1, c2, m_wkv], reuse=free)
                ikf, kf, fk = tok_f.take()
                mk = dve.do(lambda e, wk=wk, kf=kf: e.tensor_tensor(kf[:, :], wk[:, 0:D], bkv[:, 0:D], ALU.add),
                            after=[m, m_w], reuse=fk)
                mvv = dve.do(lambda e, wk=wk, t=t: e.tensor_tensor(
                    v_x[0][:, t, :, 0:HD], wk[:, D:2 * D].rearrange("p (h r) -> p h r", h=H),
                    bkv[:, D:2 * D].rearrange("p (h r) -> p h r", h=H), ALU.add),
                    after=[m, *m_qz], reuse=state["vx_free"][0])
                work.give(i, [mk, mvv])
                v_marks.append(mvv)
                yield 1.5
                ik, st, ms, rd = stack_tokens(kf[:, :], mk, q_tok, False)
                tok_f.give(ikf, rd)
                yield 1.0
                d, rdm = stack_to_rows(st, ms, t, k_st, False, state["kst_free"])
                q_tok.give(ik, [rdm])
                k_marks += d
                yield 1.0
            parts.give(ic, [m])
            ih, xh, fh = xhat.take()
            mh = layer_norm(xb, [mx, mx], xh, fh)
            yield 1.0
            ip, (hi, lo), mp, rdm = transposed_parts(xh, mh)
            xhat.give(ih, [rdm])
            yield 1.0
            q_marks = []
            for t in range(TILES):
                i, wk, free = work.take()
                tk = slice(t * P, (t + 1) * P)
                m = product3(wk[:, 0:D], lambda a, dt, tk=tk: (hi, lo)[a][:, dt, tk], lambda a, dt: wq[a][:, dt, :],
                             after=[mp, m_wq], reuse=free)
                iqf, qf, fq = tok_f.take()
                mq = dve.do(lambda e, wk=wk, qf=qf: e.tensor_tensor(qf[:, :], wk[:, 0:D], bq[:, :], ALU.add),
                            after=[m, m_w], reuse=fq)
                work.give(i, [mq])
                yield 1.0
                iq, st, ms, rd = stack_tokens(qf[:, :], mq, q_tok, True)
                tok_f.give(iqf, rd)
                yield 1.0
                d, rdm = stack_to_rows(st, ms, t, q_st[0], True, state["qst_free"])
                q_tok.give(iq, [rdm])
                q_marks += d
                yield 1.0
            parts.give(ip, [m])
            out, qk_last, av_last = yield from attention(q_st[0], k_st, v_x[0], q_marks, k_marks, v_marks, ctx_o,
                                                         state["o_free"])
            state["kst_free"] = state["qst_free"] = (qk_last,)
            state["vx_free"][0] = (av_last,)
            mb = pool.do(lambda e: e.tensor_tensor(xb[:, :, :], xb[:, :, :],
                                                   bo[:, :].unsqueeze(1).broadcast_to([P, TILES, D]), ALU.add),
                         after=[mx, m_w], reuse=mh)
            yield 1.0
            ip, (hi, lo), mp, rdm = transposed_parts(ctx_o, out)
            state["o_free"] = (rdm,)
            yield 1.0
            marks = []
            for t in range(TILES):
                i, wk, free = work.take()
                tk = slice(t * P, (t + 1) * P)
                m = product3(wk[:, 0:D], lambda a, dt, tk=tk: (hi, lo)[a][:, dt, tk], lambda a, dt: wo[a][:, dt, :],
                             after=[mp, m_wo], reuse=free)
                r = dve.do(lambda e, wk=wk, t=t: e.tensor_tensor(xb[:, t, :], xb[:, t, :], wk[:, 0:D], ALU.add),
                           after=[m, mb])
                work.give(i, [r])
                marks.append(r)
            parts.give(ip, [m])
            xs[b] = (ix, xb, marks)
            yield 1.0

        bstate = {"acc": (), "C": (), "c3": (), "route": ()}

        def mixture(n, hi, lo, mp, mC, first):
            out = [None, None]
            for t in range(TILES):
                tk = slice(t * P, (t + 1) * P)
                prev = first[t]
                for l in range(0, L, 2):
                    i, wk, free = work.take()
                    m = product3(wk[:, :].rearrange("p (l d) -> p l d", l=2),
                                 lambda a, dt, tk=tk: (hi, lo)[a][:, dt, tk],
                                 lambda a, dt, l=l: wmix[n][a][:, l:l + 2, dt, :],
                                 after=[mp, m_wmix[n * (L // 2) + l // 2]], reuse=free)
                    for k in range(2):
                        c = C[:, t, n, l + k:l + k + 1]
                        src = wk[:, k * D:(k + 1) * D]
                        if prev is None:
                            prev = dve.do(lambda e, src=src, c=c, t=t: e.tensor_scalar(
                                acc[:, t, :], src, c, None, ALU.mult), after=[m, mC], reuse=bstate["acc"])
                        else:
                            prev = dve.do(lambda e, src=src, c=c, t=t: e.scalar_tensor_tensor(
                                acc[:, t, :], src, c, acc[:, t, :], ALU.mult, ALU.add), after=[m, mC, prev])
                    work.give(i, [prev])
                    yield 1.3
                out[t] = prev
            return out, m

        def stage_b(b):
            ix, xb, mx = xs[b]
            ih, xh, fh = xhat.take()
            mh = layer_norm(xb, mx, xh, fh)
            yield 1.0
            ip, (hi, lo), mp, rdm = transposed_parts(xh, mh)
            xhat.give(ih, [rdm])
            yield 1.0
            i, wk, free = work.take()
            for t in range(TILES):
                tk = slice(t * P, (t + 1) * P)
                m = product3(wk[:, t * 64:t * 64 + 3 * L], lambda a, dt, tk=tk: (hi, lo)[a][:, dt, tk],
                             lambda a, dt: gT[a][:, dt, :], after=[mp, m_g], reuse=free)
            zsrc = wk[:, 0:TILES * 64].rearrange("p (t n) -> p t n", t=TILES)[:, :, 0:3 * L].rearrange(
                "p t (s l) -> p t s l", s=3)
            mz = dve.do(lambda e: e.tensor_copy(zb[:, :, :, 0:L], zsrc), after=[m, *m_qz],
                        reuse=bstate["route"])
            work.give(i, [mz])
            yield 1.0
            for t in range(TILES):
                for s in range(3):
                    mt = dve.do(lambda e, t=t, s=s: e.max(top[:, t, s, :], zb[:, t, s, 0:L]), after=[mz])
            m3 = dve.do(lambda e: e.tensor_copy(top3[:, :, :, 0:KR], top[:, :, :, 0:KR]), after=[mt])
            for t in range(TILES):
                for s in range(3):
                    mr = dve.do(lambda e, t=t, s=s: e.match_replace(
                        out=zr[:, t, s, :], in_to_replace=top3[:, t, s, :], in_values=zb[:, t, s, :],
                        imm_value=TAKEN), after=[m3, mz])
            mk = dve.do(lambda e: e.tensor_tensor(zmask[:, :, :, :], zr[:, :, :, 0:L], zb[:, :, :, 0:L],
                                                  ALU.not_equal), after=[mr])
            md = dve.do(lambda e: e.tensor_tensor(zexp[:, :, :, :], zb[:, :, :, 0:L],
                                                  top[:, :, :, 0:1].broadcast_to([P, TILES, 3, L]),
                                                  ALU.subtract), after=[mt])
            me = act.do(lambda e: e.activation(zexp[:, :, :, :], zexp[:, :, :, :], ACT.Exp), after=[md])
            yield 1.0
            m = dve.do(lambda e: e.tensor_tensor(zexp[:, :, :, :], zexp[:, :, :, :], zmask[:, :, :, :], ALU.mult),
                       after=[me, mk])
            m2 = dve.do(lambda e: e.tensor_reduce(zsum[:, :, :], zexp[:, :, :, :], AX_X, ALU.add), after=[m])
            m2 = dve.do(lambda e: e.reciprocal(zsum[:, :, :], zsum[:, :, :]), after=[m2])
            mC = dve.do(lambda e: e.tensor_tensor(C[:, :, :, :], zexp[:, :, :, :],
                                                  zsum[:, :, :].unsqueeze(3).broadcast_to([P, TILES, 3, L]),
                                                  ALU.mult), after=[m2], reuse=bstate["C"])
            bstate["route"] = (mC,)
            yield 1.0
            out, ml = yield from mixture(0, hi, lo, mp, mC, [None, None])
            parts.give(ip, [ml])
            ih, hb, fh = xhat.take()
            mg = act.do(lambda e: e.activation(hb[:, :, :], acc[:, :, :], ACT.Gelu), after=out, reuse=fh)
            i, wk, free = work.take()
            for t in range(TILES):
                m = pe.do(lambda e, t=t: e.transpose(wk[0:L, t * P:(t + 1) * P], C[:, t, 2, :], ident[:, :]),
                          after=[mC], reuse=free)
            mc = act.do(lambda e: e.copy(c3T[:, :], wk[0:L, 0:S]), after=[m], reuse=bstate["c3"])
            work.give(i, [mc])
            i, wk, free = work.take()
            for t in range(TILES):
                m = pe.do(lambda e, t=t: e.matmul(wk[:, t * D:(t + 1) * D], c3T[:, t * P:(t + 1) * P], b2[:, :],
                                                  start=True, stop=True), after=[mc, m_w], reuse=free)
            bstate["c3"] = (m,)
            first = []
            for t in range(TILES):
                first.append(dve.do(lambda e, t=t: e.tensor_tensor(acc[:, t, :], xb[:, t, :],
                                                                   wk[:, t * D:(t + 1) * D], ALU.add),
                                    after=[m, mg, mx[t]]))
            work.give(i, first)
            yield 1.0
            ip, (hi, lo), mp, rdm = transposed_parts(hb, [mg, mg])
            xhat.give(ih, [rdm])
            yield 1.0
            out, ml = yield from mixture(1, hi, lo, mp, mC, first)
            parts.give(ip, [ml])
            bstate["C"] = (m, *out)
            mo = pool.do(lambda e: e.tensor_copy(xb[:, :, :], acc[:, :, :]), after=out, reuse=[*first, *mh])
            bstate["acc"] = (mo,)
            xs[b] = (ix, xb, [mo, mo])
            yield 1.0

        cstate = {"k1": (), "ctx": (), "kst": ()}
        pre = {}

        def prefetch_c(b):
            src = ctxT_in[b].rearrange("(n k r) s -> k r n s", k=2, r=HD)
            for k in range(2):
                for r0 in (0, 16, 48):
                    m = sp.dma(lambda e, k=k, r0=r0: e.dma_start(k1_raw[ROWS * k + r0:ROWS * k + r0 + 16, :, :],
                                                                 src[k]), c_k1, after=[m_k1one],
                               reuse=cstate["k1"])
            pre[b] = [m]

        def prefetch_v(b):
            mt = sp.dma(lambda e: e.dma_start(ctx_tok[:, :, :], ctx_in[b].rearrange("(t p) d -> p t d", p=P)),
                        c_ctx, reuse=ctxTr.free[0])
            pre[b].append(mt)

        def stage_c(b):
            ix, xb, mx = xs[b]
            if b + 2 >= NB:
                prefetch_v(b)
            mk, mt = pre[b]
            mv_ = pool.do(lambda e: e.tensor_copy(v_x[1][:, :, :, 0:HD],
                                                  ctx_tok[:, :, :].rearrange("p t (h r) -> p t h r", h=H)),
                          after=[mt, *m_qz], reuse=state["vx_free"][1])
            ctxTr.free[0] = (mv_,)
            m1 = pool.do(lambda e: e.tensor_copy(k_st[:, :, :], k1_raw), after=[mk],
                         reuse=state["kst_free"])
            m2 = dve.do(lambda e: e.scalar_tensor_tensor(k_st[:, :, :], k_st[:, :, :].bitcast(F32), low_rows[:, :],
                                                         k1_raw, ALU.mult, ALU.add), after=[m1, m_lr])
            cstate["k1"] = (m2,)
            ih, xh, fh = xhat.take()
            mh = layer_norm(xb, mx, xh, fh)
            yield 1.0
            q_marks = []
            rds = []
            for t in range(TILES):
                iq, st, ms, rd = stack_tokens(xh[:, t, :], mh[t], q_tok, True)
                rds += rd
                yield 1.0
                d, rdm = stack_to_rows(st, ms, t, q_st[0], True, state["qst_free"])
                q_tok.give(iq, [rdm])
                q_marks += d
                yield 1.0
            xhat.give(ih, rds)
            out, qk_last, av_last = yield from attention(q_st[0], k_st, v_x[1], q_marks, [m2], [mv_], ctx_o,
                                                         state["o_free"])
            state["kst_free"] = state["qst_free"] = (qk_last,)
            state["vx_free"][1] = (av_last,)
            mo = pool.do(lambda e: e.tensor_tensor(xb[:, :, :], xb[:, :, :], ctx_o[:, :, :], ALU.add),
                         after=out, reuse=mh)
            state["o_free"] = (mo,)
            xs[b] = (ix, xb, [mo, mo])
            yield 1.0

        dstate = {"xdT": (), "sT": (), "cnt": m_cnt0, "out": [], "route": ()}

        def stage_d(b):
            ix, xb, mx = xs[b]
            ir, rw, fr = row.take()
            mh = layer_norm(xb, mx, rw, fr)
            yield 1.0
            i, v, m = transposed(rw, mh)
            mT_ = act.do(lambda e: e.copy(xdT[:, :, :], v[:, :, :]), after=[m], reuse=dstate["xdT"])
            work.give(i, [mT_])
            yield 1.0
            i, wk, free = work.take()
            for t in range(TILES):
                for dt in range(DT):
                    m = pe.do(lambda e, t=t, dt=dt: e.matmul(wk[:, t * NE:(t + 1) * NE],
                                                             xdT[:, dt, t * P:(t + 1) * P], rT[:, dt, :],
                                                             start=(dt == 0), stop=(dt == DT - 1)),
                              after=[mT_, m_w], reuse=free)
            lg = wk[:, 0:TILES * NE].rearrange("p (t n) -> p t n", t=TILES)
            ma = dve.do(lambda e: e.tensor_reduce(lmax[:, :], lg, AX_X, ALU.max), after=[m], reuse=dstate["route"])
            ms = dve.do(lambda e: e.tensor_tensor(prob[:, :, :], lg,
                                                  lmax[:, :].unsqueeze(2).broadcast_to([P, TILES, NE]),
                                                  ALU.subtract), after=[ma])
            work.give(i, [ms])
            me = act.do(lambda e: e.activation(prob[:, :, :], prob[:, :, :], ACT.Exp), after=[ms])
            yield 1.0
            m = dve.do(lambda e: e.tensor_reduce(psum_[:, :], prob[:, :, :], AX_X, ALU.add), after=[me])
            m = dve.do(lambda e: e.reciprocal(psum_[:, :], psum_[:, :]), after=[m])
            mp = dve.do(lambda e: e.tensor_tensor(prob[:, :, :], prob[:, :, :],
                                                  psum_[:, :].unsqueeze(2).broadcast_to([P, TILES, NE]), ALU.mult),
                        after=[m])
            for t in range(TILES):
                mt = dve.do(lambda e, t=t: e.max(ptop[:, t, :], prob[:, t, :]), after=[mp])
            for t in range(TILES):
                mr = dve.do(lambda e, t=t: e.match_replace(out=prep[:, t, :], in_to_replace=ptop[:, t, :],
                                                           in_values=prob[:, t, :], imm_value=-1.0), after=[mt])
            mk = dve.do(lambda e: e.tensor_scalar(pmask[:, :, :], prep[:, :, :], 0.0, None, ALU.is_lt), after=[mr])
            mkb = pool.do(lambda e: e.tensor_copy(pmask_bf[:, :, :], pmask[:, :, :]), after=[mk])
            m = dve.do(lambda e: e.tensor_reduce(tsum[:, :], ptop[:, :, :], AX_X, ALU.add), after=[mt])
            m = dve.do(lambda e: e.reciprocal(tsum[:, :], tsum[:, :]), after=[m])
            m = dve.do(lambda e: e.tensor_tensor(prob[:, :, :], prob[:, :, :],
                                                 tsum[:, :].unsqueeze(2).broadcast_to([P, TILES, NE]), ALU.mult),
                       after=[m])
            mw = dve.do(lambda e: e.tensor_tensor(rw[:, :, D:D + NE], prob[:, :, :], pmask[:, :, :], ALU.mult),
                        after=[m, mk], reuse=fr)
            yield 1.0
            for t in range(TILES):
                mn = dve.do(lambda e, t=t: e.tensor_scalar(rw[:, t, ROW - 1:ROW], token_no[:, :],
                                                           float(b * S + t * P), None, ALU.add),
                            after=[m_tok0], reuse=fr)
            i, wk, free = work.take()
            for t in range(TILES):
                m = pe.do(lambda e, t=t: e.matmul(wk[:, t * NE:(t + 1) * NE], before[:, :], pmask_bf[:, t, :],
                                                  start=True, stop=(t == 0)), after=[mkb, m_before], reuse=free)
                if t:
                    m = pe.do(lambda e: e.matmul(wk[:, NE:2 * NE], ones_bf[:, :], pmask_bf[:, 0, :],
                                                 start=False, stop=True), after=[m_ones])
            for t in range(TILES):
                m = pe.do(lambda e, t=t: e.matmul(wk[:, 2 * NE:3 * NE], ones_bf[:, :], pmask_bf[:, t, :],
                                                  start=(t == 0), stop=(t == 1)))
            old, new = seen_cnt[b % 2], seen_cnt[(b + 1) % 2]
            m1 = dve.do(lambda e: e.tensor_tensor(pos[:, :, :], wk[:, 0:2 * NE].rearrange("p (t n) -> p t n", t=TILES),
                                                  old[:, :].unsqueeze(1).broadcast_to([P, TILES, NE]), ALU.add),
                        after=[m, dstate["cnt"]])
            dstate["cnt"] = dve.do(lambda e: e.tensor_tensor(new[:, :], wk[:, 2 * NE:3 * NE], old[:, :], ALU.add),
                                   after=[m, m1])
            work.give(i, [m1, dstate["cnt"]])
            yield 1.0
            m2 = dve.do(lambda e: e.scalar_tensor_tensor(pmask[:, :, :], pos[:, :, :], float(CAP), pmask[:, :, :],
                                                         ALU.is_lt, ALU.mult), after=[m1, mkb, mw])
            m3 = dve.do(lambda e: e.tensor_tensor(sval[:, :, :], expert_end[:, :].unsqueeze(1).broadcast_to(
                [P, TILES, NE]), pos[:, :, :], ALU.subtract), after=[m1, m_end])
            m3 = dve.do(lambda e: e.tensor_tensor(sval[:, :, :], sval[:, :, :], pmask[:, :, :], ALU.mult),
                        after=[m2, m3])
            for t in range(TILES):
                m4 = dve.do(lambda e, t=t: e.max(stop8[:, t, :], sval[:, t, :]), after=[m3])
            isx, six, fs = sidx.take()
            m5 = dve.do(lambda e: e.tensor_scalar(six[:, :, :], stop8[:, :, :], -1.0, float(SLOTS), ALU.mult,
                                                  ALU.add), after=[m4], reuse=fs)
            dstate["route"] = (m5,)
            yield 1.0
            for t in range(TILES):
                for k in range(8):
                    msc = pool.dma(lambda e, t=t, k=k: e.indirect_dma_start(
                        out=slots_dram, out_offset=bass.IndirectOffsetOnAxis(ap=six[:, t, k:k + 1], axis=0),
                        in_=rw[:, t, :], in_offset=None, bounds_check=SLOTS - 1, oob_is_err=False),
                        c_scat[ir], after=[m5, mn, mw, *mh, m_init])
            row.give(ir, [msc])
            sidx.give(isx, [msc])
            yield 1.0
            banks = []
            for half in range(2):
                i, wk, free = work.take()
                for f in range(2):
                    c0 = half * FH + f * FC
                    for dt in range(DT):
                        m = pe.do(lambda e, wk=wk, f=f, dt=dt, c0=c0: e.matmul(
                            wk[0:FC, f * S:(f + 1) * S], wsgu[:, dt, c0:c0 + FC], xdT[:, dt, :],
                            start=(dt == 0), stop=(dt == DT - 1)), after=[mT_, m_w], reuse=free)
                banks.append((i, wk, m))
                yield 1.7
            dstate["xdT"] = (m,)
            (ig, gk, mg), (iu, uk, mu) = banks
            gv = gk[0:FC, :].rearrange("p (f s) -> p f s", f=2)
            uv = uk[0:FC, :].rearrange("p (f s) -> p f s", f=2)
            ma = act.do(lambda e: e.activation(sT_t[:, :, :], gv, ACT.Tanh, scale=0.5), after=[mg],
                        reuse=bstate["acc"])
            mb = dve.do(lambda e: e.scalar_tensor_tensor(sT_a[:, :, :], sT_t[:, :, :], 1.0, gv, ALU.add, ALU.mult),
                        after=[ma, mg], reuse=dstate["sT"])
            mc = dve.do(lambda e: e.scalar_tensor_tensor(sT_h[:, :, :], sT_a[:, :, :], 0.5, uv, ALU.mult, ALU.mult),
                        after=[mb, mu])
            work.give(ig, [ma, mb])
            work.give(iu, [mc])
            bstate["acc"] = (*bstate["acc"], mb)
            yield 1.0
            i, wk, free = work.take()
            for t in range(TILES):
                for f in range(2):
                    m = pe.do(lambda e, t=t, f=f: e.matmul(wk[:, t * D:(t + 1) * D], sT_h[:, f, t * P:(t + 1) * P],
                                                           wsd[:, f, :], start=(f == 0), stop=(f == 1)),
                              after=[mc, m_w], reuse=free)
            dstate["sT"] = (m,)
            mo = dve.do(lambda e: e.tensor_tensor(xb[:, :, :], xb[:, :, :], wk[:, :].rearrange(
                "p (t d) -> p t d", t=TILES), ALU.add), after=[m, *mh])
            work.give(i, [mo])
            mst = sp.dma(lambda e: e.dma_start(out_pad[b * S:(b + 1) * S, :].rearrange("(t p) d -> p t d", p=P),
                                               xb[:, :, :]), c_out[b % 2], after=[mo])
            X.give(ix, [mst])
            dstate["out"].append(mst)
            dstate["scat"] = dstate.get("scat", []) + [msc]
            yield 1.0

        def load_expert(n):
            i = n % NW
            sp.dma(lambda e: e.dma_start(ewg[i][:, :, :], wg_in[n].rearrange("(a p) f -> p a f", p=P)), c_ew[i],
                   reuse=ew_free[i])
            sp.dma(lambda e: e.dma_start(ewu[i][:, :, :], wu_in[n].rearrange("(a p) f -> p a f", p=P)), c_ew[i])
            return sp.dma(lambda e: e.dma_start(ewd[i][:, :, :], wd_in[n].rearrange("(a p) d -> p a d", p=FC)),
                          c_ew[i])

        def together(*streams):
            clocks = [0.0] * len(streams)
            alive = list(range(len(streams)))
            while alive:
                n = min(alive, key=lambda j: clocks[j])
                try:
                    clocks[n] += next(streams[n])
                except StopIteration:
                    alive.remove(n)

        def chain(*gens):
            for g in gens:
                yield from g

        def loads_c(b):
            prefetch_c(b)
            yield 0.0

        ew_marks = {}
        for step in range(NB + 3):
            one, two = [], []
            if step < NB:
                one.append(stage_a(step))
            if 0 <= step - 2 < NB:
                one.append(stage_c(step - 2))
            if 0 <= step - 1 < NB:
                two.append(stage_b(step - 1))
            if 0 <= step - 3 < NB:
                two.append(stage_d(step - 3))
            if 0 <= step - 2 < NB:
                prefetch_c(step - 2)
            if step == 1:
                m_k1one = load_mix()
            together(chain(*one), chain(*two))

        quiet = [(q.sem, q.count) for q in (pe, dve, act, pool)]
        ew_free = [tuple(quiet)] * NW
        for n in range(NW):
            ew_marks[n] = load_expert(n)


        gathered = [*dstate["out"][-2:], *dstate["scat"][-2:]]
        last_add = None
        tail_marks = [m for m in (dve.sem, act.sem, pe.sem, pool.sem)]
        quiet = [(q.sem, q.count) for q in (pe, dve, act, pool)]
        er_free = [tuple(quiet)] * NX
        ey_free = [tuple(quiet)] * 3
        exT_free = [tuple(quiet)] * 4
        id_free = [tuple(quiet)] * NX

        def load_rows(n):
            i = n % NX
            return sp.dma(lambda e: e.dma_start(erow[i], slots_dram[n * CAP:(n + 1) * CAP, :]), c_er[i],
                          after=gathered, reuse=er_free[i])

        er_marks = {n: load_rows(n) for n in range(1)}
        hid_free = [tuple(quiet)] * 2
        for n in range(NE):
            if n + 1 < NE:
                er_marks[n + 1] = load_rows(n + 1)
            rwt, mr = erow[n % NX], er_marks[n]
            mi = dve.do(lambda e, n=n, rwt=rwt: e.tensor_copy(eid[n % NX], rwt[:, ROW - 1:ROW]), after=[mr],
                        reuse=id_free[n % NX])
            i, wk, free = work.take()
            for dt in range(DT):
                m = pe.do(lambda e, dt=dt, wk=wk, rwt=rwt: e.transpose(wk[:, dt * P:(dt + 1) * P],
                                                                      rwt[:, dt * P:(dt + 1) * P], ident[:, :]),
                          after=[mr], reuse=free)
            xT = exT[n % 4].rearrange("p (a t) -> p a t", a=DT)
            mt = act.do(lambda e, wk=wk, xT=xT: e.copy(xT, wk[:, 0:D].rearrange("p (a t) -> p a t", a=DT)),
                        after=[m], reuse=exT_free[n % 4])
            work.give(i, [mt])
            i, wk, free = work.take()
            w = n % NW
            for j, (wt, f) in enumerate(((ewg[w], 0), (ewg[w], 1), (ewu[w], 0), (ewu[w], 1))):
                for dt in range(DT):
                    m = pe.do(lambda e, wk=wk, j=j, wt=wt, f=f, dt=dt, xT=xT: e.matmul(
                        wk[0:FC, j * P:(j + 1) * P], wt[:, dt, f * FC:(f + 1) * FC], xT[:, dt, :],
                        start=(dt == 0), stop=(dt == DT - 1)), after=[mt, ew_marks[n]], reuse=free)
            exT_free[n % 4] = (m,)
            gv = wk[0:FC, 0:2 * P].rearrange("p (f s) -> p f s", f=2)
            uv = wk[0:FC, 2 * P:4 * P].rearrange("p (f s) -> p f s", f=2)
            act_h = sT_t[:, :, (n % 2) * P:(n % 2 + 1) * P]
            mul_h = sT_h[:, :, (n % 2) * P:(n % 2 + 1) * P]
            ma = act.do(lambda e, gv=gv, h=act_h: e.activation(h, gv, ACT.Silu), after=[m],
                        reuse=hid_free[n % 2])
            mb = dve.do(lambda e, uv=uv, h=act_h, o=mul_h: e.tensor_tensor(o, h, uv, ALU.mult), after=[ma, m],
                        reuse=hid_free[n % 2])
            work.give(i, [ma, mb])
            i, wk, free = work.take()
            for f in range(2):
                m = pe.do(lambda e, wk=wk, f=f, o=mul_h, w=w: e.matmul(wk[:, 0:D], o[:, f, :], ewd[w][:, f, :],
                                                                    start=(f == 0), stop=(f == 1)),
                          after=[mb], reuse=free)
            ew_free[w] = (m,)
            hid_free[n % 2] = (m, mb)
            if n + NW < NE:
                ew_marks[n + NW] = load_expert(n + NW)
            y = ey[n % 3]
            my = dve.do(lambda e, wk=wk, n=n, rwt=rwt, y=y: e.tensor_scalar(y, wk[:, 0:D], rwt[:, D + n:D + n + 1],
                                                                          None, ALU.mult), after=[m],
                        reuse=ey_free[n % 3])
            work.give(i, [my])
            er_free[n % NX] = (my, mi, mt)
            last_add = pool.dma(lambda e, n=n, y=y: e.indirect_dma_start(
                out=out_pad, out_offset=bass.IndirectOffsetOnAxis(ap=eid[n % NX], axis=0), in_=y, in_offset=None,
                bounds_check=T + CAP - 1, oob_is_err=True, compute_op=ALU.add), c_add, after=[my, mi] + (
                    [last_add] if last_add else gathered))
            ey_free[n % 3] = (last_add,)
            id_free[n % NX] = (last_add,)
        pool.wait([last_add])
        sp.wait([last_add, m_init])



def kernel(**inputs):
    import concourse.bacc as bacc
    from concourse.bass_utils import run_bass_kernel_spmd

    a = {k: np.asarray(v) for k, v in inputs.items()}

    def split_rows(w):
        return np.ascontiguousarray(w.reshape(-1, P, w.shape[1]).transpose(1, 0, 2))

    def mixture_rows(w):
        n, o, i = w.shape
        return np.ascontiguousarray(w.transpose(0, 2, 1).reshape(n, i // P, P, o).transpose(2, 0, 1, 3))

    fc = a["L1_ffn_ws_down"].shape[0] // 2
    arrays = {
        "x": a["x"],
        "ctx": a["ctx_1024"],
        "ctxT": np.ascontiguousarray(a["ctx_1024"].transpose(0, 2, 1)),
        "wqT": split_rows(a["L0_xattn_Wq"].T),
        "wkvT": split_rows(np.concatenate([a["L0_xattn_Wk"].T, a["L0_xattn_Wv"].T], 1)),
        "woT": split_rows(a["L0_xattn_Wo"].T),
        "bq": a["L0_xattn_bq"],
        "bkv": np.concatenate([a["L0_xattn_bk"], a["L0_xattn_bv"]]),
        "bo": a["L0_xattn_bo"],
        "pw": a["L0_ffn_P_w"],
        "uT": np.ascontiguousarray(np.concatenate([a["L0_ffn_U1"], a["L0_ffn_U2"], a["L0_ffn_U3"]]).T),
        "w1T": mixture_rows(a["L0_ffn_W1"]),
        "w2T": mixture_rows(a["L0_ffn_W2"]),
        "b2": a["L0_ffn_b2"],
        "rT": split_rows(a["L1_ffn_router_w"].T),
        "wg": a["L1_ffn_w_gate"],
        "wu": a["L1_ffn_w_up"],
        "wd": a["L1_ffn_w_down"],
        "wsgu": split_rows(a["L1_ffn_ws_gate_up"]),
        "wsd": np.ascontiguousarray(a["L1_ffn_ws_down"].reshape(2, fc, -1).transpose(1, 0, 2)),
    }
    nc = bacc.Bacc("TRN2", target_bir_lowering=False, num_devices=1, dynamic_dma_scratch_size=4096)
    args = [nc.dram_tensor("in_" + n, v.shape, mybir.dt.from_np(v.dtype), kind="ExternalInput").ap()
            for n, v in arrays.items()]
    nb, s, d = a["x"].shape
    out = nc.dram_tensor("out", (nb * s + P, d), F32, kind="ExternalOutput").ap()
    build(nc, *args, out)
    r = run_bass_kernel_spmd(nc, [{"in_" + n: v for n, v in arrays.items()}], core_ids=[0])
    return r.results[0]["out"][:nb * s].reshape(nb, s, d)
```

```python
from contextlib import ExitStack

import numpy as np

import concourse.bass as bass
from concourse import mybir

F32 = mybir.dt.float32
F32R = mybir.dt.float32r
BF16 = mybir.dt.bfloat16
U32 = mybir.dt.uint32
ALU = mybir.AluOpType
ACT = mybir.ActivationFunctionType
AX_X = mybir.AxisListType.X

P = 128
EPS = 1e-5
SENTINEL = -1.0e30
BLOCKED = "blocked"
TAKEN = -3.0e30


DMA_NS = 2500
HANDOVER_NS = 100


class Plan:

    def __init__(self):
        self.end = {}

    def after(self, marks):
        return max([self.end[(sem.name, value)] for sem, value in marks], default=0)


class Engine:

    def __init__(self, engine, sem, plan, usual_ns):
        self.engine, self.sem, self.count, self.seen = engine, sem, 0, {}
        self.plan, self.usual_ns, self.clock = plan, usual_ns, 0

    def wait(self, marks):
        for sem, value in marks:
            if self.seen.get(sem.name, 0) < value:
                self.seen[sem.name] = value
                self.engine.wait_ge(sem, value)

    def do(self, fn, after=(), reuse=(), ns=None):
        self.wait(after)
        self.wait(reuse)
        self.count += 1
        fn(self.engine).then_inc(self.sem, 1)
        self.clock = max(self.clock, self.plan.after(after), self.plan.after(reuse)) + (ns or self.usual_ns)
        self.plan.end[(self.sem.name, self.count)] = self.clock + HANDOVER_NS
        return (self.sem, self.count)

    def dma(self, fn, counter, after=(), reuse=()):
        self.wait(after)
        self.wait(reuse)
        counter.count += 16
        fn(self.engine).then_inc(counter.sem, 16)
        start = max(self.clock, self.plan.after(after), self.plan.after(reuse))
        self.clock = start + self.usual_ns
        self.plan.end[(counter.sem.name, counter.count)] = start + DMA_NS
        return (counter.sem, counter.count)


class Counter:
    def __init__(self, sem):
        self.sem, self.count = sem, 0


class Ring:

    def __init__(self, buffers):
        self.buffers, self.free = buffers, [()] * len(buffers)
        self.idle = list(range(len(buffers)))

    def take(self):
        i = self.idle.pop(0)
        return i, self.buffers[i], self.free[i]

    def give(self, i, marks):
        assert i not in self.idle
        self.free[i] = tuple(marks)
        self.idle.append(i)


def build(nc, x_in, ctx_in, ctxT_in, wqT_in, wkvT_in, woT_in, bq_in, bkv_in, bo_in, pw_in, uT_in,
          w1T_in, w2T_in, b2_in, rT_in, wg_in, wu_in, wd_in, wsgu_in, wsd_in, out_pad):
    NB, S, D = x_in.shape
    T = NB * S
    TILES = S // P
    DT = D // P
    H, HD = 16, D // 16
    PAIRS = H // 2
    ROWS = P // 2
    L = w1T_in.shape[1]
    KR = 3
    NE = rT_in.shape[2]
    CAP = 128
    FH = wg_in.shape[2]
    FC = FH // 2
    ROW = D + NE + 1
    SLOTS = NE * CAP

    slots_dram = nc.dram_tensor("expert_slots", (SLOTS, ROW), F32, kind="Internal").ap()

    ctx = ExitStack()
    with ctx:
        def sb(name, shape, dt=F32):
            return ctx.enter_context(nc.sbuf_tensor(name, list(shape), dt))

        def ps(name):
            return ctx.enter_context(nc.psum_tensor(name, [P, 512], F32))

        def sem(name):
            return ctx.enter_context(nc.semaphore(name))

        plan = Plan()
        pe = Engine(nc.tensor, sem("pe_done"), plan, 100)
        dve = Engine(nc.vector, sem("dve_done"), plan, 200)
        act = Engine(nc.scalar, sem("act_done"), plan, 480)
        pool = Engine(nc.gpsimd, sem("pool_done"), plan, 1200)
        sp = Engine(nc.sync, sem("sp_done"), plan, 60)

        ident = sb("ident", (P, P))
        identr = sb("identr", (P, P), F32R)
        before = sb("before", (P, P), BF16)
        ones_bf = sb("ones_bf", (P, P), BF16)
        minus_half = sb("minus_half", (P, 2))
        low_rows = sb("low_rows", (P, 1))
        one_rows = sb("one_rows", (P, 1))
        token_no = sb("token_no", (P, 1))
        empty_rows = sb("empty_rows", (P, ROW))
        expert_end = sb("expert_end", (P, NE))

        wq = [sb(f"wq_{p}", (P, DT, D), F32R) for p in "hl"]
        wkv = [sb(f"wkv_{p}", (P, DT, 2 * D), F32R) for p in "hl"]
        wo = [sb(f"wo_{p}", (P, DT, D), F32R) for p in "hl"]
        wmix = [[sb(f"w{n}_{p}", (P, L, DT, D), F32R) for p in "hl"] for n in (1, 2)]
        bq = sb("bq", (P, D))
        bkv = sb("bkv", (P, 2 * D))
        bo = sb("bo", (P, D))
        b2 = sb("b2", (L, D))
        pw = sb("pw", (64, D))
        uT = sb("uT", (64, 3 * L))
        gT = [sb(f"gT_{p}", (P, DT, 3 * L), F32R) for p in "hl"]
        rT = sb("rT", (P, DT, NE))
        wsgu = sb("wsgu", (P, DT, 2 * FH))
        wsd = sb("wsd", (FC, 2, D))
        stage = sb("stage", (P, 2, 2 * D * DT))

        X = Ring([sb(f"x{i}", (P, TILES, D)) for i in range(4)])
        xhat = Ring([sb(f"xhat{i}", (P, TILES, D)) for i in range(2)])
        parts = Ring([[sb(f"part{i}{p}", (P, DT, S), F32R) for p in "hl"] for i in range(2)])
        ctxTr = Ring([sb(f"ctxT{i}", (P, DT, S)) for i in range(1)])
        tok_f = Ring([sb(f"tokf{i}", (P, D)) for i in range(1)])
        q_tok = Ring([sb(f"qtok{i}", (P, H, ROWS), F32R) for i in range(1)])
        q_st = [sb(f"qst{i}", (P, PAIRS, 2, S), F32R) for i in range(1)]
        k_st = sb("kst", (P, PAIRS, S), F32R)
        k1_raw = stage[:, :, :].rearrange("p i (n s) -> p (i n) s", s=S)
        v_x = [sb(f"vx{i}", (P, TILES, H, HD + 1)) for i in range(2)]
        ctx_tok = ctxTr.buffers[0]
        exps = sb("exps", (P, 2, TILES, 2, S))
        E = Ring([exps[:, i] for i in range(2)])
        nm = sb("nm", (P, TILES, H))
        nmp = sb("nmp", (P, TILES, 2, 2, PAIRS), F32R)
        mT = sb("mT", (4 * PAIRS, S), F32R)
        rsum = Ring([sb(f"rsum{i}", (P, H)) for i in range(2)])
        stats = Ring([sb(f"stats{i}", (P, 6)) for i in range(2)])
        mv = Ring([sb(f"mv{i}", (P, TILES, 2)) for i in range(2)])
        veps = Ring([sb(f"veps{i}", (P, TILES)) for i in range(2)])
        rstd = Ring([sb(f"rstd{i}", (P, TILES)) for i in range(2)])
        ctx_o = sb("ctx_o", (P, TILES, D))
        acc = sb("acc", (P, TILES, D))
        zb = sb("zb", (P, TILES, 3, L + 5))
        zr = sb("zr", (P, TILES, 3, L + 5))
        top = sb("top", (P, TILES, 3, 8))
        top3 = sb("top3", (P, TILES, 3, 8))
        zmask = sb("zmask", (P, TILES, 3, L))
        zexp = sb("zexp", (P, TILES, 3, L))
        zsum = sb("zsum", (P, TILES, 3))
        C = sb("C", (P, TILES, 3, L))
        c3T = sb("c3T", (L, S))
        row = Ring([sb(f"row{i}", (P, TILES, ROW)) for i in range(1)])
        xdT = sb("xdT", (P, DT, S))
        lmax = sb("lmax", (P, TILES))
        prob = sb("prob", (P, TILES, NE))
        psum_ = sb("psum_", (P, TILES))
        ptop = sb("ptop", (P, TILES, 8))
        prep = sb("prep", (P, TILES, NE))
        pmask = sb("pmask", (P, TILES, NE))
        pmask_bf = sb("pmask_bf", (P, TILES, NE), BF16)
        tsum = sb("tsum", (P, TILES))
        seen_cnt = [sb(f"seen_cnt{i}", (P, NE)) for i in range(2)]
        pos = sb("pos", (P, TILES, NE))
        sval = sb("sval", (P, TILES, NE))
        stop8 = sb("stop8", (P, TILES, 8))
        sidx = Ring([sb(f"sidx{i}", (P, TILES, 8), U32) for i in range(2)])
        sT_a = sb("sT_a", (FC, 2, S))
        NW = 2
        WE = 2 * DT * FH + 2 * D
        ew_mem = [exps[:, :, :, :, :].rearrange("p i t k s -> p (i t k s)")[:, 0:WE],
                  stage[:, :, :].rearrange("p i n -> p (i n)")[:, 0:WE]]
        ewg = [w[:, 0:DT * FH].rearrange("p (a f) -> p a f", a=DT) for w in ew_mem]
        ewu = [w[:, DT * FH:2 * DT * FH].rearrange("p (a f) -> p a f", a=DT) for w in ew_mem]
        ewd = [w[0:FC, 2 * DT * FH:WE].rearrange("p (a d) -> p a d", a=2) for w in ew_mem]
        NX = 2
        erow = [row.buffers[0][:, 0, :], row.buffers[0][:, 1, :]]
        eid = [sidx.buffers[0][:, 0, 0:1], sidx.buffers[0][:, 0, 1:2], sidx.buffers[0][:, 0, 2:3]]
        exT = [xhat.buffers[i][:, t, :] for i in range(2) for t in range(2)]
        ey = [X.buffers[i][:, 0, :] for i in range(3)]

        work = Ring([ps(f"work{i}") for i in range(4)])
        score = Ring([ps(f"score{i}") for i in range(2)])
        HB, HQ = 32, 4
        attn_out = [ps(f"attn_out{i}") for i in range(2)]

        def outT(g):
            return attn_out[g // 2][:, (g % 2) * S:(g % 2 + 1) * S]

        attn_out_free = [()] * TILES

        c_w = Counter(sem("weights_in"))
        c_stage = [Counter(sem(f"stage_in{i}")) for i in range(2)]
        c_x = [Counter(sem(f"x_in{i}")) for i in range(4)]
        c_ctxT = Counter(sem("ctxT_in"))
        c_ctx = Counter(sem("ctx_in"))
        c_k1 = Counter(sem("k1_in"))
        c_m = Counter(sem("max_rows"))
        c_init = Counter(sem("slots_init"))
        c_out = [Counter(sem(f"out_store{i}")) for i in range(2)]
        c_scat = [Counter(sem(f"dispatch{i}")) for i in range(2)]
        c_ew = [Counter(sem(f"expert_w{i}")) for i in range(NW)]
        c_er = [Counter(sem(f"expert_rows{i}")) for i in range(NX)]
        c_add = Counter(sem("combine"))

        m_id0 = pool.do(lambda e: e.memset(ident[:, :], 0.0))
        m_id = pool.do(lambda e: e.affine_select(out=ident[:, :], in_=ident[:, :], compare_op=ALU.not_equal,
                                                 fill=1.0, base=0, pattern=[[-1, P]], channel_multiplier=1),
                       after=[m_id0])
        m_idr = act.do(lambda e: e.copy(identr[:, :], ident[:, :]), after=[m_id])
        m_b0 = pool.do(lambda e: e.memset(before[:, :], 1.0))
        m_before = pool.do(lambda e: e.affine_select(out=before[:, :], in_=before[:, :], compare_op=ALU.is_ge,
                                                     fill=0.0, base=-1, pattern=[[1, P]],
                                                     channel_multiplier=-1), after=[m_b0])
        m_ones = pool.do(lambda e: e.memset(ones_bf[:, :], 1.0))
        m_mh = pool.do(lambda e: e.memset(minus_half[:, :], -0.5))
        m_tok0 = pool.do(lambda e: e.iota(token_no[:, :], [[0, 1]], base=0, channel_multiplier=1,
                                          allow_small_or_imprecise_dtypes=True))
        m_er0 = pool.do(lambda e: e.memset(empty_rows[:, :], 0.0))
        m_er = pool.do(lambda e: e.tensor_scalar(empty_rows[:, ROW - 1:ROW], token_no[:, :], float(T), None,
                                                 ALU.add), after=[m_er0, m_tok0])
        m_end = pool.do(lambda e: e.iota(expert_end[:, :], [[-CAP, NE]], base=SLOTS, channel_multiplier=0,
                                         allow_small_or_imprecise_dtypes=True))
        m_lr = pool.do(lambda e: e.memset(low_rows[:, :], 0.0), after=[m_end])
        for base in (0, ROWS):
            m_lr = pool.do(lambda e, b=base: e.memset(low_rows[b + 32:b + 64, :], -1.0), after=[m_lr])
            m_lr = pool.do(lambda e, b=base: e.affine_select(
                out=low_rows[b + 32:b + 64, :], in_=low_rows[b + 32:b + 64, :], compare_op=ALU.is_ge, fill=0.0,
                base=-16, pattern=[[0, 1]], channel_multiplier=1), after=[m_lr])
        m_or = pool.do(lambda e: e.memset(one_rows[:, :], 0.0), after=[m_lr])
        for base in (0, ROWS):
            m_or = pool.do(lambda e, b=base: e.memset(one_rows[b + 32:b + 64, :], 1.0), after=[m_or])
            m_or = pool.do(lambda e, b=base: e.affine_select(
                out=one_rows[b + 32:b + 64, :], in_=one_rows[b + 32:b + 64, :], compare_op=ALU.is_gt, fill=0.0,
                base=16, pattern=[[0, 1]], channel_multiplier=-1), after=[m_or])
        m_qz = []
        for t in q_tok.buffers:
            m_qz.append(dve.do(lambda e, t=t: e.memset(t[:, :, :].bitcast(F32), 0.0)))
        for t in q_st:
            m_qz.append(pool.do(lambda e, t=t: e.memset(t[:, :, :, :].bitcast(F32), 0.0), after=[m_or]))
        for t in v_x:
            m_qz.append(dve.do(lambda e, t=t: e.memset(t[:, :, :, HD:HD + 1], 1.0)))
        m_qz.append(dve.do(lambda e: e.memset(zb[:, :, :, L:], SENTINEL)))
        m_qz.append(dve.do(lambda e: e.memset(top3[:, :, :, KR:], SENTINEL)))
        m_ao = [dve.do(lambda e, t=t: e.memset(t[:, :], 0.0)) for t in attn_out]
        m_cnt0 = dve.do(lambda e: e.memset(seen_cnt[0][:, :], 0.0))

        m_init = sp.dma(lambda e: e.dma_start(slots_dram.rearrange("(e c) f -> c e f", c=CAP),
                                              empty_rows[:, :].unsqueeze(1).broadcast_to([P, NE, ROW])),
                        c_init, after=[m_er])

        m_init = sp.dma(lambda e: e.dma_start(out_pad[T:T + CAP, :], empty_rows[:, 0:D]), c_init, after=[m_er])

        def bcast(v, n):
            return v.rearrange("(a d) -> a d", a=1).broadcast_to([P, n])

        for dst, src in ((bq[:, :], bcast(bq_in, D)), (bkv[:, :], bcast(bkv_in, 2 * D)), (bo[:, :], bcast(bo_in, D)),
                         (b2[:, :], b2_in), (pw[:, :], pw_in), (uT[:, :], uT_in), (rT[:, :, :], rT_in),
                         (wsgu[:, :, :], wsgu_in), (wsd[:, :, :], wsd_in)):
            m_w = sp.dma(lambda e, d=dst, s=src: e.dma_start(d, s), c_w)

        _, wk, free = work.take()
        for dt in range(DT):
            m = pe.do(lambda e, wk=wk, dt=dt: e.matmul(wk[:, dt * 64:dt * 64 + 3 * L], pw[:, dt * P:(dt + 1) * P],
                                                      uT[:, :], start=True, stop=True), after=[m_w])
        gsrc = wk[:, 0:DT * 64].rearrange("p (t n) -> p t n", t=DT)[:, :, 0:3 * L]
        m1 = act.do(lambda e: e.copy(gT[0][:, :, :], gsrc), after=[m])
        m_g = dve.do(lambda e: e.tensor_tensor(gT[1][:, :, :], gsrc, gT[0][:, :, :].bitcast(F32), ALU.subtract),
                     after=[m, m1])
        work.give(0, [m1, m_g])

        stage_free = [(), ()]
        n_st = 0

        def load_parts(dst, src, n):
            nonlocal n_st
            i = n_st % 2
            n_st += 1
            buf = stage[:, i, 0:n]
            m = sp.dma(lambda e: e.dma_start(buf, src), c_stage[i], reuse=stage_free[i])
            mh = act.do(lambda e: e.copy(dst[0], buf), after=[m])
            ml = dve.do(lambda e: e.tensor_tensor(dst[1], buf, dst[0].bitcast(F32), ALU.subtract), after=[m, mh])
            stage_free[i] = (mh, ml)
            return ml

        def flat(t):
            return t.rearrange("p a b -> p (a b)")

        m_wq = load_parts([flat(w[:, :, :]) for w in wq], flat(wq_in_ap := wqT_in), DT * D)
        m_wkv = load_parts([flat(w[:, :, :]) for w in wkv], flat(wkvT_in), DT * 2 * D)
        m_wo = load_parts([flat(w[:, :, :]) for w in wo], flat(woT_in), DT * D)
        m_wmix = []
        mix_jobs = []
        for n, src in ((0, w1T_in), (1, w2T_in)):
            for l in range(0, L, 2):
                mix_jobs.append((n, l, src))

        def load_mix():
            for n, l, src in mix_jobs:
                m = load_parts([w[:, l:l + 2, :, :].rearrange("p l a b -> p (l a b)") for w in wmix[n]],
                               src[:, l:l + 2, :, :].rearrange("p l a b -> p (l a b)"), 2 * DT * D)
                m_wmix.append(m)
            return dve.do(lambda e: e.memset(k1_raw, 1.0), reuse=[*stage_free[0], *stage_free[1]])

        def layer_norm(src, src_marks, dst, dst_free):
            im, mvb, fm = mv.take()
            iv, ve, fv = veps.take()
            ir, rs, fr = rstd.take()
            last = None
            for t in range(TILES):
                i, st, f = stats.take()
                m = dve.do(lambda e, st=st, t=t: e.bn_stats(st[:, :], src[:, t, :]), after=[src_marks[t]], ns=335)
                m = dve.do(lambda e, st=st, t=t: e.bn_aggr(mvb[:, t, :], st[:, :]), after=[m], reuse=fm, ns=75)
                stats.give(i, [m])
            m = dve.do(lambda e: e.tensor_scalar(ve[:, :], mvb[:, :, 1], EPS, None, ALU.add), after=[m], reuse=fv)
            m = pool.do(lambda e: e.tensor_tensor(rs[:, :], ve[:, :], minus_half[:, :], ALU.pow),
                        after=[m, m_mh], reuse=fr, ns=630)
            veps.give(iv, [m])
            out = []
            for t in range(TILES):
                out.append(dve.do(lambda e, t=t: e.tensor_scalar(dst[:, t, 0:D], src[:, t, :], mvb[:, t, 0:1],
                                                                rs[:, t:t + 1], ALU.subtract, ALU.mult),
                                  after=[m], reuse=dst_free, ns=323))
            mv.give(im, out)
            rstd.give(ir, out)
            return out

        def transposed(src, marks):
            i, wk, free = work.take()
            v = wk[:, :].rearrange("p (a b) -> p a b", a=DT)
            for t in range(TILES):
                for dt in range(DT):
                    m = pe.do(lambda e, t=t, dt=dt: e.transpose(v[:, dt, t * P:(t + 1) * P],
                                                                src[:, t, dt * P:(dt + 1) * P], ident[:, :]),
                              after=[marks[t], m_id], reuse=free, ns=171)
            return i, v, m

        def transposed_parts(src, marks):
            i, v, m = transposed(src, marks)
            ip, (hi, lo), free = parts.take()
            mh = act.do(lambda e: e.copy(hi[:, :, :], v[:, :, :]), after=[m], reuse=free)
            ml = dve.do(lambda e: e.tensor_tensor(lo[:, :, :], v[:, :, :], hi[:, :, :].bitcast(F32), ALU.subtract),
                        after=[m, mh], reuse=free, ns=602)
            work.give(i, [mh, ml])
            return ip, (hi, lo), ml, m

        TERMS = ((0, 0), (1, 0), (0, 1))

        def product3(out, left, right, after, reuse, ns=107):
            n = 0
            for a, b in TERMS:
                for dt in range(DT):
                    lhs, rhs = left(a, dt), right(b, dt)
                    m = pe.do(lambda e: e.matmul(out, lhs, rhs, start=(n == 0), stop=(n == 3 * DT - 1)),
                              after=after, reuse=reuse, ns=ns)
                    n += 1
            return m

        def stack_tokens(src, src_mark, ring, is_q):
            i, st, free = ring.take()
            v = src.rearrange("p (h r) -> p h r", h=H)
            blocks = st[:, :, :].rearrange("p h (a r) -> p h a r", r=HD)
            high = blocks[:, :, 0:4:3, :] if is_q else blocks[:, :, 0:2, :]
            m1 = act.do(lambda e: e.copy(high, v.unsqueeze(2).broadcast_to([P, H, 2, HD])),
                        after=[src_mark, *m_qz], reuse=free)
            m2 = dve.do(lambda e: e.tensor_tensor(blocks[:, :, 1 if is_q else 3, :], v,
                                                  blocks[:, :, 0, :].bitcast(F32), ALU.subtract),
                        after=[m1], reuse=free, ns=335)
            return i, st, [m1, m2], [m1, m2]

        def stack_to_rows(st, marks, t, dst, is_q, dst_free):
            v = st[:, :, :].rearrange("p (n k) r -> p n (k r)", k=2)
            done = []
            for half in range(2):
                i, wk, free = work.take()
                for n in range(4):
                    m = pe.do(lambda e, n=n, half=half, wk=wk: e.transpose(
                        wk[:, n * P:(n + 1) * P].bitcast(F32R), v[:, half * 4 + n, :], identr[:, :]),
                        after=[*marks, m_idr], reuse=free, ns=85)
                src = wk[:, :].rearrange("p (n t) -> p n t", n=4)
                pr = slice(half * 4, half * 4 + 4)
                tk = slice(t * P, (t + 1) * P)
                if is_q:
                    a = act.do(lambda e, src=src, pr=pr, tk=tk: e.copy(dst[0:ROWS, pr, 0, tk], src[0:ROWS]),
                               after=[m, *m_qz], reuse=dst_free)
                    b = act.do(lambda e, src=src, pr=pr, tk=tk: e.copy(dst[ROWS:P, pr, 1, tk], src[ROWS:P]),
                               after=[m], reuse=dst_free)
                    work.give(i, [a, b])
                    done += [a, b]
                else:
                    a = act.do(lambda e, src=src, pr=pr, tk=tk: e.activation(
                        dst[:, pr, tk], src, ACT.Identity, bias=one_rows[:, :]), after=[m, m_or], reuse=dst_free)
                    work.give(i, [a])
                    done.append(a)
            return done, m

        state = {"nm_free": (), "mmark": (), "kst_free": (), "qst_free": (), "vx_free": [(), ()],
                 "o_free": (), "acc_free": ()}

        def attention(qs, ks, vx, q_marks, k_marks, v_marks, dst, dst_free):
            red = []
            for p in range(PAIRS):
                for t in range(TILES):
                    i, wk, free = work.take()
                    for k in range(2):
                        m = pe.do(lambda e, wk=wk, p=p, t=t, k=k: e.matmul(
                            wk[:, k * S:(k + 1) * S], qs[:, p, k, t * P:(t + 1) * P], ks[:, p, :],
                            start=True, stop=True), after=[*q_marks, *k_marks], reuse=free, ns=130)
                    r = dve.do(lambda e, wk=wk, p=p, t=t: e.tensor_reduce(
                        nm[:, t, 2 * p:2 * p + 2], wk[:, :].rearrange("p (k s) -> p k s", k=2), AX_X, ALU.max,
                        negate=True), after=[m], reuse=state["nm_free"], ns=598)
                    work.give(i, [r])
                    yield ()
            v = nm[:, :, :].rearrange("p t (n k) -> p t k n", k=2)
            m1 = dve.do(lambda e: e.tensor_copy(nmp[:, :, 0, :, :], v), after=[r], reuse=state["mmark"])
            m2 = dve.do(lambda e: e.tensor_tensor(nmp[:, :, 1, :, :], v, nmp[:, :, 0, :, :].bitcast(F32),
                                                  ALU.subtract), after=[m1])
            state["nm_free"] = (m2,)
            i, wk, free = work.take()
            for t in range(TILES):
                m = pe.do(lambda e, t=t, wk=wk: e.transpose(
                    wk[0:4 * PAIRS, t * P:(t + 1) * P].bitcast(F32R),
                    nmp[:, t, :, :, :].rearrange("p a k n -> p (a k n)"), identr[:, :]),
                    after=[m1, m2], reuse=free)
            mc = act.do(lambda e, wk=wk: e.copy(mT[:, :], wk[0:4 * PAIRS, 0:S]), after=[m], reuse=state["mmark"])
            work.give(i, [mc])
            for part in range(2):
                for k in range(2):
                    r0 = (part * 2 + k) * PAIRS
                    mm = sp.dma(lambda e, part=part, k=k, r0=r0: e.dma_start(
                        qs[ROWS * k + 32 + part:ROWS * k + 33 + part, :, k, :].bitcast(F32),
                        mT[r0:r0 + PAIRS, :].bitcast(F32)), c_m,
                        after=[mc], reuse=[m, *q_marks])
            state["mmark"] = (mm,)
            yield [mm]
            pend = None

            def times_v(p, iE, Eb, marks):
                for s in range(TILES):
                    for k in range(2):
                        h = 2 * p + k
                        r0 = HB * (h % HQ)
                        m = pe.do(lambda e, k=k, h=h, s=s, r0=r0: e.matmul(
                            outT(h // HQ)[r0:r0 + HD + 1, :], vx[:, s, h, :], Eb[:, s, k, :],
                            start=(s == 0), stop=(s == TILES - 1)),
                            after=[*marks, *v_marks, *m_ao], reuse=attn_out_free[h // HQ // 2], ns=220)
                E.give(iE, [m])
                return m

            for p in range(PAIRS):
                iE, Eb, fE = E.take()
                marks = []
                for s in range(TILES):
                    i, sc, free = score.take()
                    m = pe.do(lambda e, sc=sc, p=p, s=s: e.matmul(
                        sc[:, :], ks[:, p, s * P:(s + 1) * P], qs[:, p, :, :].rearrange("p k t -> p (k t)"),
                        start=True, stop=True), after=[mm], reuse=free, ns=333)
                    a = act.do(lambda e, sc=sc, s=s, Eb=Eb: e.activation(
                        Eb[:, s, :, :].rearrange("p k t -> p (k t)"), sc[:, :], ACT.Exp, scale=0.25),
                        after=[m], reuse=fE)
                    score.give(i, [a])
                    marks.append(a)
                    if s == 0:
                        yield score.free[score.idle[0]]
                if pend:
                    yield pend[3]
                    times_v(*pend)
                pend = (p, iE, Eb, marks)
                yield [*score.free[score.idle[0]], *E.free[E.idle[0]]]
            qk_last = m
            yield pend[3]
            m = times_v(*pend)
            yield [m]
            iT, oT, fT = E.take()
            oT = oT.rearrange("p t k s -> p (t k) s")
            mc = []
            for i in range(2):
                mc.append(act.do(lambda e, i=i: e.copy(oT[:, 2 * i:2 * i + 2, :].rearrange("p g s -> p (g s)"),
                                                       attn_out[i][:, :]), after=[m], reuse=fT))
                attn_out_free[i] = (mc[-1],)
            yield mc
            out, last = [], []
            for t in range(TILES):
                i, wk, free = work.take()
                for g in range(H // HQ):
                    mt = pe.do(lambda e, g=g, t=t, wk=wk: e.transpose(wk[:, g * P:(g + 1) * P],
                                                                      oT[:, g, t * P:(t + 1) * P], ident[:, :]),
                               after=[mc[g // 2], m_id], reuse=free, ns=171)
                last.append(mt)
                ir, rs, fr = rsum.take()
                o = wk[:, :].rearrange("p (h r) -> p h r", h=H)
                r = dve.do(lambda e, o=o, rs=rs: e.reciprocal(rs[:, :], o[:, :, HD]), after=[mt], reuse=fr)
                w = dve.do(lambda e, o=o, rs=rs, t=t: e.tensor_tensor(
                    dst[:, t, :].rearrange("p (h r) -> p h r", h=H), o[:, :, 0:HD],
                    rs[:, :].unsqueeze(2).broadcast_to([P, H, HD]), ALU.mult), after=[r], reuse=dst_free)
                work.give(i, [r, w])
                rsum.give(ir, [w])
                out.append(w)
            E.give(iT, last)
            return out, qk_last, m

        emitted = {"A": -1, "B": -1, "C": -1}
        xs = {}

        def stage_a(b):
            ix, xb, fx = X.take()
            mx = sp.dma(lambda e: e.dma_start(xb[:, :, :], x_in[b].rearrange("(t p) d -> p t d", p=P)), c_x[ix],
                        reuse=fx)
            i, ct, fc = ctxTr.take()
            mc = sp.dma(lambda e: e.dma_start(ct[:, :, :], ctxT_in[b].rearrange("(a p) s -> p a s", p=P)), c_ctxT,
                        reuse=fc)
            ic, (ch, cl), fcp = parts.take()
            c1 = act.do(lambda e: e.copy(ch[:, :, :], ct[:, :, :]), after=[mc], reuse=fcp)
            c2 = pool.do(lambda e: e.tensor_tensor(cl[:, :, :], ct[:, :, :], ch[:, :, :].bitcast(F32), ALU.subtract),
                         after=[c1], reuse=fcp)
            ctxTr.give(i, [c2])
            if b >= 2:
                prefetch_v(b - 2)
            yield [c2]
            k_marks, v_marks = [], []
            for t in range(TILES):
                i, wk, free = work.take()
                tk = slice(t * P, (t + 1) * P)
                m = product3(wk[:, :], lambda a, dt, tk=tk: (ch, cl)[a][:, dt, tk], lambda a, dt: wkv[a][:, dt, :],
                             after=[c1, c2, m_wkv], reuse=free, ns=213)
                ikf, kf, fk = tok_f.take()
                mk = dve.do(lambda e, wk=wk, kf=kf: e.tensor_tensor(kf[:, :], wk[:, 0:D], bkv[:, 0:D], ALU.add),
                            after=[m, m_w], reuse=fk)
                mvv = dve.do(lambda e, wk=wk, t=t: e.tensor_tensor(
                    v_x[0][:, t, :, 0:HD], wk[:, D:2 * D].rearrange("p (h r) -> p h r", h=H),
                    bkv[:, D:2 * D].rearrange("p (h r) -> p h r", h=H), ALU.add),
                    after=[m, *m_qz], reuse=state["vx_free"][0])
                work.give(i, [mk, mvv])
                v_marks.append(mvv)
                ik, st, ms, rd = stack_tokens(kf[:, :], mk, q_tok, False)
                tok_f.give(ikf, rd)
                yield ms
                d, rdm = stack_to_rows(st, ms, t, k_st, False, state["kst_free"])
                q_tok.give(ik, [rdm])
                k_marks += d
            parts.give(ic, [m])
            ih, xh, fh = xhat.take()
            mh = layer_norm(xb, [mx, mx], xh, fh)
            yield mh
            ip, (hi, lo), mp, rdm = transposed_parts(xh, mh)
            xhat.give(ih, [rdm])
            yield [mp]
            q_marks = []
            for t in range(TILES):
                i, wk, free = work.take()
                tk = slice(t * P, (t + 1) * P)
                m = product3(wk[:, 0:D], lambda a, dt, tk=tk: (hi, lo)[a][:, dt, tk], lambda a, dt: wq[a][:, dt, :],
                             after=[mp, m_wq], reuse=free)
                iqf, qf, fq = tok_f.take()
                mq = dve.do(lambda e, wk=wk, qf=qf: e.tensor_tensor(qf[:, :], wk[:, 0:D], bq[:, :], ALU.add),
                            after=[m, m_w], reuse=fq)
                work.give(i, [mq])
                iq, st, ms, rd = stack_tokens(qf[:, :], mq, q_tok, True)
                tok_f.give(iqf, rd)
                yield ms
                d, rdm = stack_to_rows(st, ms, t, q_st[0], True, state["qst_free"])
                q_tok.give(iq, [rdm])
                q_marks += d
            parts.give(ip, [m])
            yield q_marks
            out, qk_last, av_last = yield from attention(q_st[0], k_st, v_x[0], q_marks, k_marks, v_marks, ctx_o,
                                                         state["o_free"])
            state["kst_free"] = state["qst_free"] = (qk_last,)
            state["vx_free"][0] = (av_last,)
            mb = pool.do(lambda e: e.tensor_tensor(xb[:, :, :], xb[:, :, :],
                                                   bo[:, :].unsqueeze(1).broadcast_to([P, TILES, D]), ALU.add),
                         after=[mx, m_w], reuse=mh)
            yield out
            ip, (hi, lo), mp, rdm = transposed_parts(ctx_o, out)
            state["o_free"] = (rdm,)
            yield [mp]
            marks = []
            for t in range(TILES):
                i, wk, free = work.take()
                tk = slice(t * P, (t + 1) * P)
                m = product3(wk[:, 0:D], lambda a, dt, tk=tk: (hi, lo)[a][:, dt, tk], lambda a, dt: wo[a][:, dt, :],
                             after=[mp, m_wo], reuse=free)
                r = dve.do(lambda e, wk=wk, t=t: e.tensor_tensor(xb[:, t, :], xb[:, t, :], wk[:, 0:D], ALU.add),
                           after=[m, mb])
                work.give(i, [r])
                marks.append(r)
            parts.give(ip, [m])
            xs[b] = (ix, xb, marks)
            emitted["A"] = b
            yield ()

        bstate = {"acc": (), "C": (), "c3": (), "route": ()}

        def mixture(n, hi, lo, mp, mC, first):
            out = [None, None]
            for t in range(TILES):
                tk = slice(t * P, (t + 1) * P)
                prev = first[t]
                for l in range(0, L, 2):
                    i, wk, free = work.take()
                    m = product3(wk[:, :].rearrange("p (l d) -> p l d", l=2),
                                 lambda a, dt, tk=tk: (hi, lo)[a][:, dt, tk],
                                 lambda a, dt, l=l: wmix[n][a][:, l:l + 2, dt, :],
                                 after=[mp, m_wmix[n * (L // 2) + l // 2]], reuse=free, ns=213)
                    for k in range(2):
                        c = C[:, t, n, l + k:l + k + 1]
                        src = wk[:, k * D:(k + 1) * D]
                        if prev is None:
                            prev = dve.do(lambda e, src=src, c=c, t=t: e.tensor_scalar(
                                acc[:, t, :], src, c, None, ALU.mult), after=[m, mC], reuse=bstate["acc"], ns=396)
                        else:
                            prev = dve.do(lambda e, src=src, c=c, t=t: e.scalar_tensor_tensor(
                                acc[:, t, :], src, c, acc[:, t, :], ALU.mult, ALU.add), after=[m, mC, prev], ns=396)
                    work.give(i, [prev])
                    yield ()
                out[t] = prev
            return out, m

        def stage_b(b):
            ix, xb, mx = xs[b]
            ih, xh, fh = xhat.take()
            mh = layer_norm(xb, mx, xh, fh)
            yield mh
            ip, (hi, lo), mp, rdm = transposed_parts(xh, mh)
            xhat.give(ih, [rdm])
            yield [mp]
            i, wk, free = work.take()
            for t in range(TILES):
                tk = slice(t * P, (t + 1) * P)
                m = product3(wk[:, t * 64:t * 64 + 3 * L], lambda a, dt, tk=tk: (hi, lo)[a][:, dt, tk],
                             lambda a, dt: gT[a][:, dt, :], after=[mp, m_g], reuse=free)
            zsrc = wk[:, 0:TILES * 64].rearrange("p (t n) -> p t n", t=TILES)[:, :, 0:3 * L].rearrange(
                "p t (s l) -> p t s l", s=3)
            mz = dve.do(lambda e: e.tensor_copy(zb[:, :, :, 0:L], zsrc), after=[m, *m_qz],
                        reuse=bstate["route"])
            work.give(i, [mz])
            yield [mz]
            for t in range(TILES):
                for s in range(3):
                    mt = dve.do(lambda e, t=t, s=s: e.max(top[:, t, s, :], zb[:, t, s, 0:L]), after=[mz])
            m3 = dve.do(lambda e: e.tensor_copy(top3[:, :, :, 0:KR], top[:, :, :, 0:KR]), after=[mt])
            for t in range(TILES):
                for s in range(3):
                    mr = dve.do(lambda e, t=t, s=s: e.match_replace(
                        out=zr[:, t, s, :], in_to_replace=top3[:, t, s, :], in_values=zb[:, t, s, :],
                        imm_value=TAKEN), after=[m3, mz])
            mk = dve.do(lambda e: e.tensor_tensor(zmask[:, :, :, :], zr[:, :, :, 0:L], zb[:, :, :, 0:L],
                                                  ALU.not_equal), after=[mr])
            md = dve.do(lambda e: e.tensor_tensor(zexp[:, :, :, :], zb[:, :, :, 0:L],
                                                  top[:, :, :, 0:1].broadcast_to([P, TILES, 3, L]),
                                                  ALU.subtract), after=[mt])
            me = act.do(lambda e: e.activation(zexp[:, :, :, :], zexp[:, :, :, :], ACT.Exp), after=[md])
            yield [me]
            m = dve.do(lambda e: e.tensor_tensor(zexp[:, :, :, :], zexp[:, :, :, :], zmask[:, :, :, :], ALU.mult),
                       after=[me, mk])
            m2 = dve.do(lambda e: e.tensor_reduce(zsum[:, :, :], zexp[:, :, :, :], AX_X, ALU.add), after=[m])
            m2 = dve.do(lambda e: e.reciprocal(zsum[:, :, :], zsum[:, :, :]), after=[m2])
            mC = dve.do(lambda e: e.tensor_tensor(C[:, :, :, :], zexp[:, :, :, :],
                                                  zsum[:, :, :].unsqueeze(3).broadcast_to([P, TILES, 3, L]),
                                                  ALU.mult), after=[m2], reuse=bstate["C"])
            bstate["route"] = (mC,)
            yield [mC]
            out, ml = yield from mixture(0, hi, lo, mp, mC, [None, None])
            parts.give(ip, [ml])
            ih, hb, fh = xhat.take()
            mg = act.do(lambda e: e.activation(hb[:, :, :], acc[:, :, :], ACT.Gelu), after=out, reuse=fh)
            i, wk, free = work.take()
            for t in range(TILES):
                m = pe.do(lambda e, t=t: e.transpose(wk[0:L, t * P:(t + 1) * P], C[:, t, 2, :], ident[:, :]),
                          after=[mC], reuse=free)
            mc = act.do(lambda e: e.copy(c3T[:, :], wk[0:L, 0:S]), after=[m], reuse=bstate["c3"])
            work.give(i, [mc])
            i, wk, free = work.take()
            for t in range(TILES):
                m = pe.do(lambda e, t=t: e.matmul(wk[:, t * D:(t + 1) * D], c3T[:, t * P:(t + 1) * P], b2[:, :],
                                                  start=True, stop=True), after=[mc, m_w], reuse=free)
            bstate["c3"] = (m,)
            first = []
            for t in range(TILES):
                first.append(dve.do(lambda e, t=t: e.tensor_tensor(acc[:, t, :], xb[:, t, :],
                                                                   wk[:, t * D:(t + 1) * D], ALU.add),
                                    after=[m, mg, mx[t]]))
            work.give(i, first)
            yield [mg]
            ip, (hi, lo), mp, rdm = transposed_parts(hb, [mg, mg])
            xhat.give(ih, [rdm])
            yield [mp]
            out, ml = yield from mixture(1, hi, lo, mp, mC, first)
            parts.give(ip, [ml])
            bstate["C"] = (m, *out)
            mo = pool.do(lambda e: e.tensor_copy(xb[:, :, :], acc[:, :, :]), after=out, reuse=[*first, *mh])
            bstate["acc"] = (mo,)
            xs[b] = (ix, xb, [mo, mo])
            emitted["B"] = b
            yield ()

        cstate = {"k1": (), "ctx": (), "kst": ()}
        pre = {}

        def prefetch_c(b):
            src = ctxT_in[b].rearrange("(n k r) s -> k r n s", k=2, r=HD)
            for k in range(2):
                for r0 in (0, 16, 48):
                    m = sp.dma(lambda e, k=k, r0=r0: e.dma_start(k1_raw[ROWS * k + r0:ROWS * k + r0 + 16, :, :],
                                                                 src[k]), c_k1, after=[m_k1one],
                               reuse=cstate["k1"])
            pre[b] = [m]

        def prefetch_v(b):
            mt = sp.dma(lambda e: e.dma_start(ctx_tok[:, :, :], ctx_in[b].rearrange("(t p) d -> p t d", p=P)),
                        c_ctx, reuse=ctxTr.free[0])
            pre[b].append(mt)

        def stage_c(b):
            ix, xb, mx = xs[b]
            if b + 2 >= NB:
                prefetch_v(b)
            mk, mt = pre[b]
            mv_ = pool.do(lambda e: e.tensor_copy(v_x[1][:, :, :, 0:HD],
                                                  ctx_tok[:, :, :].rearrange("p t (h r) -> p t h r", h=H)),
                          after=[mt, *m_qz], reuse=state["vx_free"][1])
            ctxTr.free[0] = (mv_,)
            m1 = act.do(lambda e: e.copy(k_st[:, :, :], k1_raw), after=[mk], reuse=state["kst_free"], ns=2000)
            m2 = dve.do(lambda e: e.scalar_tensor_tensor(k_st[:, :, :], k_st[:, :, :].bitcast(F32), low_rows[:, :],
                                                         k1_raw, ALU.mult, ALU.add), after=[m1, m_lr], ns=2263)
            cstate["k1"] = (m2,)
            ih, xh, fh = xhat.take()
            mh = layer_norm(xb, mx, xh, fh)
            q_marks = []
            rds = []
            for t in range(TILES):
                iq, st, ms, rd = stack_tokens(xh[:, t, :], mh[t], q_tok, True)
                rds += rd
                yield ms
                d, rdm = stack_to_rows(st, ms, t, q_st[0], True, state["qst_free"])
                q_tok.give(iq, [rdm])
                q_marks += d
            xhat.give(ih, rds)
            yield q_marks
            out, qk_last, av_last = yield from attention(q_st[0], k_st, v_x[1], q_marks, [m2], [mv_], ctx_o,
                                                         state["o_free"])
            state["kst_free"] = state["qst_free"] = (qk_last,)
            state["vx_free"][1] = (av_last,)
            mo = pool.do(lambda e: e.tensor_tensor(xb[:, :, :], xb[:, :, :], ctx_o[:, :, :], ALU.add),
                         after=out, reuse=mh)
            state["o_free"] = (mo,)
            xs[b] = (ix, xb, [mo, mo])
            emitted["C"] = b
            yield ()

        dstate = {"xdT": (), "sT": (), "cnt": m_cnt0, "out": [], "route": ()}

        def stage_d(b):
            ix, xb, mx = xs[b]
            ir, rw, fr = row.take()
            mh = layer_norm(xb, mx, rw, fr)
            yield mh
            i, v, m = transposed(rw, mh)
            mT_ = act.do(lambda e: e.copy(xdT[:, :, :], v[:, :, :]), after=[m], reuse=dstate["xdT"])
            work.give(i, [mT_])
            yield [mT_]
            i, wk, free = work.take()
            for t in range(TILES):
                for dt in range(DT):
                    m = pe.do(lambda e, t=t, dt=dt: e.matmul(wk[:, t * NE:(t + 1) * NE],
                                                             xdT[:, dt, t * P:(t + 1) * P], rT[:, dt, :],
                                                             start=(dt == 0), stop=(dt == DT - 1)),
                              after=[mT_, m_w], reuse=free)
            lg = wk[:, 0:TILES * NE].rearrange("p (t n) -> p t n", t=TILES)
            ma = dve.do(lambda e: e.tensor_reduce(lmax[:, :], lg, AX_X, ALU.max), after=[m], reuse=dstate["route"])
            ms = dve.do(lambda e: e.tensor_tensor(prob[:, :, :], lg,
                                                  lmax[:, :].unsqueeze(2).broadcast_to([P, TILES, NE]),
                                                  ALU.subtract), after=[ma])
            work.give(i, [ms])
            me = act.do(lambda e: e.activation(prob[:, :, :], prob[:, :, :], ACT.Exp), after=[ms])
            yield [me]
            m = dve.do(lambda e: e.tensor_reduce(psum_[:, :], prob[:, :, :], AX_X, ALU.add), after=[me])
            m = dve.do(lambda e: e.reciprocal(psum_[:, :], psum_[:, :]), after=[m])
            mp = dve.do(lambda e: e.tensor_tensor(prob[:, :, :], prob[:, :, :],
                                                  psum_[:, :].unsqueeze(2).broadcast_to([P, TILES, NE]), ALU.mult),
                        after=[m])
            for t in range(TILES):
                mt = dve.do(lambda e, t=t: e.max(ptop[:, t, :], prob[:, t, :]), after=[mp])
            for t in range(TILES):
                mr = dve.do(lambda e, t=t: e.match_replace(out=prep[:, t, :], in_to_replace=ptop[:, t, :],
                                                           in_values=prob[:, t, :], imm_value=-1.0), after=[mt])
            mk = dve.do(lambda e: e.tensor_scalar(pmask[:, :, :], prep[:, :, :], 0.0, None, ALU.is_lt), after=[mr])
            mkb = pool.do(lambda e: e.tensor_copy(pmask_bf[:, :, :], pmask[:, :, :]), after=[mk])
            m = dve.do(lambda e: e.tensor_reduce(tsum[:, :], ptop[:, :, :], AX_X, ALU.add), after=[mt])
            m = dve.do(lambda e: e.reciprocal(tsum[:, :], tsum[:, :]), after=[m])
            m = dve.do(lambda e: e.tensor_tensor(prob[:, :, :], prob[:, :, :],
                                                 tsum[:, :].unsqueeze(2).broadcast_to([P, TILES, NE]), ALU.mult),
                       after=[m])
            mw = dve.do(lambda e: e.tensor_tensor(rw[:, :, D:D + NE], prob[:, :, :], pmask[:, :, :], ALU.mult),
                        after=[m, mk], reuse=fr)
            yield [mkb]
            for t in range(TILES):
                mn = dve.do(lambda e, t=t: e.tensor_scalar(rw[:, t, ROW - 1:ROW], token_no[:, :],
                                                           float(b * S + t * P), None, ALU.add),
                            after=[m_tok0], reuse=fr)
            i, wk, free = work.take()
            for t in range(TILES):
                m = pe.do(lambda e, t=t: e.matmul(wk[:, t * NE:(t + 1) * NE], before[:, :], pmask_bf[:, t, :],
                                                  start=True, stop=(t == 0)), after=[mkb, m_before], reuse=free)
                if t:
                    m = pe.do(lambda e: e.matmul(wk[:, NE:2 * NE], ones_bf[:, :], pmask_bf[:, 0, :],
                                                 start=False, stop=True), after=[m_ones])
            for t in range(TILES):
                m = pe.do(lambda e, t=t: e.matmul(wk[:, 2 * NE:3 * NE], ones_bf[:, :], pmask_bf[:, t, :],
                                                  start=(t == 0), stop=(t == 1)))
            old, new = seen_cnt[b % 2], seen_cnt[(b + 1) % 2]
            m1 = dve.do(lambda e: e.tensor_tensor(pos[:, :, :], wk[:, 0:2 * NE].rearrange("p (t n) -> p t n", t=TILES),
                                                  old[:, :].unsqueeze(1).broadcast_to([P, TILES, NE]), ALU.add),
                        after=[m, dstate["cnt"]])
            dstate["cnt"] = dve.do(lambda e: e.tensor_tensor(new[:, :], wk[:, 2 * NE:3 * NE], old[:, :], ALU.add),
                                   after=[m, m1])
            work.give(i, [m1, dstate["cnt"]])
            yield ()
            m2 = dve.do(lambda e: e.scalar_tensor_tensor(pmask[:, :, :], pos[:, :, :], float(CAP), pmask[:, :, :],
                                                         ALU.is_lt, ALU.mult), after=[m1, mkb, mw])
            m3 = dve.do(lambda e: e.tensor_tensor(sval[:, :, :], expert_end[:, :].unsqueeze(1).broadcast_to(
                [P, TILES, NE]), pos[:, :, :], ALU.subtract), after=[m1, m_end])
            m3 = dve.do(lambda e: e.tensor_tensor(sval[:, :, :], sval[:, :, :], pmask[:, :, :], ALU.mult),
                        after=[m2, m3])
            for t in range(TILES):
                m4 = dve.do(lambda e, t=t: e.max(stop8[:, t, :], sval[:, t, :]), after=[m3])
            isx, six, fs = sidx.take()
            m5 = dve.do(lambda e: e.tensor_scalar(six[:, :, :], stop8[:, :, :], -1.0, float(SLOTS), ALU.mult,
                                                  ALU.add), after=[m4], reuse=fs)
            dstate["route"] = (m5,)
            yield [m5]
            for t in range(TILES):
                for k in range(8):
                    msc = pool.dma(lambda e, t=t, k=k: e.indirect_dma_start(
                        out=slots_dram, out_offset=bass.IndirectOffsetOnAxis(ap=six[:, t, k:k + 1], axis=0),
                        in_=rw[:, t, :], in_offset=None, bounds_check=SLOTS - 1, oob_is_err=False),
                        c_scat[ir], after=[m5, mn, mw, *mh, m_init])
                    if k % 2:
                        yield (pool.sem, pool.count),
            row.give(ir, [msc])
            sidx.give(isx, [msc])
            banks = []
            for half in range(2):
                i, wk, free = work.take()
                for f in range(2):
                    c0 = half * FH + f * FC
                    for dt in range(DT):
                        m = pe.do(lambda e, wk=wk, f=f, dt=dt, c0=c0: e.matmul(
                            wk[0:FC, f * S:(f + 1) * S], wsgu[:, dt, c0:c0 + FC], xdT[:, dt, :],
                            start=(dt == 0), stop=(dt == DT - 1)), after=[mT_, m_w], reuse=free, ns=253)
                banks.append((i, wk, m))
                yield ()
            dstate["xdT"] = (m,)
            (ig, gk, mg), (iu, uk, mu) = banks
            gv = gk[0:FC, :].rearrange("p (f s) -> p f s", f=2)
            uv = uk[0:FC, :].rearrange("p (f s) -> p f s", f=2)
            ma = act.do(lambda e: e.activation(sT_a[:, :, :], gv, ACT.Tanh, scale=0.5), after=[mg],
                        reuse=dstate["sT"])
            mb = dve.do(lambda e: e.scalar_tensor_tensor(sT_a[:, :, :], sT_a[:, :, :], 1.0, gv, ALU.add, ALU.mult),
                        after=[ma, mg], ns=600)
            mc = dve.do(lambda e: e.scalar_tensor_tensor(sT_a[:, :, :], sT_a[:, :, :], 0.5, uv, ALU.mult, ALU.mult),
                        after=[mb, mu], ns=600)
            work.give(ig, [ma, mb])
            work.give(iu, [mc])
            yield [mc]
            i, wk, free = work.take()
            for t in range(TILES):
                for f in range(2):
                    m = pe.do(lambda e, t=t, f=f: e.matmul(wk[:, t * D:(t + 1) * D], sT_a[:, f, t * P:(t + 1) * P],
                                                           wsd[:, f, :], start=(f == 0), stop=(f == 1)),
                              after=[mc, m_w], reuse=free)
            dstate["sT"] = (m,)
            mo = dve.do(lambda e: e.tensor_tensor(xb[:, :, :], xb[:, :, :], wk[:, :].rearrange(
                "p (t d) -> p t d", t=TILES), ALU.add), after=[m, *mh])
            work.give(i, [mo])
            mst = sp.dma(lambda e: e.dma_start(out_pad[b * S:(b + 1) * S, :].rearrange("(t p) d -> p t d", p=P),
                                               xb[:, :, :]), c_out[b % 2], after=[mo])
            X.give(ix, [mst])
            dstate["out"].append(mst)
            dstate["scat"] = dstate.get("scat", []) + [msc]
            yield ()

        def load_expert(n):
            i = n % NW
            sp.dma(lambda e: e.dma_start(ewg[i][:, :, :], wg_in[n].rearrange("(a p) f -> p a f", p=P)), c_ew[i],
                   reuse=ew_free[i])
            sp.dma(lambda e: e.dma_start(ewu[i][:, :, :], wu_in[n].rearrange("(a p) f -> p a f", p=P)), c_ew[i])
            return sp.dma(lambda e: e.dma_start(ewd[i][:, :, :], wd_in[n].rearrange("(a p) d -> p a d", p=FC)),
                          c_ew[i])

        def together(*streams):
            ready = [0] * len(streams)
            alive = list(range(len(streams)))
            blocked = set()
            while alive:
                n = min((j for j in alive if j not in blocked), key=lambda j: max(ready[j], pe.clock))
                try:
                    y = next(streams[n])
                    if y is BLOCKED:
                        blocked.add(n)
                    else:
                        ready[n] = plan.after(y)
                        blocked.clear()
                except StopIteration:
                    alive.remove(n)
                    blocked.clear()

        m_k1one = None

        def attentions():
            nonlocal m_k1one
            for b in range(NB + 2):
                if b < NB:
                    while not X.idle:
                        yield BLOCKED
                    yield from stage_a(b)
                    if b == 0:
                        m_k1one = load_mix()
                if b >= 2:
                    while emitted["B"] < b - 2:
                        yield BLOCKED
                    yield from stage_c(b - 2)
                    if b - 1 < NB:
                        prefetch_c(b - 1)
                elif b == 1:
                    prefetch_c(0)

        def mixtures():
            for b in range(NB):
                while emitted["A"] < b:
                    yield BLOCKED
                yield from stage_b(b)

        def dispatches():
            for b in range(NB):
                while emitted["C"] < b:
                    yield BLOCKED
                yield from stage_d(b)

        together(attentions(), dispatches(), mixtures())

        ew_marks = {}
        quiet = [(q.sem, q.count) for q in (pe, dve, act, pool)]
        ew_free = [tuple(quiet)] * NW
        for n in range(NW):
            ew_marks[n] = load_expert(n)


        gathered = [*dstate["out"][-2:], *dstate["scat"][-2:]]
        last_add = None
        tail_marks = [m for m in (dve.sem, act.sem, pe.sem, pool.sem)]
        quiet = [(q.sem, q.count) for q in (pe, dve, act, pool)]
        er_free = [tuple(quiet)] * NX
        ey_free = [tuple(quiet)] * 3
        exT_free = [tuple(quiet)] * 4
        id_free = [tuple(quiet)] * NX

        def load_rows(n):
            i = n % NX
            return sp.dma(lambda e: e.dma_start(erow[i], slots_dram[n * CAP:(n + 1) * CAP, :]), c_er[i],
                          after=gathered, reuse=er_free[i])

        er_marks = {n: load_rows(n) for n in range(1)}
        hid_free = [tuple(quiet)] * 2
        for n in range(NE):
            if n + 1 < NE:
                er_marks[n + 1] = load_rows(n + 1)
            rwt, mr = erow[n % NX], er_marks[n]
            mi = dve.do(lambda e, n=n, rwt=rwt: e.tensor_copy(eid[n % NX], rwt[:, ROW - 1:ROW]), after=[mr],
                        reuse=id_free[n % NX])
            i, wk, free = work.take()
            for dt in range(DT):
                m = pe.do(lambda e, dt=dt, wk=wk, rwt=rwt: e.transpose(wk[:, dt * P:(dt + 1) * P],
                                                                      rwt[:, dt * P:(dt + 1) * P], ident[:, :]),
                          after=[mr], reuse=free)
            xT = exT[n % 4].rearrange("p (a t) -> p a t", a=DT)
            mt = act.do(lambda e, wk=wk, xT=xT: e.copy(xT, wk[:, 0:D].rearrange("p (a t) -> p a t", a=DT)),
                        after=[m], reuse=exT_free[n % 4])
            work.give(i, [mt])
            i, wk, free = work.take()
            w = n % NW
            for j, (wt, f) in enumerate(((ewg[w], 0), (ewg[w], 1), (ewu[w], 0), (ewu[w], 1))):
                for dt in range(DT):
                    m = pe.do(lambda e, wk=wk, j=j, wt=wt, f=f, dt=dt, xT=xT: e.matmul(
                        wk[0:FC, j * P:(j + 1) * P], wt[:, dt, f * FC:(f + 1) * FC], xT[:, dt, :],
                        start=(dt == 0), stop=(dt == DT - 1)), after=[mt, ew_marks[n]], reuse=free)
            exT_free[n % 4] = (m,)
            gv = wk[0:FC, 0:2 * P].rearrange("p (f s) -> p f s", f=2)
            uv = wk[0:FC, 2 * P:4 * P].rearrange("p (f s) -> p f s", f=2)
            act_h = sT_a[:, :, (n % 2) * P:(n % 2 + 1) * P]
            mul_h = sT_a[:, :, (n % 2) * P:(n % 2 + 1) * P]
            ma = act.do(lambda e, gv=gv, h=act_h: e.activation(h, gv, ACT.Silu), after=[m],
                        reuse=hid_free[n % 2])
            mb = dve.do(lambda e, uv=uv, h=act_h, o=mul_h: e.tensor_tensor(o, h, uv, ALU.mult), after=[ma, m],
                        reuse=hid_free[n % 2])
            work.give(i, [ma, mb])
            i, wk, free = work.take()
            for f in range(2):
                m = pe.do(lambda e, wk=wk, f=f, o=mul_h, w=w: e.matmul(wk[:, 0:D], o[:, f, :], ewd[w][:, f, :],
                                                                    start=(f == 0), stop=(f == 1)),
                          after=[mb], reuse=free)
            ew_free[w] = (m,)
            hid_free[n % 2] = (m, mb)
            if n + NW < NE:
                ew_marks[n + NW] = load_expert(n + NW)
            y = ey[n % 3]
            my = dve.do(lambda e, wk=wk, n=n, rwt=rwt, y=y: e.tensor_scalar(y, wk[:, 0:D], rwt[:, D + n:D + n + 1],
                                                                          None, ALU.mult), after=[m],
                        reuse=ey_free[n % 3])
            work.give(i, [my])
            er_free[n % NX] = (my, mi, mt)
            last_add = pool.dma(lambda e, n=n, y=y: e.indirect_dma_start(
                out=out_pad, out_offset=bass.IndirectOffsetOnAxis(ap=eid[n % NX], axis=0), in_=y, in_offset=None,
                bounds_check=T + CAP - 1, oob_is_err=True, compute_op=ALU.add), c_add, after=[my, mi] + (
                    [last_add] if last_add else gathered))
            ey_free[n % 3] = (last_add,)
            id_free[n % NX] = (last_add,)
        pool.wait([last_add])
        sp.wait([last_add, m_init])



def kernel(**inputs):
    import concourse.bacc as bacc
    from concourse.bass_utils import run_bass_kernel_spmd

    a = {k: np.asarray(v) for k, v in inputs.items()}

    def split_rows(w):
        return np.ascontiguousarray(w.reshape(-1, P, w.shape[1]).transpose(1, 0, 2))

    def mixture_rows(w):
        n, o, i = w.shape
        return np.ascontiguousarray(w.transpose(0, 2, 1).reshape(n, i // P, P, o).transpose(2, 0, 1, 3))

    fc = a["L1_ffn_ws_down"].shape[0] // 2
    arrays = {
        "x": a["x"],
        "ctx": a["ctx_1024"],
        "ctxT": np.ascontiguousarray(a["ctx_1024"].transpose(0, 2, 1)),
        "wqT": split_rows(a["L0_xattn_Wq"].T),
        "wkvT": split_rows(np.concatenate([a["L0_xattn_Wk"].T, a["L0_xattn_Wv"].T], 1)),
        "woT": split_rows(a["L0_xattn_Wo"].T),
        "bq": a["L0_xattn_bq"],
        "bkv": np.concatenate([a["L0_xattn_bk"], a["L0_xattn_bv"]]),
        "bo": a["L0_xattn_bo"],
        "pw": a["L0_ffn_P_w"],
        "uT": np.ascontiguousarray(np.concatenate([a["L0_ffn_U1"], a["L0_ffn_U2"], a["L0_ffn_U3"]]).T),
        "w1T": mixture_rows(a["L0_ffn_W1"]),
        "w2T": mixture_rows(a["L0_ffn_W2"]),
        "b2": a["L0_ffn_b2"],
        "rT": split_rows(a["L1_ffn_router_w"].T),
        "wg": a["L1_ffn_w_gate"],
        "wu": a["L1_ffn_w_up"],
        "wd": a["L1_ffn_w_down"],
        "wsgu": split_rows(a["L1_ffn_ws_gate_up"]),
        "wsd": np.ascontiguousarray(a["L1_ffn_ws_down"].reshape(2, fc, -1).transpose(1, 0, 2)),
    }
    nc = bacc.Bacc("TRN2", target_bir_lowering=False, num_devices=1, dynamic_dma_scratch_size=4096)
    args = [nc.dram_tensor("in_" + n, v.shape, mybir.dt.from_np(v.dtype), kind="ExternalInput").ap()
            for n, v in arrays.items()]
    nb, s, d = a["x"].shape
    out = nc.dram_tensor("out", (nb * s + P, d), F32, kind="ExternalOutput").ap()
    build(nc, *args, out)
    r = run_bass_kernel_spmd(nc, [{"in_" + n: v for n, v in arrays.items()}], core_ids=[0])
    return r.results[0]["out"][:nb * s].reshape(nb, s, d)
```

```python
from contextlib import ExitStack

import numpy as np

import concourse.bass as bass
from concourse import mybir

F32 = mybir.dt.float32
F32R = mybir.dt.float32r
BF16 = mybir.dt.bfloat16
U32 = mybir.dt.uint32
ALU = mybir.AluOpType
ACT = mybir.ActivationFunctionType
AX_X = mybir.AxisListType.X

P = 128
EPS = 1e-5
SENTINEL = -1.0e30
BLOCKED = "blocked"
TAKEN = -3.0e30


DMA_NS = 2500
LATE_NS = 0
HANDOVER_NS = 100


class Plan:

    def __init__(self):
        self.end = {}

    def after(self, marks):
        return max([self.end[(sem.name, value)] for sem, value in marks], default=0)


class Engine:

    def __init__(self, engine, sem, plan, usual_ns):
        self.engine, self.sem, self.count, self.seen = engine, sem, 0, {}
        self.plan, self.usual_ns, self.clock = plan, usual_ns, 0

    def wait(self, marks):
        for sem, value in marks:
            if self.seen.get(sem.name, 0) < value:
                self.seen[sem.name] = value
                self.engine.wait_ge(sem, value)

    def do(self, fn, after=(), reuse=(), ns=None):
        self.wait(after)
        self.wait(reuse)
        self.count += 1
        fn(self.engine).then_inc(self.sem, 1)
        self.clock = max(self.clock, self.plan.after(after), self.plan.after(reuse)) + (ns or self.usual_ns)
        self.plan.end[(self.sem.name, self.count)] = self.clock + HANDOVER_NS
        return (self.sem, self.count)

    def dma(self, fn, counter, after=(), reuse=()):
        self.wait(after)
        self.wait(reuse)
        counter.count += 16
        fn(self.engine).then_inc(counter.sem, 16)
        start = max(self.clock, self.plan.after(after), self.plan.after(reuse))
        self.clock = start + self.usual_ns
        self.plan.end[(counter.sem.name, counter.count)] = start + DMA_NS
        return (counter.sem, counter.count)


class Counter:
    def __init__(self, sem):
        self.sem, self.count = sem, 0


class Ring:

    def __init__(self, buffers):
        self.buffers, self.free = buffers, [()] * len(buffers)
        self.idle = list(range(len(buffers)))

    def take(self):
        i = self.idle.pop(0)
        return i, self.buffers[i], self.free[i]

    def give(self, i, marks):
        assert i not in self.idle
        self.free[i] = tuple(marks)
        self.idle.append(i)


def build(nc, x_in, ctx_in, ctxT_in, wqT_in, wkvT_in, woT_in, bq_in, bkv_in, bo_in, pw_in, uT_in,
          w1T_in, w2T_in, b2_in, rT_in, wg_in, wu_in, wd_in, wsgu_in, wsd_in, out_pad):
    NB, S, D = x_in.shape
    T = NB * S
    TILES = S // P
    DT = D // P
    H, HD = 16, D // 16
    PAIRS = H // 2
    HP = PAIRS // 2
    ROWS = P // 2
    L = w1T_in.shape[1]
    KR = 3
    NE = rT_in.shape[2]
    CAP = 128
    FH = wg_in.shape[2]
    FC = FH // 2
    ROW = D + NE + 1
    SLOTS = NE * CAP

    slots_dram = nc.dram_tensor("expert_slots", (SLOTS, ROW), F32, kind="Internal").ap()

    ctx = ExitStack()
    with ctx:
        def sb(name, shape, dt=F32):
            return ctx.enter_context(nc.sbuf_tensor(name, list(shape), dt))

        def ps(name):
            return ctx.enter_context(nc.psum_tensor(name, [P, 512], F32))

        def sem(name):
            return ctx.enter_context(nc.semaphore(name))

        plan = Plan()
        pe = Engine(nc.tensor, sem("pe_done"), plan, 100)
        dve = Engine(nc.vector, sem("dve_done"), plan, 200)
        act = Engine(nc.scalar, sem("act_done"), plan, 480)
        pool = Engine(nc.gpsimd, sem("pool_done"), plan, 1200)
        sp = Engine(nc.sync, sem("sp_done"), plan, 60)

        identr = sb("identr", (P, P), F32R)
        before = sb("before", (P, P), BF16)
        ones_bf = sb("ones_bf", (P, P), BF16)
        minus_half = sb("minus_half", (P, 2))
        low_rows = sb("low_rows", (P, 1))
        one_rows = sb("one_rows", (P, 1))
        token_no = sb("token_no", (P, 1))
        expert_end = sb("expert_end", (P, NE))

        wq = [sb(f"wq_{p}", (P, DT, D), F32R) for p in "hl"]
        wkv = [sb(f"wkv_{p}", (P, DT, 2 * D), F32R) for p in "hl"]
        wo = [sb(f"wo_{p}", (P, DT, D), F32R) for p in "hl"]
        wmix = [[sb(f"w{n}_{p}", (P, L, DT, D), F32R) for p in "hl"] for n in (1, 2)]
        bq = sb("bq", (P, D))
        bkv = sb("bkv", (P, 2 * D))
        bo = sb("bo", (P, D))
        b2 = sb("b2", (L, D))
        pw = sb("pw", (64, D))
        uT = sb("uT", (64, 3 * L))
        gT = [sb(f"gT_{p}", (P, DT, 3 * L), F32R) for p in "hl"]
        rT = sb("rT", (P, DT, NE))
        wsgu = sb("wsgu", (P, DT, 2 * FH))
        wsd = sb("wsd", (FC, 2, D))

        X = Ring([sb(f"x{i}", (P, TILES, D)) for i in range(4)])
        xhat = Ring([sb(f"xhat{i}", (P, TILES, D)) for i in range(4)])
        parts = Ring([[sb(f"part{i}{p}", (P, DT, S), F32R) for p in "hl"] for i in range(3)])
        ctxTr = Ring([sb(f"ctxT{i}", (P, DT, S)) for i in range(1)])
        stack = Ring([sb(f"stack{i}", (P, H // 2, ROWS), F32R) for i in range(2)])
        q_st = sb("qst", (P, PAIRS, 2, S), F32R)
        k_st = sb("kst", (P, PAIRS, S), F32R)
        k1_raw = sb("k1_raw", (P, HP, S))
        k1 = Ring([k1_raw])
        v_x = [sb(f"vx{i}", (P, TILES, H, HD + 1)) for i in range(2)]
        ctx_tok = ctxTr.buffers[0]
        exps = sb("exps", (P, 3, TILES, 2, S))
        E = Ring([exps[:, i] for i in range(3)])
        nm = [sb(f"nm{i}", (P, TILES, H // 2)) for i in range(2)]
        nmp = [sb(f"nmp{i}", (P, TILES, 2, 2, HP), F32R) for i in range(2)]
        mT = [sb(f"mT{i}", (4 * HP, S), F32R) for i in range(2)]
        rsum = Ring([sb(f"rsum{i}", (P, TILES, H // 2)) for i in range(2)])
        stats = Ring([sb(f"stats{i}", (P, 6)) for i in range(2)])
        mv = Ring([sb(f"mv{i}", (P, TILES, 2)) for i in range(2)])
        veps = Ring([sb(f"veps{i}", (P, TILES)) for i in range(2)])
        rstd = Ring([sb(f"rstd{i}", (P, TILES)) for i in range(2)])
        ctx_o = sb("ctx_o", (P, TILES, D))
        zb = sb("zb", (P, TILES, 3, L + 5))
        zr = sb("zr", (P, TILES, 3, L + 5))
        top = sb("top", (P, TILES, 3, 8))
        top3 = sb("top3", (P, TILES, 3, 8))
        zmask = zr[:, :, :, 0:L]
        zexp = sb("zexp", (P, TILES, 3, L))
        zsum = sb("zsum", (P, TILES, 3))
        C_buf = Ring([sb(f"C{i}", (P, TILES, 3, L)) for i in range(2)])
        c3T = pw[0:L, :]
        row = Ring([sb(f"row{i}", (P, TILES, ROW)) for i in range(1)])
        router_mem = sb("router_mem", (P, 2, DT, S))
        xdT = router_mem[:, 0]
        lmax = sb("lmax", (P, TILES))
        prob = sb("prob", (P, TILES, NE))
        psum_ = sb("psum_", (P, TILES))
        ptop = sb("ptop", (P, TILES, 8))
        prep = sb("prep", (P, TILES, NE))
        pmask = sb("pmask", (P, TILES, NE))
        pmask_bf = sb("pmask_bf", (P, TILES, NE), BF16)
        tsum = sb("tsum", (P, TILES))
        seen_cnt = [sb(f"seen_cnt{i}", (P, NE)) for i in range(2)]
        pos = prob
        sval = prep
        stop8 = sb("stop8", (P, TILES, 8))
        sidx = Ring([sb(f"sidx{i}", (P, TILES, 8), U32) for i in range(2)])
        sT_a = router_mem[0:FC, 1]
        stage = [k1_raw[:, :, :].rearrange("p n s -> p (n s)"),
                 router_mem[:, :, :, :].rearrange("p a b s -> p (a b s)")]
        empty_rows = row.buffers[0][:, 0, :]
        NW = 2
        WE = 2 * DT * FH + 2 * D
        ew_mem = exps[:, :, :, :, :].rearrange("p i t k s -> p (i t k s)")[:, 0:NW * WE].rearrange(
            "p (i n) -> p i n", i=NW)
        ew_mem = [ew_mem[:, i, :] for i in range(NW)]
        ewg = [w[:, 0:DT * FH].rearrange("p (a f) -> p a f", a=DT) for w in ew_mem]
        ewu = [w[:, DT * FH:2 * DT * FH].rearrange("p (a f) -> p a f", a=DT) for w in ew_mem]
        ewd = [w[0:FC, 2 * DT * FH:WE].rearrange("p (a d) -> p a d", a=2) for w in ew_mem]
        NX = 2
        erow = [row.buffers[0][:, 0, :], row.buffers[0][:, 1, :]]
        eid = [sidx.buffers[0][:, 0, 0:1], sidx.buffers[0][:, 0, 1:2], sidx.buffers[0][:, 0, 2:3]]
        exT = [xhat.buffers[i][:, t, :] for i in range(2) for t in range(2)]
        ey = [X.buffers[i][:, 0, :] for i in range(3)]

        work = Ring([ps(f"work{i}") for i in range(4)])
        score = Ring([ps(f"score{i}") for i in range(2)])
        HB, HQ = 32, 4
        attn_out = [ps(f"attn_out{i}") for i in range(2)]

        def outT(g):
            return attn_out[g // 2][:, (g % 2) * S:(g % 2 + 1) * S]

        attn_out_free = [()] * TILES

        c_w = Counter(sem("weights_in"))
        c_stage = [Counter(sem(f"stage_in{i}")) for i in range(2)]
        c_x = [Counter(sem(f"x_in{i}")) for i in range(4)]
        c_ctxT = Counter(sem("ctxT_in"))
        c_ctx = Counter(sem("ctx_in"))
        c_k1 = Counter(sem("k1_in"))
        c_m = [Counter(sem(f"max_rows{i}")) for i in range(2)]
        c_init = Counter(sem("slots_init"))
        c_out = [Counter(sem(f"out_store{i}")) for i in range(2)]
        c_scat = [Counter(sem(f"dispatch{i}")) for i in range(2)]
        c_ew = [Counter(sem(f"expert_w{i}")) for i in range(NW)]
        c_er = [Counter(sem(f"expert_rows{i}")) for i in range(NX)]
        c_add = Counter(sem("combine"))

        ident0 = xhat.buffers[0][:, 0, 0:P]
        m_id0 = pool.do(lambda e: e.memset(ident0, 0.0))
        m_id = pool.do(lambda e: e.affine_select(out=ident0, in_=ident0, compare_op=ALU.not_equal,
                                                 fill=1.0, base=0, pattern=[[-1, P]], channel_multiplier=1),
                       after=[m_id0])
        m_id = m_idr = act.do(lambda e: e.copy(identr[:, :], ident0), after=[m_id])
        xhat.free[0] = (m_idr,)
        ident = identr[:, :].bitcast(F32)
        m_b0 = pool.do(lambda e: e.memset(before[:, :], 1.0))
        m_before = pool.do(lambda e: e.affine_select(out=before[:, :], in_=before[:, :], compare_op=ALU.is_ge,
                                                     fill=0.0, base=-1, pattern=[[1, P]],
                                                     channel_multiplier=-1), after=[m_b0])
        m_ones = pool.do(lambda e: e.memset(ones_bf[:, :], 1.0))
        m_mh = pool.do(lambda e: e.memset(minus_half[:, :], -0.5))
        m_tok0 = pool.do(lambda e: e.iota(token_no[:, :], [[0, 1]], base=0, channel_multiplier=1,
                                          allow_small_or_imprecise_dtypes=True))
        m_er0 = pool.do(lambda e: e.memset(empty_rows, 0.0))
        m_er = pool.do(lambda e: e.tensor_scalar(empty_rows[:, ROW - 1:ROW], token_no[:, :], float(T), None,
                                                 ALU.add), after=[m_er0, m_tok0])
        m_end = pool.do(lambda e: e.iota(expert_end[:, :], [[-CAP, NE]], base=SLOTS, channel_multiplier=0,
                                         allow_small_or_imprecise_dtypes=True))
        m_lr = pool.do(lambda e: e.memset(low_rows[:, :], 0.0), after=[m_end])
        for base in (0, ROWS):
            m_lr = pool.do(lambda e, b=base: e.memset(low_rows[b + 32:b + 64, :], -1.0), after=[m_lr])
            m_lr = pool.do(lambda e, b=base: e.affine_select(
                out=low_rows[b + 32:b + 64, :], in_=low_rows[b + 32:b + 64, :], compare_op=ALU.is_ge, fill=0.0,
                base=-16, pattern=[[0, 1]], channel_multiplier=1), after=[m_lr])
        m_or = pool.do(lambda e: e.memset(one_rows[:, :], 0.0), after=[m_lr])
        for base in (0, ROWS):
            m_or = pool.do(lambda e, b=base: e.memset(one_rows[b + 32:b + 64, :], 1.0), after=[m_or])
            m_or = pool.do(lambda e, b=base: e.affine_select(
                out=one_rows[b + 32:b + 64, :], in_=one_rows[b + 32:b + 64, :], compare_op=ALU.is_gt, fill=0.0,
                base=16, pattern=[[0, 1]], channel_multiplier=-1), after=[m_or])
        m_qz = []
        for t in stack.buffers:
            m_qz.append(dve.do(lambda e, t=t: e.memset(t[:, :, :].bitcast(F32), 0.0)))
        m_qz.append(pool.do(lambda e: e.memset(q_st[:, :, :, :].bitcast(F32), 0.0), after=[m_or]))
        for t in v_x:
            m_qz.append(dve.do(lambda e, t=t: e.memset(t[:, :, :, HD:HD + 1], 1.0)))
        m_qz.append(dve.do(lambda e: e.memset(zb[:, :, :, L:], SENTINEL)))
        m_qz.append(dve.do(lambda e: e.memset(top3[:, :, :, KR:], SENTINEL)))
        m_ao = [dve.do(lambda e, t=t: e.memset(t[:, :], 0.0)) for t in attn_out]
        m_cnt0 = dve.do(lambda e: e.memset(seen_cnt[0][:, :], 0.0))

        m_init = sp.dma(lambda e: e.dma_start(slots_dram.rearrange("(e c) f -> c e f", c=CAP),
                                              empty_rows.unsqueeze(1).broadcast_to([P, NE, ROW])),
                        c_init, after=[m_er])

        m_init = sp.dma(lambda e: e.dma_start(out_pad[T:T + CAP, :], empty_rows[:, 0:D]), c_init, after=[m_er])
        row.free[0] = (m_init,)

        def bcast(v, n):
            return v.rearrange("(a d) -> a d", a=1).broadcast_to([P, n])

        for dst, src in ((bq[:, :], bcast(bq_in, D)), (bkv[:, :], bcast(bkv_in, 2 * D)), (bo[:, :], bcast(bo_in, D)),
                         (b2[:, :], b2_in), (pw[:, :], pw_in), (uT[:, :], uT_in), (rT[:, :, :], rT_in),
                         (wsgu[:, :, :], wsgu_in), (wsd[:, :, :], wsd_in)):
            m_w = sp.dma(lambda e, d=dst, s=src: e.dma_start(d, s), c_w)

        _, wk, free = work.take()
        for dt in range(DT):
            m = pe.do(lambda e, wk=wk, dt=dt: e.matmul(wk[:, dt * 64:dt * 64 + 3 * L], pw[:, dt * P:(dt + 1) * P],
                                                      uT[:, :], start=True, stop=True), after=[m_w])
        gsrc = wk[:, 0:DT * 64].rearrange("p (t n) -> p t n", t=DT)[:, :, 0:3 * L]
        m1 = act.do(lambda e: e.copy(gT[0][:, :, :], gsrc), after=[m])
        m_g = dve.do(lambda e: e.tensor_tensor(gT[1][:, :, :], gsrc, gT[0][:, :, :].bitcast(F32), ALU.subtract),
                     after=[m, m1])
        work.give(0, [m1, m_g])

        stage_free = [(), ()]
        n_st = 0

        def load_parts(dst, src, n):
            nonlocal n_st
            i = n_st % 2
            n_st += 1
            buf = stage[i][:, 0:n]
            m = sp.dma(lambda e: e.dma_start(buf, src), c_stage[i], reuse=stage_free[i])
            mh = act.do(lambda e: e.copy(dst[0], buf), after=[m])
            ml = dve.do(lambda e: e.tensor_tensor(dst[1], buf, dst[0].bitcast(F32), ALU.subtract), after=[m, mh])
            stage_free[i] = (mh, ml)
            return ml

        def flat(t):
            return t.rearrange("p a b -> p (a b)")

        m_wq = load_parts([flat(w[:, :, :]) for w in wq], flat(wqT_in), DT * D)
        m_wkv = load_parts([flat(w[:, :, :]) for w in wkv], flat(wkvT_in), DT * 2 * D)
        m_wo = load_parts([flat(w[:, :, :]) for w in wo], flat(woT_in), DT * D)
        m_wmix = []
        mix_jobs = []
        for n, src in ((0, w1T_in), (1, w2T_in)):
            for l in range(0, L, 2):
                mix_jobs.append((n, l, src))

        def load_mix():
            nonlocal m_k1one
            for n, l, src in mix_jobs:
                m = load_parts([w[:, l:l + 2, :, :].rearrange("p l a b -> p (l a b)") for w in wmix[n]],
                               src[:, l:l + 2, :, :].rearrange("p l a b -> p (l a b)"), 2 * DT * D)
                m_wmix.append(m)
                yield stage_free[n_st % 2]
            m_k1one = dve.do(lambda e: e.memset(k1_raw[:, :, :], 1.0), reuse=stage_free[0])
            dstate["xdT"] = dstate["sT"] = stage_free[1]

        m_k1one = None

        def layer_norm(src, src_marks, dst, dst_free):
            im, mvb, fm = mv.take()
            iv, ve, fv = veps.take()
            ir, rs, fr = rstd.take()
            last = None
            for t in range(TILES):
                i, st, f = stats.take()
                m = dve.do(lambda e, st=st, t=t: e.bn_stats(st[:, :], src[:, t, :]), after=[src_marks[t]], ns=335)
                m = dve.do(lambda e, st=st, t=t: e.bn_aggr(mvb[:, t, :], st[:, :]), after=[m], reuse=fm, ns=75)
                stats.give(i, [m])
            m = dve.do(lambda e: e.tensor_scalar(ve[:, :], mvb[:, :, 1], EPS, None, ALU.add), after=[m], reuse=fv)
            m = pool.do(lambda e: e.tensor_tensor(rs[:, :], ve[:, :], minus_half[:, :], ALU.pow),
                        after=[m, m_mh], reuse=fr, ns=630)
            veps.give(iv, [m])
            out = []
            for t in range(TILES):
                out.append(dve.do(lambda e, t=t: e.tensor_scalar(dst[:, t, 0:D], src[:, t, :], mvb[:, t, 0:1],
                                                                rs[:, t:t + 1], ALU.subtract, ALU.mult),
                                  after=[m], reuse=dst_free, ns=323))
            mv.give(im, out)
            rstd.give(ir, out)
            return out

        def transposed(src, marks, both=False):
            i, wk, free = work.take()
            v = wk[:, :].rearrange("p (a b) -> p a b", a=DT)
            for t in range(TILES):
                for dt in range(DT):
                    m = pe.do(lambda e, t=t, dt=dt: e.transpose(v[:, dt, t * P:(t + 1) * P],
                                                                src[:, t, dt * P:(dt + 1) * P], ident),
                              after=[*(marks if both else [marks[t]]), m_id], reuse=free, ns=107)
            return i, v, m

        def claim(ring):
            while not ring.idle:
                yield BLOCKED
            return ring.take()

        def transposed_parts(src, marks, both=False):
            ip, (hi, lo), free = yield from claim(parts)
            i, v, m = transposed(src, marks, both)
            mh = act.do(lambda e: e.copy(hi[:, :, :], v[:, :, :]), after=[m], reuse=free)
            ml = dve.do(lambda e: e.tensor_tensor(lo[:, :, :], v[:, :, :], hi[:, :, :].bitcast(F32), ALU.subtract),
                        after=[m, mh], reuse=free, ns=602)
            work.give(i, [mh, ml])
            return ip, (hi, lo), ml, m

        TERMS = ((0, 0), (1, 0), (0, 1))

        def product3(out, left, right, after, reuse, ns=107):
            n = 0
            for a, b in TERMS:
                for dt in range(DT):
                    lhs, rhs = left(a, dt), right(b, dt)
                    m = pe.do(lambda e: e.matmul(out, lhs, rhs, start=(n == 0), stop=(n == 3 * DT - 1)),
                              after=after, reuse=reuse, ns=ns)
                    n += 1
            return m

        def stack_half(src, marks, t, half, is_q, dst, dst_free):
            i, st, free = yield from claim(stack)
            v = src.rearrange("p (h r) -> p h r", r=HD)
            blocks = st[:, :, :].rearrange("p h (a r) -> p h a r", r=HD)
            high = blocks[:, :, 0:4:3, :] if is_q else blocks[:, :, 0:2, :]
            m1 = act.do(lambda e: e.copy(high, v.unsqueeze(2).broadcast_to([P, H // 2, 2, HD])),
                        after=[*marks, *m_qz], reuse=free, ns=340)
            m2 = dve.do(lambda e: e.tensor_tensor(blocks[:, :, 1 if is_q else 3, :], v,
                                                  blocks[:, :, 0, :].bitcast(F32), ALU.subtract),
                        after=[m1], reuse=free, ns=200)
            yield [m2]
            pair = st[:, :, :].rearrange("p (n k) r -> p n (k r)", k=2)
            iw, wk, free = work.take()
            for n in range(HP):
                m = pe.do(lambda e, n=n: e.transpose(wk[:, n * P:(n + 1) * P].bitcast(F32R), pair[:, n, :],
                                                     identr[:, :]), after=[m1, m2, m_idr], reuse=free, ns=85)
            stack.give(i, [m])
            rows = wk[:, :].rearrange("p (n t) -> p n t", n=HP)
            pr = slice(half * HP, (half + 1) * HP)
            tk = slice(t * P, (t + 1) * P)
            if is_q:
                done = [act.do(lambda e, k=k: e.copy(dst[k * ROWS:(k + 1) * ROWS, pr, k, tk],
                                                     rows[k * ROWS:(k + 1) * ROWS]),
                               after=[m, *m_qz], reuse=dst_free) for k in range(2)]
            else:
                done = [act.do(lambda e: e.activation(dst[:, pr, tk], rows, ACT.Identity, bias=one_rows[:, :]),
                               after=[m, m_or], reuse=dst_free)]
            work.give(iw, done)
            return done, [m1, m2]

        hstate = [{"nm": (), "m_rows": (), "st": ()} for _ in range(2)]
        ctx_o_free = []

        def attend(n, half, vx, q_marks, k_marks, v_marks):
            hs = hstate[half]
            pairs = range(half * HP, (half + 1) * HP)
            earlier = []
            for p in pairs:
                for t in range(TILES):
                    i, wk, free = work.take()
                    for k in range(2):
                        m = pe.do(lambda e, wk=wk, p=p, t=t, k=k: e.matmul(
                            wk[:, k * S:(k + 1) * S], q_st[:, p, k, t * P:(t + 1) * P], k_st[:, p, :],
                            start=True, stop=True), after=[*q_marks, *k_marks], reuse=free, ns=130)
                    h0 = 2 * (p - half * HP)
                    r = dve.do(lambda e, wk=wk, h0=h0, t=t: e.tensor_reduce(
                        nm[half][:, t, h0:h0 + 2], wk[:, :].rearrange("p (k s) -> p k s", k=2), AX_X, ALU.max,
                        negate=True), after=[m], reuse=hs["nm"], ns=598)
                    work.give(i, [r])
                    yield earlier
                    earlier = [r]
            yield [r]
            v = nm[half][:, :, :].rearrange("p t (n k) -> p t k n", k=2)
            np_ = nmp[half]
            m1 = dve.do(lambda e: e.tensor_copy(np_[:, :, 0, :, :], v), after=[r], reuse=hs["m_rows"], ns=85)
            m2 = dve.do(lambda e: e.tensor_tensor(np_[:, :, 1, :, :], v, np_[:, :, 0, :, :].bitcast(F32),
                                                  ALU.subtract), after=[m1], ns=100)
            hs["nm"] = (m2,)
            yield [m2]
            i, wk, free = work.take()
            for t in range(TILES):
                mt = pe.do(lambda e, t=t, wk=wk: e.transpose(
                    wk[0:4 * HP, t * P:(t + 1) * P].bitcast(F32R),
                    np_[:, t, :, :, :].rearrange("p a k n -> p (a k n)"), identr[:, :]),
                    after=[m1, m2], reuse=free)
            mc = act.do(lambda e, wk=wk: e.copy(mT[half][:, :], wk[0:4 * HP, 0:S]), after=[mt],
                        reuse=hs["m_rows"], ns=264)
            work.give(i, [mc])
            for part in range(2):
                for k in range(2):
                    r0 = (part * 2 + k) * HP
                    mm = sp.dma(lambda e, part=part, k=k, r0=r0: e.dma_start(
                        q_st[ROWS * k + 32 + part:ROWS * k + 33 + part, half * HP:(half + 1) * HP, k, :].bitcast(F32),
                        mT[half][r0:r0 + HP, :].bitcast(F32)), c_m[half],
                        after=[mc], reuse=[m, *q_marks])
            hs["m_rows"] = (mm,)
            yield [mm]
            pend = None

            def times_v(p, iE, Eb, marks):
                for s in range(TILES):
                    for k in range(2):
                        h = 2 * p + k
                        r0 = HB * (h % HQ)
                        m = pe.do(lambda e, k=k, h=h, s=s, r0=r0: e.matmul(
                            outT(h // HQ)[r0:r0 + HD + 1, :], vx[:, s, h, :], Eb[:, s, k, :],
                            start=(s == 0), stop=(s == TILES - 1)),
                            after=[*marks, *v_marks, *m_ao], reuse=attn_out_free[half], ns=220)
                E.give(iE, [m])
                return m

            for p in pairs:
                iE, Eb, fE = yield from claim(E)
                marks = []
                for s in range(TILES):
                    i, sc, free = score.take()
                    m = pe.do(lambda e, sc=sc, p=p, s=s: e.matmul(
                        sc[:, :], k_st[:, p, s * P:(s + 1) * P], q_st[:, p, :, :].rearrange("p k t -> p (k t)"),
                        start=True, stop=True), after=[mm], reuse=free, ns=240)
                    a = act.do(lambda e, sc=sc, s=s, Eb=Eb: e.activation(
                        Eb[:, s, :, :].rearrange("p k t -> p (k t)"), sc[:, :], ACT.Exp, scale=0.25),
                        after=[m], reuse=fE)
                    score.give(i, [a])
                    marks.append(a)
                    if s == 0:
                        yield score.free[score.idle[0]]
                if pend:
                    yield pend[3]
                    times_v(*pend)
                pend = (p, iE, Eb, marks)
                if p != pairs[-1]:
                    yield score.free[score.idle[0]]
            hs["st"] = (m,)
            yield pend[3]
            m_av = times_v(*pend)
            iT, oT, fT = yield from claim(E)
            yield [m_av]
            oT = oT.rearrange("p t k s -> p (t k) s")
            mc = act.do(lambda e: e.copy(oT[:, 0:2, :].rearrange("p g s -> p (g s)"), attn_out[half][:, :]),
                        after=[m_av], reuse=fT)
            attn_out_free[half] = (mc,)
            while completed < n - 1:
                yield BLOCKED
            yield [mc]
            i, wk, free = work.take()
            for t in range(TILES):
                for g in range(2):
                    mt = pe.do(lambda e, g=g, t=t: e.transpose(wk[:, (2 * t + g) * P:(2 * t + g + 1) * P],
                                                               oT[:, g, t * P:(t + 1) * P], ident),
                               after=[mc, m_id], reuse=free, ns=107)
            E.give(iT, [mt])
            ir, rs, fr = rsum.take()
            o = wk[:, :].rearrange("p (t h r) -> p t h r", t=TILES, r=HB)
            r = dve.do(lambda e: e.reciprocal(rs[:, :, :], o[:, :, :, HD]), after=[mt], reuse=fr)
            w = dve.do(lambda e: e.tensor_tensor(
                ctx_o[:, :, half * P:(half + 1) * P].rearrange("p t (h r) -> p t h r", r=HD), o[:, :, :, 0:HD],
                rs[:, :, :].unsqueeze(3).broadcast_to([P, TILES, H // 2, HD]), ALU.mult), after=[r],
                reuse=ctx_o_free, ns=400)
            work.give(i, [r, w])
            rsum.give(ir, [w])
            return w, m_av

        emitted = {"A": -1, "B": -1, "C": -1}
        xs = {}

        order = []
        for b in range(NB + 2):
            if b < NB:
                order.append((0, b))
            if b >= 2:
                order.append((1, b - 2))
        jobs = [{"layer": layer, "b": b, "halves": []} for layer, b in order]
        completed = -1
        v_free = [(), ()]
        k_raw = []

        def prepare_0(job):
            b = job["b"]
            ix, xb, fx = yield from claim(X)
            mx = sp.dma(lambda e: e.dma_start(xb[:, :, :], x_in[b].rearrange("(t p) d -> p t d", p=P)), c_x[ix],
                        reuse=fx)
            i, ct, fc = ctxTr.take()
            mc = sp.dma(lambda e: e.dma_start(ct[:, :, :], ctxT_in[b].rearrange("(a p) s -> p a s", p=P)), c_ctxT,
                        reuse=fc)
            yield [mc]
            ikt, kt, fk = yield from claim(xhat)
            ic, (ch, cl), fcp = yield from claim(parts)
            c1 = act.do(lambda e: e.copy(ch[:, :, :], ct[:, :, :]), after=[mc], reuse=fcp)
            c2 = pool.do(lambda e: e.tensor_tensor(cl[:, :, :], ct[:, :, :], ch[:, :, :].bitcast(F32), ALU.subtract),
                         after=[c1], reuse=fcp)
            ctxTr.give(i, [c2])
            ih, xh, fh = yield from claim(xhat)
            mh = layer_norm(xb, [mx, mx], xh, fh)
            yield [c2]
            mk, mv_ = [], []
            for t in range(TILES):
                i, wk, free = work.take()
                tk = slice(t * P, (t + 1) * P)
                m = product3(wk[:, :], lambda a, dt, tk=tk: (ch, cl)[a][:, dt, tk], lambda a, dt: wkv[a][:, dt, :],
                             after=[c1, c2, m_wkv], reuse=free, ns=213)
                mk.append(dve.do(lambda e, wk=wk, t=t: e.tensor_tensor(kt[:, t, :], wk[:, 0:D], bkv[:, 0:D],
                                                                      ALU.add), after=[m, m_w], reuse=fk, ns=335))
                mv_.append(dve.do(lambda e, wk=wk, t=t: e.tensor_tensor(
                    v_x[0][:, t, :, 0:HD], wk[:, D:2 * D].rearrange("p (h r) -> p h r", h=H),
                    bkv[:, D:2 * D].rearrange("p (h r) -> p h r", h=H), ALU.add),
                    after=[m, *m_qz], reuse=v_free[0], ns=335))
                work.give(i, [mk[t], mv_[t]])
                yield ()
            parts.give(ic, [m])
            ip, (hi, lo), mp, rdm = yield from transposed_parts(xh, mh)
            yield [mp]
            mq = []
            for t in range(TILES):
                i, wk, free = work.take()
                tk = slice(t * P, (t + 1) * P)
                m = product3(wk[:, 0:D], lambda a, dt, tk=tk: (hi, lo)[a][:, dt, tk], lambda a, dt: wq[a][:, dt, :],
                             after=[mp, m_wq], reuse=free)
                mq.append(dve.do(lambda e, wk=wk, t=t: e.tensor_tensor(xh[:, t, :], wk[:, 0:D], bq[:, :], ALU.add),
                                 after=[m, m_w], reuse=[rdm], ns=335))
                work.give(i, [mq[t]])
                yield ()
            parts.give(ip, [m])
            mb = pool.do(lambda e: e.tensor_tensor(xb[:, :, :], xb[:, :, :],
                                                   bo[:, :].unsqueeze(1).broadcast_to([P, TILES, D]), ALU.add),
                         after=[mx, m_w], reuse=mh)
            job.update(x=(ix, xb, mb), q=(ih, xh, mq), k=(ikt, kt, mk), v=(v_x[0], mv_), stacked=[])

        def prepare_1(job):
            while emitted["B"] < job["b"]:
                yield BLOCKED
            ix, xb, mx = xs[job["b"]]
            i, ct, fc = ctxTr.take()
            mt = sp.dma(lambda e: e.dma_start(ctx_tok[:, :, :], ctx_in[job["b"]].rearrange("(t p) d -> p t d", p=P)),
                        c_ctx, reuse=fc)
            ih, xh, fh = yield from claim(xhat)
            mh = layer_norm(xb, mx, xh, fh)
            yield [mt]
            mv_ = pool.do(lambda e: e.tensor_copy(v_x[1][:, :, :, 0:HD],
                                                  ctx_tok[:, :, :].rearrange("p t (h r) -> p t h r", h=H)),
                          after=[mt, *m_qz], reuse=v_free[1])
            ctxTr.give(i, [mv_])
            job.update(x=(ix, xb, mh), q=(ih, xh, mh), v=(v_x[1], [mv_]), stacked=[])

        def prepare():
            last = [None, None]
            for job in jobs:
                layer = job["layer"]
                while last[layer] and len(last[layer]["halves"]) < 2:
                    yield BLOCKED
                if last[layer]:
                    v_free[layer] = tuple(av for _, av in last[layer]["halves"])
                yield from (prepare_0 if layer == 0 else prepare_1)(job)
                last[layer] = job
                yield ()

        def raw_keys():
            while m_k1one is None:
                yield BLOCKED
            for layer, b in order:
                if layer == 1:
                    src = ctxT_in[b].rearrange("(n k r) s -> k r n s", k=2, r=HD)
                    for half in range(2):
                        i, raw, free = yield from claim(k1)
                        for k in range(2):
                            for r0 in (0, 16, 48):
                                m = sp.dma(lambda e, k=k, r0=r0, half=half: e.dma_start(
                                    raw[ROWS * k + r0:ROWS * k + r0 + 16, :, :],
                                    src[k][:, half * HP:(half + 1) * HP, :]), c_k1, after=[m_k1one], reuse=free)
                        k_raw.append((i, raw, m))
                        yield ()

        def attend_half(half):
            hs = hstate[half]
            hd = slice(half * P, (half + 1) * P)
            taken = 0
            for n, job in enumerate(jobs):
                while "q" not in job:
                    yield BLOCKED
                vx, v_marks = job["v"]
                k_marks, q_marks = [], []
                rd = []
                if job["layer"] == 0:
                    ikt, kt, mk = job["k"]
                    for t in range(TILES):
                        d, r = yield from stack_half(kt[:, t, hd], [mk[t]], t, half, False, k_st, hs["st"])
                        k_marks += d
                        rd += r
                    job.setdefault("k_read", []).append(rd)
                    if len(job["k_read"]) == 2:
                        xhat.give(ikt, [m for r in job["k_read"] for m in r])
                else:
                    pr = slice(half * HP, (half + 1) * HP)
                    while len(k_raw) <= 2 * job["b"] + half:
                        yield BLOCKED
                    ik, raw, mr = k_raw[2 * job["b"] + half]
                    yield [mr]
                    m1 = act.do(lambda e: e.copy(k_st[:, pr, :], raw[:, :, :]), after=[mr], reuse=hs["st"], ns=950)
                    m2 = dve.do(lambda e: e.scalar_tensor_tensor(k_st[:, pr, :], k_st[:, pr, :].bitcast(F32),
                                                                 low_rows[:, :], raw[:, :, :], ALU.mult, ALU.add),
                                after=[m1, m_lr], ns=1150)
                    k1.give(ik, [m2])
                    k_marks = [m2]
                ih, xh, mq = job["q"]
                rd = []
                for t in range(TILES):
                    d, r = yield from stack_half(xh[:, t, hd], [mq[t]], t, half, True, q_st, hs["st"])
                    q_marks += d
                    rd += r
                job.setdefault("q_read", []).append(rd)
                if len(job["q_read"]) == 2:
                    xhat.give(ih, [m for r in job["q_read"] for m in r])
                yield q_marks
                job["halves"].append((yield from attend(n, half, vx, q_marks, k_marks, v_marks)))
                yield ()

        def complete():
            nonlocal completed
            for n, job in enumerate(jobs):
                while len(job["halves"]) < 2:
                    yield BLOCKED
                ix, xb, mb = job["x"]
                out = [w for w, _ in job["halves"]]
                yield out
                if job["layer"] == 0:
                    ip, (hi, lo), mp, rdm = yield from transposed_parts(ctx_o, out, both=True)
                    ctx_o_free[:] = [rdm]
                    completed = n
                    yield [mp]
                    marks = []
                    for t in range(TILES):
                        i, wk, free = work.take()
                        tk = slice(t * P, (t + 1) * P)
                        m = product3(wk[:, 0:D], lambda a, dt, tk=tk: (hi, lo)[a][:, dt, tk],
                                     lambda a, dt: wo[a][:, dt, :], after=[mp, m_wo], reuse=free)
                        r = dve.do(lambda e, wk=wk, t=t: e.tensor_tensor(xb[:, t, :], xb[:, t, :], wk[:, 0:D],
                                                                         ALU.add), after=[m, mb], ns=335)
                        work.give(i, [r])
                        marks.append(r)
                    parts.give(ip, [m])
                    xs[job["b"]] = (ix, xb, marks)
                    emitted["A"] = job["b"]
                else:
                    mo = pool.do(lambda e: e.tensor_tensor(xb[:, :, :], xb[:, :, :], ctx_o[:, :, :], ALU.add),
                                 after=out, reuse=mb)
                    ctx_o_free[:] = [mo]
                    completed = n
                    xs[job["b"]] = (ix, xb, [mo, mo])
                    emitted["C"] = job["b"]
                yield ()

        bstate = {"c3": (m_g,), "route": ()}

        def mixture(n, hi, lo, mp, C, mC, acc, first, reuse):
            out = [None, None]
            for t in range(TILES):
                tk = slice(t * P, (t + 1) * P)
                prev = first[t]
                for l in range(0, L, 2):
                    i, wk, free = work.take()
                    m = product3(wk[:, :].rearrange("p (l d) -> p l d", l=2),
                                 lambda a, dt, tk=tk: (hi, lo)[a][:, dt, tk],
                                 lambda a, dt, l=l: wmix[n][a][:, l:l + 2, dt, :],
                                 after=[mp, m_wmix[n * (L // 2) + l // 2]], reuse=free, ns=213)
                    for k in range(2):
                        c = C[:, t, n, l + k:l + k + 1]
                        src = wk[:, k * D:(k + 1) * D]
                        if prev is None:
                            prev = dve.do(lambda e, src=src, c=c, t=t: e.tensor_scalar(
                                acc[:, t, :], src, c, None, ALU.mult), after=[m, mC], reuse=reuse, ns=396)
                        else:
                            prev = dve.do(lambda e, src=src, c=c, t=t: e.scalar_tensor_tensor(
                                acc[:, t, :], src, c, acc[:, t, :], ALU.mult, ALU.add), after=[m, mC, prev], ns=396)
                    work.give(i, [prev])
                    yield ()
                out[t] = prev
            return out, m

        routed = []

        def route(b):
            ix, xb, mx = xs[b]
            ih, xh, fh = yield from claim(xhat)
            mh = layer_norm(xb, mx, xh, fh)
            yield mh
            ip, (hi, lo), mp, rdm = yield from transposed_parts(xh, mh)
            xhat.give(ih, [rdm])
            yield [mp]
            i, wk, free = work.take()
            for t in range(TILES):
                tk = slice(t * P, (t + 1) * P)
                m = product3(wk[:, t * 64:t * 64 + 3 * L], lambda a, dt, tk=tk: (hi, lo)[a][:, dt, tk],
                             lambda a, dt: gT[a][:, dt, :], after=[mp, m_g], reuse=free)
            zsrc = wk[:, 0:TILES * 64].rearrange("p (t n) -> p t n", t=TILES)[:, :, 0:3 * L].rearrange(
                "p t (s l) -> p t s l", s=3)
            mz = dve.do(lambda e: e.tensor_copy(zb[:, :, :, 0:L], zsrc), after=[m, *m_qz],
                        reuse=bstate["route"])
            work.give(i, [mz])
            yield [mz]
            for t in range(TILES):
                for s in range(3):
                    mt = dve.do(lambda e, t=t, s=s: e.max(top[:, t, s, :], zb[:, t, s, 0:L]), after=[mz])
            m3 = dve.do(lambda e: e.tensor_copy(top3[:, :, :, 0:KR], top[:, :, :, 0:KR]), after=[mt])
            for t in range(TILES):
                for s in range(3):
                    mr = dve.do(lambda e, t=t, s=s: e.match_replace(
                        out=zr[:, t, s, :], in_to_replace=top3[:, t, s, :], in_values=zb[:, t, s, :],
                        imm_value=TAKEN), after=[m3, mz])
            mk = dve.do(lambda e: e.tensor_tensor(zmask[:, :, :, :], zr[:, :, :, 0:L], zb[:, :, :, 0:L],
                                                  ALU.not_equal), after=[mr])
            md = dve.do(lambda e: e.tensor_tensor(zexp[:, :, :, :], zb[:, :, :, 0:L],
                                                  top[:, :, :, 0:1].broadcast_to([P, TILES, 3, L]),
                                                  ALU.subtract), after=[mt])
            me = act.do(lambda e: e.activation(zexp[:, :, :, :], zexp[:, :, :, :], ACT.Exp), after=[md])
            yield [me]
            m = dve.do(lambda e: e.tensor_tensor(zexp[:, :, :, :], zexp[:, :, :, :], zmask[:, :, :, :], ALU.mult),
                       after=[me, mk])
            m2 = dve.do(lambda e: e.tensor_reduce(zsum[:, :, :], zexp[:, :, :, :], AX_X, ALU.add), after=[m])
            m2 = dve.do(lambda e: e.reciprocal(zsum[:, :, :], zsum[:, :, :]), after=[m2])
            iC, C, fC = yield from claim(C_buf)
            mC = dve.do(lambda e: e.tensor_tensor(C[:, :, :, :], zexp[:, :, :, :],
                                                  zsum[:, :, :].unsqueeze(3).broadcast_to([P, TILES, 3, L]),
                                                  ALU.mult), after=[m2], reuse=fC)
            bstate["route"] = (mC,)
            routed.append((ip, hi, lo, mp, iC, C, mC, mh))

        def mix(b):
            ix, xb, mx = xs[b]
            ip, hi, lo, mp, iC, C, mC, mh = routed[b]
            ih, hb, fh = yield from claim(xhat)
            out, ml = yield from mixture(0, hi, lo, mp, C, mC, hb, [None, None], fh)
            parts.give(ip, [ml])
            mg = act.do(lambda e: e.activation(hb[:, :, :], hb[:, :, :], ACT.Gelu), after=out)
            i, wk, free = work.take()
            for t in range(TILES):
                m = pe.do(lambda e, t=t: e.transpose(wk[0:L, t * P:(t + 1) * P], C[:, t, 2, :], ident),
                          after=[mC], reuse=free)
            mc = act.do(lambda e: e.copy(c3T[:, :], wk[0:L, 0:S]), after=[m], reuse=bstate["c3"])
            work.give(i, [mc])
            i, wk, free = work.take()
            for t in range(TILES):
                m = pe.do(lambda e, t=t: e.matmul(wk[:, t * D:(t + 1) * D], c3T[:, t * P:(t + 1) * P], b2[:, :],
                                                  start=True, stop=True), after=[mc, m_w], reuse=free)
            bstate["c3"] = (m,)
            first = []
            for t in range(TILES):
                first.append(dve.do(lambda e, t=t: e.tensor_tensor(xb[:, t, :], xb[:, t, :],
                                                                   wk[:, t * D:(t + 1) * D], ALU.add),
                                    after=[m, mx[t]], reuse=mh))
            work.give(i, first)
            yield [mg]
            ip, (hi, lo), mp, rdm = yield from transposed_parts(hb, [mg, mg])
            xhat.give(ih, [rdm])
            yield [mp]
            out, ml = yield from mixture(1, hi, lo, mp, C, mC, xb, first, ())
            parts.give(ip, [ml])
            C_buf.give(iC, [m, *out])
            xs[b] = (ix, xb, out)
            emitted["B"] = b
            yield ()

        dstate = {"xdT": (), "sT": (), "cnt": m_cnt0, "out": [], "route": ()}

        def stage_d(b):
            ix, xb, mx = xs[b]
            ir, rw, fr = row.take()
            mh = layer_norm(xb, mx, rw, fr)
            yield mh
            i, v, m = transposed(rw, mh)
            mT_ = act.do(lambda e: e.copy(xdT[:, :, :], v[:, :, :]), after=[m], reuse=dstate["xdT"])
            work.give(i, [mT_])
            yield [mT_]
            i, wk, free = work.take()
            for t in range(TILES):
                for dt in range(DT):
                    m = pe.do(lambda e, t=t, dt=dt: e.matmul(wk[:, t * NE:(t + 1) * NE],
                                                             xdT[:, dt, t * P:(t + 1) * P], rT[:, dt, :],
                                                             start=(dt == 0), stop=(dt == DT - 1)),
                              after=[mT_, m_w], reuse=free)
            lg = wk[:, 0:TILES * NE].rearrange("p (t n) -> p t n", t=TILES)
            ma = dve.do(lambda e: e.tensor_reduce(lmax[:, :], lg, AX_X, ALU.max), after=[m], reuse=dstate["route"])
            ms = dve.do(lambda e: e.tensor_tensor(prob[:, :, :], lg,
                                                  lmax[:, :].unsqueeze(2).broadcast_to([P, TILES, NE]),
                                                  ALU.subtract), after=[ma])
            work.give(i, [ms])
            me = act.do(lambda e: e.activation(prob[:, :, :], prob[:, :, :], ACT.Exp), after=[ms])
            yield [me]
            m = dve.do(lambda e: e.tensor_reduce(psum_[:, :], prob[:, :, :], AX_X, ALU.add), after=[me])
            m = dve.do(lambda e: e.reciprocal(psum_[:, :], psum_[:, :]), after=[m])
            mp = dve.do(lambda e: e.tensor_tensor(prob[:, :, :], prob[:, :, :],
                                                  psum_[:, :].unsqueeze(2).broadcast_to([P, TILES, NE]), ALU.mult),
                        after=[m])
            for t in range(TILES):
                mt = dve.do(lambda e, t=t: e.max(ptop[:, t, :], prob[:, t, :]), after=[mp])
            for t in range(TILES):
                mr = dve.do(lambda e, t=t: e.match_replace(out=prep[:, t, :], in_to_replace=ptop[:, t, :],
                                                           in_values=prob[:, t, :], imm_value=-1.0), after=[mt])
            mk = dve.do(lambda e: e.tensor_scalar(pmask[:, :, :], prep[:, :, :], 0.0, None, ALU.is_lt), after=[mr])
            mkb = pool.do(lambda e: e.tensor_copy(pmask_bf[:, :, :], pmask[:, :, :]), after=[mk])
            m = dve.do(lambda e: e.tensor_reduce(tsum[:, :], ptop[:, :, :], AX_X, ALU.add), after=[mt])
            m = dve.do(lambda e: e.reciprocal(tsum[:, :], tsum[:, :]), after=[m])
            m = dve.do(lambda e: e.tensor_tensor(prob[:, :, :], prob[:, :, :],
                                                 tsum[:, :].unsqueeze(2).broadcast_to([P, TILES, NE]), ALU.mult),
                       after=[m])
            mw = dve.do(lambda e: e.tensor_tensor(rw[:, :, D:D + NE], prob[:, :, :], pmask[:, :, :], ALU.mult),
                        after=[m, mk], reuse=fr)
            yield [mkb]
            for t in range(TILES):
                mn = dve.do(lambda e, t=t: e.tensor_scalar(rw[:, t, ROW - 1:ROW], token_no[:, :],
                                                           float(b * S + t * P), None, ALU.add),
                            after=[m_tok0], reuse=fr)
            i, wk, free = work.take()
            for t in range(TILES):
                m = pe.do(lambda e, t=t: e.matmul(wk[:, t * NE:(t + 1) * NE], before[:, :], pmask_bf[:, t, :],
                                                  start=True, stop=(t == 0)), after=[mkb, m_before], reuse=free)
                if t:
                    m = pe.do(lambda e: e.matmul(wk[:, NE:2 * NE], ones_bf[:, :], pmask_bf[:, 0, :],
                                                 start=False, stop=True), after=[m_ones])
            for t in range(TILES):
                m = pe.do(lambda e, t=t: e.matmul(wk[:, 2 * NE:3 * NE], ones_bf[:, :], pmask_bf[:, t, :],
                                                  start=(t == 0), stop=(t == 1)))
            old, new = seen_cnt[b % 2], seen_cnt[(b + 1) % 2]
            m1 = dve.do(lambda e: e.tensor_tensor(pos[:, :, :], wk[:, 0:2 * NE].rearrange("p (t n) -> p t n", t=TILES),
                                                  old[:, :].unsqueeze(1).broadcast_to([P, TILES, NE]), ALU.add),
                        after=[m, dstate["cnt"]], reuse=[mw])
            dstate["cnt"] = dve.do(lambda e: e.tensor_tensor(new[:, :], wk[:, 2 * NE:3 * NE], old[:, :], ALU.add),
                                   after=[m, m1])
            work.give(i, [m1, dstate["cnt"]])
            yield ()
            m2 = dve.do(lambda e: e.scalar_tensor_tensor(pmask[:, :, :], pos[:, :, :], float(CAP), pmask[:, :, :],
                                                         ALU.is_lt, ALU.mult), after=[m1, mkb, mw])
            m3 = dve.do(lambda e: e.tensor_tensor(sval[:, :, :], expert_end[:, :].unsqueeze(1).broadcast_to(
                [P, TILES, NE]), pos[:, :, :], ALU.subtract), after=[m1, m_end])
            m3 = dve.do(lambda e: e.tensor_tensor(sval[:, :, :], sval[:, :, :], pmask[:, :, :], ALU.mult),
                        after=[m2, m3])
            for t in range(TILES):
                m4 = dve.do(lambda e, t=t: e.max(stop8[:, t, :], sval[:, t, :]), after=[m3])
            isx, six, fs = sidx.take()
            m5 = dve.do(lambda e: e.tensor_scalar(six[:, :, :], stop8[:, :, :], -1.0, float(SLOTS), ALU.mult,
                                                  ALU.add), after=[m4], reuse=fs)
            dstate["route"] = (m5,)
            yield [m5]
            for t in range(TILES):
                for k in range(8):
                    msc = pool.dma(lambda e, t=t, k=k: e.indirect_dma_start(
                        out=slots_dram, out_offset=bass.IndirectOffsetOnAxis(ap=six[:, t, k:k + 1], axis=0),
                        in_=rw[:, t, :], in_offset=None, bounds_check=SLOTS - 1, oob_is_err=False),
                        c_scat[ir], after=[m5, mn, mw, *mh, m_init])
                    if k % 2:
                        yield (pool.sem, pool.count),
            row.give(ir, [msc])
            sidx.give(isx, [msc])
            banks = []
            for half in range(2):
                i, wk, free = work.take()
                for f in range(2):
                    c0 = half * FH + f * FC
                    for dt in range(DT):
                        m = pe.do(lambda e, wk=wk, f=f, dt=dt, c0=c0: e.matmul(
                            wk[0:FC, f * S:(f + 1) * S], wsgu[:, dt, c0:c0 + FC], xdT[:, dt, :],
                            start=(dt == 0), stop=(dt == DT - 1)), after=[mT_, m_w], reuse=free, ns=253)
                banks.append((i, wk, m))
                yield ()
            dstate["xdT"] = (m,)
            (ig, gk, mg), (iu, uk, mu) = banks
            gv = gk[0:FC, :].rearrange("p (f s) -> p f s", f=2)
            uv = uk[0:FC, :].rearrange("p (f s) -> p f s", f=2)
            ma = act.do(lambda e: e.activation(sT_a[:, :, :], gv, ACT.Tanh, scale=0.5), after=[mg],
                        reuse=dstate["sT"])
            mb = dve.do(lambda e: e.scalar_tensor_tensor(sT_a[:, :, :], sT_a[:, :, :], 1.0, gv, ALU.add, ALU.mult),
                        after=[ma, mg], ns=600)
            mc = dve.do(lambda e: e.scalar_tensor_tensor(sT_a[:, :, :], sT_a[:, :, :], 0.5, uv, ALU.mult, ALU.mult),
                        after=[mb, mu], ns=600)
            work.give(ig, [ma, mb])
            work.give(iu, [mc])
            yield [mc]
            i, wk, free = work.take()
            for t in range(TILES):
                for f in range(2):
                    m = pe.do(lambda e, t=t, f=f: e.matmul(wk[:, t * D:(t + 1) * D], sT_a[:, f, t * P:(t + 1) * P],
                                                           wsd[:, f, :], start=(f == 0), stop=(f == 1)),
                              after=[mc, m_w], reuse=free)
            dstate["sT"] = (m,)
            mo = dve.do(lambda e: e.tensor_tensor(xb[:, :, :], xb[:, :, :], wk[:, :].rearrange(
                "p (t d) -> p t d", t=TILES), ALU.add), after=[m, *mh])
            work.give(i, [mo])
            mst = sp.dma(lambda e: e.dma_start(out_pad[b * S:(b + 1) * S, :].rearrange("(t p) d -> p t d", p=P),
                                               xb[:, :, :]), c_out[b % 2], after=[mo])
            X.give(ix, [mst])
            dstate["out"].append(mst)
            dstate["scat"] = dstate.get("scat", []) + [msc]
            yield ()

        def load_expert(n):
            i = n % NW
            sp.dma(lambda e: e.dma_start(ewg[i][:, :, :], wg_in[n].rearrange("(a p) f -> p a f", p=P)), c_ew[i],
                   reuse=ew_free[i])
            sp.dma(lambda e: e.dma_start(ewu[i][:, :, :], wu_in[n].rearrange("(a p) f -> p a f", p=P)), c_ew[i])
            return sp.dma(lambda e: e.dma_start(ewd[i][:, :, :], wd_in[n].rearrange("(a p) d -> p a d", p=FC)),
                          c_ew[i])

        def together(*streams):
            ready = [0] * len(streams)
            alive = list(range(len(streams)))
            blocked = set()
            while alive:
                n = min((j for j in alive if j not in blocked), key=lambda j: max(ready[j] + streams[j][1], pe.clock))
                try:
                    y = next(streams[n][0])
                    if y is BLOCKED:
                        blocked.add(n)
                    else:
                        ready[n] = plan.after(y)
                        blocked.clear()
                except StopIteration:
                    alive.remove(n)
                    blocked.clear()

        def routes():
            for b in range(NB):
                while emitted["A"] < b:
                    yield BLOCKED
                yield from route(b)
                yield ()

        def mixtures():
            for b in range(NB):
                while len(m_wmix) < len(mix_jobs):
                    yield BLOCKED
                while len(routed) <= b:
                    yield BLOCKED
                yield from mix(b)

        def dispatches():
            for b in range(NB):
                while emitted["C"] < b:
                    yield BLOCKED
                yield from stage_d(b)

        together((complete(), 0), (attend_half(0), 0), (attend_half(1), 0), (prepare(), 0), (raw_keys(), 0),
                 (routes(), 0), (dispatches(), 0), (mixtures(), LATE_NS), (load_mix(), 0))

        ew_marks = {}
        quiet = [(q.sem, q.count) for q in (pe, dve, act, pool)]
        ew_free = [tuple(quiet)] * NW
        for n in range(NW):
            ew_marks[n] = load_expert(n)


        gathered = [*dstate["out"][-2:], *dstate["scat"][-2:]]
        last_add = None
        quiet = [(q.sem, q.count) for q in (pe, dve, act, pool)]
        er_free = [tuple(quiet)] * NX
        ey_free = [tuple(quiet)] * 3
        exT_free = [tuple(quiet)] * 4
        id_free = [tuple(quiet)] * NX

        def load_rows(n):
            i = n % NX
            return sp.dma(lambda e: e.dma_start(erow[i], slots_dram[n * CAP:(n + 1) * CAP, :]), c_er[i],
                          after=gathered, reuse=er_free[i])

        er_marks = {n: load_rows(n) for n in range(1)}
        hid_free = [tuple(quiet)] * 2
        for n in range(NE):
            if n + 1 < NE:
                er_marks[n + 1] = load_rows(n + 1)
            rwt, mr = erow[n % NX], er_marks[n]
            mi = dve.do(lambda e, n=n, rwt=rwt: e.tensor_copy(eid[n % NX], rwt[:, ROW - 1:ROW]), after=[mr],
                        reuse=id_free[n % NX])
            i, wk, free = work.take()
            for dt in range(DT):
                m = pe.do(lambda e, dt=dt, wk=wk, rwt=rwt: e.transpose(wk[:, dt * P:(dt + 1) * P],
                                                                      rwt[:, dt * P:(dt + 1) * P], ident),
                          after=[mr], reuse=free)
            xT = exT[n % 4].rearrange("p (a t) -> p a t", a=DT)
            mt = act.do(lambda e, wk=wk, xT=xT: e.copy(xT, wk[:, 0:D].rearrange("p (a t) -> p a t", a=DT)),
                        after=[m], reuse=exT_free[n % 4])
            work.give(i, [mt])
            i, wk, free = work.take()
            w = n % NW
            for j, (wt, f) in enumerate(((ewg[w], 0), (ewg[w], 1), (ewu[w], 0), (ewu[w], 1))):
                for dt in range(DT):
                    m = pe.do(lambda e, wk=wk, j=j, wt=wt, f=f, dt=dt, xT=xT: e.matmul(
                        wk[0:FC, j * P:(j + 1) * P], wt[:, dt, f * FC:(f + 1) * FC], xT[:, dt, :],
                        start=(dt == 0), stop=(dt == DT - 1)), after=[mt, ew_marks[n]], reuse=free)
            exT_free[n % 4] = (m,)
            gv = wk[0:FC, 0:2 * P].rearrange("p (f s) -> p f s", f=2)
            uv = wk[0:FC, 2 * P:4 * P].rearrange("p (f s) -> p f s", f=2)
            act_h = sT_a[:, :, (n % 2) * P:(n % 2 + 1) * P]
            mul_h = sT_a[:, :, (n % 2) * P:(n % 2 + 1) * P]
            ma = act.do(lambda e, gv=gv, h=act_h: e.activation(h, gv, ACT.Silu), after=[m],
                        reuse=hid_free[n % 2])
            mb = dve.do(lambda e, uv=uv, h=act_h, o=mul_h: e.tensor_tensor(o, h, uv, ALU.mult), after=[ma, m],
                        reuse=hid_free[n % 2])
            work.give(i, [ma, mb])
            i, wk, free = work.take()
            for f in range(2):
                m = pe.do(lambda e, wk=wk, f=f, o=mul_h, w=w: e.matmul(wk[:, 0:D], o[:, f, :], ewd[w][:, f, :],
                                                                    start=(f == 0), stop=(f == 1)),
                          after=[mb], reuse=free)
            ew_free[w] = (m,)
            hid_free[n % 2] = (m, mb)
            if n + NW < NE:
                ew_marks[n + NW] = load_expert(n + NW)
            y = ey[n % 3]
            my = dve.do(lambda e, wk=wk, n=n, rwt=rwt, y=y: e.tensor_scalar(y, wk[:, 0:D], rwt[:, D + n:D + n + 1],
                                                                          None, ALU.mult), after=[m],
                        reuse=ey_free[n % 3])
            work.give(i, [my])
            er_free[n % NX] = (my, mi, mt)
            last_add = pool.dma(lambda e, n=n, y=y: e.indirect_dma_start(
                out=out_pad, out_offset=bass.IndirectOffsetOnAxis(ap=eid[n % NX], axis=0), in_=y, in_offset=None,
                bounds_check=T + CAP - 1, oob_is_err=True, compute_op=ALU.add), c_add, after=[my, mi] + (
                    [last_add] if last_add else gathered))
            ey_free[n % 3] = (last_add,)
            id_free[n % NX] = (last_add,)
        pool.wait([last_add])
        sp.wait([last_add, m_init])



def kernel(**inputs):
    import concourse.bacc as bacc
    from concourse.bass_utils import run_bass_kernel_spmd

    a = {k: np.asarray(v) for k, v in inputs.items()}

    def split_rows(w):
        return np.ascontiguousarray(w.reshape(-1, P, w.shape[1]).transpose(1, 0, 2))

    def mixture_rows(w):
        n, o, i = w.shape
        return np.ascontiguousarray(w.transpose(0, 2, 1).reshape(n, i // P, P, o).transpose(2, 0, 1, 3))

    fc = a["L1_ffn_ws_down"].shape[0] // 2
    arrays = {
        "x": a["x"],
        "ctx": a["ctx_1024"],
        "ctxT": np.ascontiguousarray(a["ctx_1024"].transpose(0, 2, 1)),
        "wqT": split_rows(a["L0_xattn_Wq"].T),
        "wkvT": split_rows(np.concatenate([a["L0_xattn_Wk"].T, a["L0_xattn_Wv"].T], 1)),
        "woT": split_rows(a["L0_xattn_Wo"].T),
        "bq": a["L0_xattn_bq"],
        "bkv": np.concatenate([a["L0_xattn_bk"], a["L0_xattn_bv"]]),
        "bo": a["L0_xattn_bo"],
        "pw": a["L0_ffn_P_w"],
        "uT": np.ascontiguousarray(np.concatenate([a["L0_ffn_U1"], a["L0_ffn_U2"], a["L0_ffn_U3"]]).T),
        "w1T": mixture_rows(a["L0_ffn_W1"]),
        "w2T": mixture_rows(a["L0_ffn_W2"]),
        "b2": a["L0_ffn_b2"],
        "rT": split_rows(a["L1_ffn_router_w"].T),
        "wg": a["L1_ffn_w_gate"],
        "wu": a["L1_ffn_w_up"],
        "wd": a["L1_ffn_w_down"],
        "wsgu": split_rows(a["L1_ffn_ws_gate_up"]),
        "wsd": np.ascontiguousarray(a["L1_ffn_ws_down"].reshape(2, fc, -1).transpose(1, 0, 2)),
    }
    nc = bacc.Bacc("TRN2", target_bir_lowering=False, num_devices=1, dynamic_dma_scratch_size=4096)
    args = [nc.dram_tensor("in_" + n, v.shape, mybir.dt.from_np(v.dtype), kind="ExternalInput").ap()
            for n, v in arrays.items()]
    nb, s, d = a["x"].shape
    out = nc.dram_tensor("out", (nb * s + P, d), F32, kind="ExternalOutput").ap()
    build(nc, *args, out)
    r = run_bass_kernel_spmd(nc, [{"in_" + n: v for n, v in arrays.items()}], core_ids=[0])
    return r.results[0]["out"][:nb * s].reshape(nb, s, d)
```
